# Optimizing a Trainium2 kernel written in Bass

```python
import numpy as np
import jax
import jax.numpy as jnp

def _softmax(x, axis=-1):
    return jax.nn.softmax(x, axis=axis)

def _gelu(x):
    return jax.nn.gelu(x, approximate=True)

def _silu(x):
    return jax.nn.silu(x)

def _sigmoid(x):
    return jax.nn.sigmoid(x)

def _layernorm(x, axis=-1, eps=1e-05):
    m = jnp.mean(x, axis=axis, keepdims=True)
    v = jnp.var(x, axis=axis, keepdims=True)
    return (x - m) / jnp.sqrt(v + eps)

def _scatter_add(tgt, idx, src, axis=0):
    return tgt.at[idx].add(src)

def _segment_sum(src, seg, n):
    return jax.ops.segment_sum(src, seg, n)
kernel_name = 'mk_adj_ffn_d2_adj_r2_33fd1d'

def setup_inputs(seed: int=0):
    np.random.seed(seed)
    _w = jnp.asarray

    def _rec_inputs():
        import jax
        import jax.numpy as jnp
        _gk = jax.random.key(seed)
        x = -0.0002928 + 1 * jax.random.normal(jax.random.fold_in(_gk, 1), (128, 64, 128), jnp.float32)
        _a = jax.random.bernoulli(jax.random.fold_in(_gk, 2), 0.125, (128, 64, 64))
        _a = jnp.logical_or(_a, jnp.swapaxes(_a, -1, -2))
        _a = jnp.logical_or(_a, jnp.eye(64, dtype=bool))
        _af = _a.astype(jnp.float32)
        _af = _af * jax.random.uniform(jax.random.fold_in(_gk, 3), (128, 64, 64), jnp.float32, 0.05, 1)
        adj = _af
        return (x, adj)
    x, adj = _rec_inputs()

    def _L0_gnn_setup():
        import jax, jax.numpy as jnp
        import numpy as np
        key = jax.random.key(seed)
        k1, k2, k3, k4 = jax.random.split(key, 4)
        B, N, F_in, F_out = (8, 1024, 128, 128)
        x = jax.random.normal(k1, (B, N, F_in), dtype=jnp.float32)
        adj = jax.random.uniform(k2, (B, N, N), dtype=jnp.float32)
        stdv = 1.0 / np.sqrt(F_out)
        weight = jax.random.uniform(k3, (F_in, F_out), dtype=jnp.float32, minval=-stdv, maxval=stdv)
        bias = jax.random.uniform(k4, (F_out,), dtype=jnp.float32, minval=-stdv, maxval=stdv)
        return {'x': x, 'adj': adj, 'weight': weight, 'bias': bias}
    _L0_gnn_all = _L0_gnn_setup()
    _L0_gnn_in = {k: v for k, v in _L0_gnn_all.items() if k in ('weight', 'bias')}
    del _L0_gnn_all

    def _L0_ffn_setup():
        import jax, jax.numpy as jnp
        import numpy as np
        B, T, C = (64, 192, 128)
        NH, NKV = (4, 2)
        HD = C // NH
        NREP = NH // NKV
        NE, TOPK = (8, 2)
        HID = int(8 / 3 * C)
        EPS_RMS = 1e-06

        def _rope_tables(t_len):
            inv_freq = 1.0 / 10000.0 ** (np.arange(0, HD, 2, dtype=np.float32) / HD)
            t = np.arange(t_len, dtype=np.float32)
            freqs = np.outer(t, inv_freq)
            emb = np.concatenate([freqs, freqs], axis=-1)
            return (jnp.asarray(np.cos(emb)), jnp.asarray(np.sin(emb)))

        def _rotate_half(x):
            h = x.shape[-1] // 2
            return jnp.concatenate([-x[..., h:], x[..., :h]], axis=-1)

        def _rmsnorm(v, w):
            return v * jax.lax.rsqrt(jnp.mean(v * v, axis=-1, keepdims=True) + EPS_RMS) * w
        key = jax.random.key(seed)
        ks = jax.random.split(key, 10)
        s = lambda k, shape: jax.random.normal(k, shape, jnp.float32) * 0.02
        return {'x': jax.random.normal(ks[0], (B, T, C), jnp.float32), 'ln1_w': jnp.ones((C,), jnp.float32), 'ln2_w': jnp.ones((C,), jnp.float32), 'wq': s(ks[1], (NH * HD, C)), 'wk': s(ks[2], (NKV * HD, C)), 'wv': s(ks[3], (NKV * HD, C)), 'wo': s(ks[4], (C, C)), 'router_w': s(ks[5], (NE, C)), 'w1': s(ks[6], (NE, HID, C)), 'w2': s(ks[7], (NE, C, HID)), 'w3': s(ks[8], (NE, HID, C))}
    _L0_ffn_all = _L0_ffn_setup()
    _L0_ffn_in = {k: v for k, v in _L0_ffn_all.items() if k in ('ln1_w', 'ln2_w', 'wq', 'wk', 'wv', 'wo', 'router_w', 'w1', 'w2', 'w3')}
    del _L0_ffn_all

    def _L1_gnn_setup():
        import jax, jax.numpy as jnp
        import numpy as np
        B, N, C_IN, C_OUT = (8, 1024, 128, 128)
        key = jax.random.key(seed)
        k1, k2, k3 = jax.random.split(key, 3)
        x = jax.random.normal(k1, (B, N, C_IN), dtype=jnp.float32)
        adj = jax.random.uniform(k2, (B, N, N), dtype=jnp.float32)
        limit = float(np.sqrt(6.0 / (C_IN + C_OUT)))
        weight = jax.random.uniform(k3, (C_IN, C_OUT), minval=-limit, maxval=limit, dtype=jnp.float32)
        bias = jnp.zeros((C_OUT,), dtype=jnp.float32)
        return {'x': x, 'adj': adj, 'weight': weight, 'bias': bias}
    _L1_gnn_all = _L1_gnn_setup()
    _L1_gnn_in = {k: v for k, v in _L1_gnn_all.items() if k in ('weight', 'bias')}
    del _L1_gnn_all

    def _L1_ffn_setup():
        import jax, jax.numpy as jnp
        import numpy as np
        E, D, H, TOP_K = (6, 128, 128, 2)
        ROUTER_H = D // 2
        key = jax.random.key(seed)
        ks = jax.random.split(key, 12)
        s = 1.0 / np.sqrt(D)
        sh = 1.0 / np.sqrt(H)
        sr = 1.0 / np.sqrt(ROUTER_H)
        return {'features': jax.random.normal(ks[0], (8, 2048, D), dtype=jnp.float32), 'router_w1': jax.random.uniform(ks[1], (D, ROUTER_H), jnp.float32, -s, s), 'router_b1': jnp.zeros((ROUTER_H,), jnp.float32), 'router_w2': jax.random.uniform(ks[2], (ROUTER_H, E), jnp.float32, -sr, sr), 'router_b2': jnp.zeros((E,), jnp.float32), 'expert_w1': jax.random.uniform(ks[3], (E, D, H), jnp.float32, -s, s), 'expert_b1': jnp.zeros((E, H), jnp.float32), 'expert_w2': jax.random.uniform(ks[4], (E, H, H), jnp.float32, -sh, sh), 'expert_b2': jnp.zeros((E, H), jnp.float32), 'expert_w3': jax.random.uniform(ks[5], (E, H, D), jnp.float32, -sh, sh), 'expert_b3': jnp.zeros((E, D), jnp.float32)}
    _L1_ffn_all = _L1_ffn_setup()
    _L1_ffn_in = {k: v for k, v in _L1_ffn_all.items() if k in ('router_w1', 'router_b1', 'router_w2', 'router_b2', 'expert_w1', 'expert_b1', 'expert_w2', 'expert_b2', 'expert_w3', 'expert_b3')}
    del _L1_ffn_all
    return {'x': x, 'adj': adj, 'L0_gnn_weight': _L0_gnn_in['weight'], 'L0_gnn_bias': _L0_gnn_in['bias'], 'L0_ffn_ln1_w': _L0_ffn_in['ln1_w'], 'L0_ffn_ln2_w': _L0_ffn_in['ln2_w'], 'L0_ffn_wq': _L0_ffn_in['wq'], 'L0_ffn_wk': _L0_ffn_in['wk'], 'L0_ffn_wv': _L0_ffn_in['wv'], 'L0_ffn_wo': _L0_ffn_in['wo'], 'L0_ffn_router_w': _L0_ffn_in['router_w'], 'L0_ffn_w1': _L0_ffn_in['w1'], 'L0_ffn_w2': _L0_ffn_in['w2'], 'L0_ffn_w3': _L0_ffn_in['w3'], 'L1_gnn_weight': _L1_gnn_in['weight'], 'L1_gnn_bias': _L1_gnn_in['bias'], 'L1_ffn_router_w1': _L1_ffn_in['router_w1'], 'L1_ffn_router_b1': _L1_ffn_in['router_b1'], 'L1_ffn_router_w2': _L1_ffn_in['router_w2'], 'L1_ffn_router_b2': _L1_ffn_in['router_b2'], 'L1_ffn_expert_w1': _L1_ffn_in['expert_w1'], 'L1_ffn_expert_b1': _L1_ffn_in['expert_b1'], 'L1_ffn_expert_w2': _L1_ffn_in['expert_w2'], 'L1_ffn_expert_b2': _L1_ffn_in['expert_b2'], 'L1_ffn_expert_w3': _L1_ffn_in['expert_w3'], 'L1_ffn_expert_b3': _L1_ffn_in['expert_b3']}

def reference(x, adj, L0_gnn_weight, L0_gnn_bias, L0_ffn_ln1_w, L0_ffn_ln2_w, L0_ffn_wq, L0_ffn_wk, L0_ffn_wv, L0_ffn_wo, L0_ffn_router_w, L0_ffn_w1, L0_ffn_w2, L0_ffn_w3, L1_gnn_weight, L1_gnn_bias, L1_ffn_router_w1, L1_ffn_router_b1, L1_ffn_router_w2, L1_ffn_router_b2, L1_ffn_expert_w1, L1_ffn_expert_b1, L1_ffn_expert_w2, L1_ffn_expert_b2, L1_ffn_expert_w3, L1_ffn_expert_b3):
    import jax
    import jax.numpy as jnp

    def _L0_gnn_ref(x, adj, weight, bias):
        import jax, jax.numpy as jnp
        import numpy as np
        support = jnp.einsum('bni,io->bno', x, weight)
        out = jnp.einsum('bnm,bmo->bno', adj, support)
        return out + bias

    def _L0_ffn_ref(x, ln1_w, ln2_w, wq, wk, wv, wo, router_w, w1, w2, w3):
        import jax, jax.numpy as jnp
        import numpy as np
        B, T, C = (64, 192, 128)
        NH, NKV = (4, 2)
        HD = C // NH
        NREP = NH // NKV
        NE, TOPK = (8, 2)
        HID = int(8 / 3 * C)
        EPS_RMS = 1e-06

        def _rope_tables(t_len):
            inv_freq = 1.0 / 10000.0 ** (np.arange(0, HD, 2, dtype=np.float32) / HD)
            t = np.arange(t_len, dtype=np.float32)
            freqs = np.outer(t, inv_freq)
            emb = np.concatenate([freqs, freqs], axis=-1)
            return (jnp.asarray(np.cos(emb)), jnp.asarray(np.sin(emb)))

        def _rotate_half(x):
            h = x.shape[-1] // 2
            return jnp.concatenate([-x[..., h:], x[..., :h]], axis=-1)

        def _rmsnorm(v, w):
            return v * jax.lax.rsqrt(jnp.mean(v * v, axis=-1, keepdims=True) + EPS_RMS) * w
        Bx, Tx, Cx = x.shape
        h = _rmsnorm(x, ln1_w)
        q = (h @ wq.T).reshape(Bx, Tx, NH, HD).transpose(0, 2, 1, 3)
        k = (h @ wk.T).reshape(Bx, Tx, NKV, HD).transpose(0, 2, 1, 3)
        v = (h @ wv.T).reshape(Bx, Tx, NKV, HD).transpose(0, 2, 1, 3)
        cos, sin = _rope_tables(Tx)
        cos, sin = (cos[None, None], sin[None, None])
        q = q * cos + _rotate_half(q) * sin
        k = k * cos + _rotate_half(k) * sin
        k = jnp.repeat(k, NREP, axis=1)
        v = jnp.repeat(v, NREP, axis=1)
        scores = jnp.einsum('bhtd,bhsd->bhts', q, k) / jnp.sqrt(jnp.float32(HD))
        causal = jnp.tril(jnp.ones((Tx, Tx), dtype=bool))
        scores = jnp.where(causal[None, None], scores, jnp.float32(-1e+30))
        att = jax.nn.softmax(scores, axis=-1)
        y = jnp.einsum('bhts,bhsd->bhtd', att, v).transpose(0, 2, 1, 3).reshape(Bx, Tx, Cx)
        x = x + y @ wo.T
        flat = _rmsnorm(x, ln2_w).reshape(-1, Cx)
        probs = jax.nn.softmax(flat @ router_w.T, axis=-1)
        tp, ti = jax.lax.top_k(probs, TOPK)
        tp = tp / (jnp.sum(tp, axis=-1, keepdims=True) + 1e-09)
        weights = jnp.sum(tp[..., None] * jax.nn.one_hot(ti, NE, dtype=flat.dtype), axis=1)
        out = jnp.zeros_like(flat)
        for e in range(NE):
            hh = jax.nn.silu(flat @ w1[e].T) * (flat @ w3[e].T)
            out = out + weights[:, e:e + 1] * (hh @ w2[e].T)
        return x + out.reshape(Bx, Tx, Cx)

    def _L1_gnn_ref(x, adj, weight, bias):
        import jax, jax.numpy as jnp
        import numpy as np
        B, N, C_IN, C_OUT = (8, 1024, 128, 128)
        d_inv_sqrt = (jnp.sum(adj, axis=-1) + 1e-05) ** (-0.5)
        adj_norm = d_inv_sqrt[..., :, None] * adj * d_inv_sqrt[..., None, :]
        support = jnp.einsum('bni,io->bno', x, weight)
        return jnp.einsum('bnm,bmo->bno', adj_norm, support) + bias

    def _L1_ffn_ref(features, router_w1, router_b1, router_w2, router_b2, expert_w1, expert_b1, expert_w2, expert_b2, expert_w3, expert_b3):
        import jax, jax.numpy as jnp
        import numpy as np
        E, D, H, TOP_K = (6, 128, 128, 2)
        ROUTER_H = D // 2
        rh = jax.nn.relu(features @ router_w1 + router_b1)
        expert_logits = jax.nn.softmax(rh @ router_w2 + router_b2, axis=-1)
        top_w, top_i = jax.lax.top_k(expert_logits, TOP_K)
        routing_weights = jax.nn.softmax(top_w, axis=-1)
        h1 = jax.nn.relu(jnp.einsum('bsd,edh->bseh', features, expert_w1) + expert_b1)
        h2 = jax.nn.relu(jnp.einsum('bseh,ehf->bsef', h1, expert_w2) + expert_b2)
        expert_out = jnp.einsum('bsef,efo->bseo', h2, expert_w3) + expert_b3
        sel = jnp.take_along_axis(expert_out, top_i[:, :, :, None], axis=2)
        combined = jnp.sum(sel * routing_weights[..., None], axis=2)
        return combined
    x = x + _L0_gnn_ref(_layernorm(x, axis=-1), adj, L0_gnn_weight, L0_gnn_bias)
    x = x + _L0_ffn_ref(_layernorm(x, axis=-1), L0_ffn_ln1_w, L0_ffn_ln2_w, L0_ffn_wq, L0_ffn_wk, L0_ffn_wv, L0_ffn_wo, L0_ffn_router_w, L0_ffn_w1, L0_ffn_w2, L0_ffn_w3)
    x = x + _L1_gnn_ref(_layernorm(x, axis=-1), adj, L1_gnn_weight, L1_gnn_bias)
    x = x + _L1_ffn_ref(_layernorm(x, axis=-1), L1_ffn_router_w1, L1_ffn_router_b1, L1_ffn_router_w2, L1_ffn_router_b2, L1_ffn_expert_w1, L1_ffn_expert_b1, L1_ffn_expert_w2, L1_ffn_expert_b2, L1_ffn_expert_w3, L1_ffn_expert_b3)
    return x

_drawn_inputs = setup_inputs


def setup_inputs(seed=0):
    import zlib

    import numpy as np

    out = dict(_drawn_inputs(seed))
    spreads = {'L0_ffn_ln1_w': (1.0, 0.6),
     'L0_ffn_ln2_w': (1.0, 0.6),
     'L1_gnn_bias': (0.0, 0.8),
     'L1_ffn_router_b1': (0.0, 0.426),
     'L1_ffn_router_b2': (0.0, 0.546),
     'L1_ffn_expert_b1': (0.0, 2.0),
     'L1_ffn_expert_b2': (0.0, 2.0),
     'L1_ffn_expert_b3': (0.0, 1.584)}
    factors = {'L0_ffn_wq': 8.0,
     'L0_ffn_wk': 8.0,
     'L0_ffn_wv': 5.906,
     'L0_ffn_wo': 5.829,
     'L0_ffn_router_w': 8.0,
     'L0_ffn_w1': 8.0,
     'L0_ffn_w2': 8.0,
     'L0_ffn_w3': 8.0,
     'L1_ffn_expert_w1': 3.129,
     'L1_ffn_expert_w2': 2.718}
    for name, (base, spread) in spreads.items():
        noise = np.random.default_rng([zlib.crc32(name.encode()), seed]).standard_normal(out[name].shape)
        drawn = base * np.exp(spread * noise) if base else spread * noise
        out[name] = jnp.asarray(drawn.astype(out[name].dtype))
    for name, factor in factors.items():
        out[name] = (out[name] * factor).astype(out[name].dtype)
    return out
```

```python
from contextlib import ExitStack

import numpy as np
import concourse.bass as bass
from concourse import mybir

P = 128
NB, NN, C = 128, 64, 128
TOK = NB * NN
TG = 4
GT = TG * P
NG = TOK // GT
GR = GT // NN
NH, HD = 4, 32
NE0, HID = 8, 341
HIDP = HID + 1
KC = 3
NE1, RH = 6, 64
MB = TOK // P
REG = MB + 1
DUM = NE0 * REG
NBLK = 2 * TOK // P + NE0
NDUM = NE0
ROWS = (DUM + NDUM) * P

C_ID, C_COS, C_SIN, C_MASK = 0, 128, 192, 256
C_TRI, C_ONE, C_IOTA, C_BASE = 320, 448, 576, 584
C_BLK, C_TRI8 = 592, 592 + NBLK
C_N = C_TRI8 + 64


def constants():
    c = np.zeros((P, C_N), np.float32)
    c[:, C_ID:C_ID + P] = np.eye(P)
    inv = 1.0 / 10000.0 ** (np.arange(0, HD, 2, dtype=np.float32) / HD)
    fr = np.outer(np.arange(NN, dtype=np.float32), inv)
    emb = np.concatenate([fr, fr], -1)
    sign = np.where(np.arange(HD) < HD // 2, -1.0, 1.0)
    c[:, C_COS:C_COS + NN] = np.tile(np.cos(emb).T, (NH, 1))
    c[:, C_SIN:C_SIN + NN] = np.tile((np.sin(emb) * sign).T, (NH, 1))
    t = np.arange(P) % NN
    c[:, C_MASK:C_MASK + NN] = np.where(np.arange(NN)[None] <= t[:, None], 0.0, -1e30)
    c[:, C_TRI:C_TRI + P] = np.arange(P)[:, None] < np.arange(P)[None]
    c[:, C_ONE:C_ONE + P] = 1.0
    c[:, C_IOTA:C_IOTA + 8] = np.arange(8)
    c[:, C_BASE:C_BASE + 8] = np.arange(8) * REG * P
    c[:, C_BLK:C_BLK + NBLK] = np.arange(NBLK)
    c[:, C_TRI8:C_TRI8 + 64] = (np.arange(8)[None] <= np.arange(8)[:, None]).reshape(-1)
    return c


class Steps:

    def __init__(self, sem, names):
        self.sem, self.names = sem, names.split()

    def at(self, name, g):
        return g * len(self.names) + (self.names.index(name) + 1)


def build(nc, x, adj_t, gnn0_w, gnn0_b, ln1, ln2, wqkv, wo, router0, w13, w2, gnn1_w, gnn1_b,
          r1_w1, r1_b1, r1_w2, r1_b2, e_w1, e_b1, e_w2, e_b2, e_w3, e_b3, consts, out):
    f32, f32r, bf16 = mybir.dt.float32, mybir.dt.float32r, mybir.dt.bfloat16
    u32, i32 = mybir.dt.uint32, mybir.dt.int32
    ALU, ACT, AX = mybir.AluOpType, mybir.ActivationFunctionType, mybir.AxisListType
    V, S, T, G = nc.vector, nc.scalar, nc.tensor, nc.gpsimd
    SCALE = float(HD) ** -0.5

    slots_in = nc.dram_tensor("slots_in", (ROWS, C), f32, kind="Internal").ap()
    slots_out = nc.dram_tensor("slots_out", (NBLK * P, C), f32, kind="Internal").ap()
    gates_dram = [nc.dram_tensor(f"gates_dram{i}", (NE1, GT), f32, kind="Internal").ap() for i in range(2)]

    def first(g):
        return isinstance(g, int) and g == 0

    with ExitStack() as whole:
        def sb_in(ctx):
            return lambda name, shape, dt=f32: ctx.enter_context(nc.sbuf_tensor(name, shape, dt))

        def sem_in(ctx):
            return lambda name: ctx.enter_context(nc.semaphore(name))

        sb, sem = sb_in(whole), sem_in(whole)
        banks = [whole.enter_context(nc.psum_tensor(f"bank{i}", [P, 512], f32)) for i in range(8)]

        cst = sb("cst", [P, C_N])
        ident = cst[:, C_ID:C_ID + P]
        iota8 = cst[:, C_IOTA:C_IOTA + 8]
        base_all = sb("base_all", [P, NG * TG, C])
        slots_all = sb("slots_all", [P, NG, 2 * TG], u32)
        gates_all = sb("gates_all", [P, NG, 2 * TG])
        w13_hi = sb("w13_hi", [P, NE0 * 2 * HIDP], f32r)
        w13_lo = sb("w13_lo", [P, NE0 * 2 * HIDP], f32r)
        w2_sb = sb("w2_sb", [P, NE0 * KC * C])
        table = sb("table", [1, 2, NBLK], i32)

        with ExitStack() as ctx:
            sb, sem = sb_in(ctx), sem_in(ctx)
            f_all = sb("f_all", [P, NG * TG, C])
            stage = f_all[:, NG * TG - 43:, :].rearrange("p t c -> p (t c)")[:, 0:NE0 * 2 * HIDP]
            gw, gb, wo_sb = sb("gw", [P, C]), sb("gb", [P, C]), sb("wo_sb", [P, C])
            rw, ln = sb("rw", [P, NE0]), sb("ln", [P, 2])
            rws = sb("rws", [P, NE0])
            wq_raw = sb("wq_raw", [P, 576])
            wq_hi, wq_lo = sb("wq_hi", [P, 576], f32r), sb("wq_lo", [P, 576], f32r)
            trib, oneb = sb("trib", [P, P], bf16), sb("oneb", [P, P], bf16)
            xt, xb, xn, adjt = (sb(n, [P, TG, C]) for n in ("xt", "xb", "xn", "adjt"))
            tT, x1, hp = (sb(n, [P, TG, C]) for n in ("tT", "x1", "hp"))
            hT_hi, hT_lo = sb("hT_hi", [P, GT + NN], f32r), sb("hT_lo", [P, GT + NN], f32r)
            q_cos, q_sin, k_cos, k_sin = (sb(n, [P, GT]) for n in ("q_cos", "q_sin", "k_cos", "k_sin"))
            q_rot, k_rot = sb("q_rot", [P, GT]), sb("k_rot", [P, GT])
            v_diag = sb("v_diag", [P, GR, 2, 66])
            sc, pr = sb("sc", [P, TG, NH, NN]), sb("pr", [P, TG, NH, NN])
            prT = sb("prT", [P, 2, TG, P])
            yn, yT, f2, flat, flatT = (sb(n, [P, TG, C]) for n in ("yn", "yT", "f2", "flat", "flatT"))
            junk = sb("junk", [P, TG, C])
            zrow = sb("zrow", [P, C])
            st_a, mv_a, rs_a = sb("st_a", [P, TG, 6]), sb("mv_a", [P, TG, 2]), sb("rs_a", [P, TG])
            var_a, var_b, mhalf = sb("var_a", [P, TG]), sb("var_b", [P, 2, TG]), sb("mhalf", [P, 2, TG])
            st_b, mv_b = sb("st_b", [P, TG, 6]), sb("mv_b", [P, TG, 2])
            rs_b = sb("rs_b", [P, 2, TG])
            mx, nmx = sb("mx", [P, TG * NH]), sb("nmx", [P, TG * NH])
            rden = sb("rden", [P, TG, NH])
            ss, ssv, rr2 = sb("ss", [P, TG]), sb("ssv", [P, TG]), sb("rr2", [P, TG])
            lg, top, topi = sb("lg", [P, TG, 8]), sb("top", [P, TG, 8]), sb("topi", [P, TG, 8], u32)
            topf, oh = sb("topf", [P, TG, 2]), sb("oh", [P, TG, 2, 8])
            sel, carry, carry_b = sb("sel", [P, TG, 8], bf16), sb("carry", [P, 8]), sb("carry_b", [P, 8], bf16)
            selsum = sb("selsum", [P, 8])
            dtop, etop = sb("dtop", [P, TG, 8]), sb("etop", [P, TG, 8])
            z, s2, den, rec = (sb(n, [P, TG]) for n in ("z", "s2", "den", "rec"))
            rank, ohr, slotf = sb("rank", [P, TG, 8]), sb("ohr", [P, TG, 2, 8]), sb("slotf", [P, TG * 2])
            slot_now = sb("slot_now", [P, 2 * TG], u32)
            cnti, nblk = sb("cnti", [P, 8], i32), sb("nblk", [P, 8])
            slots_f, gaps = sb("slots_f", [P, NG, 2 * TG]), sb("gaps", [P, 8])
            tri_nb, cum = sb("tri_nb", [1, 8, 8]), sb("cum", [1, 8])
            left = f_all[:, :, :].rearrange("p t c -> p (t c)")
            past, pastn = (left[0:1, i * NBLK * 8:(i + 1) * NBLK * 8].rearrange("p (k e) -> p k e", e=8) for i in range(2))
            gap = left[:, 2 * NBLK * 8:2 * NBLK * 8 + NG * 2 * TG * 7].rearrange("p (s e) -> p s e", e=7)
            back = left[:, 3 * NBLK * 8:3 * NBLK * 8 + NG * 2 * TG]
            bexp, bprev, brow = sb("bexp", [1, NBLK]), sb("bprev", [1, NBLK]), sb("brow", [1, NBLK])
            fill = sb("fill", [1, 8], i32)
            spare = sb("spare", [P, 1])

            ld_x, ld_adj, ld_w, ld_big = sem("ld_x"), sem("ld_adj"), sem("ld_w"), sem("ld_big")
            zeroed, zero_fill, scattered = sem("zeroed"), sem("zero_fill"), sem("scattered")
            act_w, dve_w, pool_w = sem("act_w"), sem("dve_w"), sem("pool_w")
            dve_t, pe_t = sem("dve_t"), sem("pe_t")
            va = Steps(sem("va"), "stats moments var xn x1 stats1 moments1 var1 var2 f hp")
            vb = Steps(sem("vb"), "lo q_cos q_sin k_cos k_sin")
            vc = Steps(sem("vc"), "masked max nmax")
            vy = Steps(sem("vy"), "rden yn")
            vd = Steps(sem("vd"), "f2 base ssv flat")
            vr = Steps(sem("vr"), "lg top topi topf oh sel carry_b selsum carry dtop z den rec gate rank ohr slotf slot keep")
            aa = Steps(sem("aa"), "tT")
            ab = Steps(sem("ab"), "hi v")
            ac = Steps(sem("ac"), "exp prT")
            ad = Steps(sem("ad"), "yT sumsq flatT")
            ar = Steps(sem("ar"), "etop")
            pa = Steps(sem("pa"), "rstd xb rstd1 base")
            pb = Steps(sem("pb"), "q k")
            pd = Steps(sem("pd"), "rms")
            ta = Steps(sem("ta"), "tT gnn")
            tb = Steps(sem("tb"), "hT q q_swap k k_swap v")
            tc = Steps(sem("tc"), "scores prT y")
            td = Steps(sem("td"), "yT wo flatT logits rank")

            def sweep(engine, body, skew):
                for i in range(skew):
                    body([i - k if i >= k else None for k in range(skew + 1)])
                with engine.Fori(skew, NG) as i:
                    body([i - k for k in range(skew + 1)])
                for i in range(NG, NG + skew):
                    body([i - k if i - k < NG else None for k in range(skew + 1)])

            with nc.Block() as block:
                @block.sync
                def _(sp):
                    def load_x(g):
                        if not first(g):
                            sp.wait_ge(va.sem, va.at("xn", g - 1))
                            sp.wait_ge(pa.sem, pa.at("xb", g - 1))
                            sp.wait_ge(ta.sem, ta.at("tT", g - 1))
                        sp.dma_start(xt[:, :, :], x[bass.ds(g * GT, GT), :].rearrange("(t p) c -> p t c", p=P)).then_inc(ld_x, 16)
                        rows = adj_t[bass.ds(g * GT, GT), :].rearrange("(t b m) n -> b m t n", b=2, m=NN)
                        if first(g):
                            sp.wait_ge(zeroed, 1)
                        for b in range(2):
                            sp.dma_start(adjt[b * NN:(b + 1) * NN, :, b * NN:(b + 1) * NN], rows[b]).then_inc(ld_adj, 16)

                    load_x(0)
                    for dst, src in ((cst[:, :], consts), (gw[:, :], gnn0_w), (gb[:, :], gnn0_b.partition_broadcast(P)),
                                     (ln[:, 0:1], ln1), (ln[:, 1:2], ln2), (wo_sb[:, :], wo), (rw[:, :], router0),
                                     (wq_raw[:, :], wqkv)):
                        sp.dma_start(dst, src).then_inc(ld_w, 16)
                    sp.dma_start(stage, w13).then_inc(ld_big, 16)
                    sp.dma_start(w2_sb[:, :], w2).then_inc(ld_big, 16)
                    sp.wait_ge(zeroed, 2)
                    for k in range(NDUM):
                        sp.dma_start(slots_in[(DUM + k) * P:(DUM + k + 1) * P, :], zrow[:, :]).then_inc(zero_fill, 16)
                    with sp.Fori(1, NG) as g:
                        load_x(g)
                    sp.wait_ge(dve_t, 3)
                    for e in range(NE0):
                        row = sp.value_load(fill[0:1, e:e + 1], min_val=0, max_val=ROWS - P)
                        sp.dma_start(slots_in[bass.ds(row, P), :], zrow[:, :]).then_inc(zero_fill, 16)
                    sp.wait_ge(zero_fill, 16 * (NDUM + NE0))
                    sp.wait_ge(ld_big, 32)

                @block.gpsimd
                def _(pool):
                    G.memset(adjt[:, :, :], 0.0).then_inc(zeroed, 1)
                    G.memset(zrow[:, :], 0.0).then_inc(zeroed, 1)
                    G.memset(v_diag[:, :, :, :], 0.0).then_inc(pool_w, 1)
                    G.memset(carry[:, :], 0.0).then_inc(pool_w, 1)
                    G.memset(mhalf[:, :, :], -0.5).then_inc(pool_w, 1)
                    pool.wait_ge(pool_w, 3)
                    G.memset(v_diag[0:NN, :, :, 32:33], 1.0).then_inc(pool_w, 1)
                    pool.wait_ge(pool_w, 4)
                    G.memset(v_diag[NN:P, :, :, 65:66], 1.0).then_inc(pool_w, 1)
                    pool.wait_ge(pool_w, 5)

                    def body(gs):
                        a, b, c, d, e = gs
                        def scatter(n):
                            if e is None:
                                return
                            for t, k in ((n // 2, n % 2),):
                                G.indirect_dma_start(
                                    out=slots_in, out_offset=bass.IndirectOffsetOnAxis(ap=slot_now[:, 2 * t + k:2 * t + k + 1], axis=0),
                                    in_=flat[:, t, :], in_offset=None, bounds_check=ROWS - 1).then_inc(scattered, 16)

                        def add_rotated(rot, cos, sin, done):
                            pool.wait_ge(vb.sem, vb.at(done, b))
                            if not first(b):
                                pool.wait_ge(tc.sem, tc.at("scores", b - 1))
                            G.tensor_tensor(rot[:, :], cos[:, :], sin[:, :], ALU.add).then_inc(pb.sem, 1)

                        if e is not None:
                            pool.wait_ge(vr.sem, vr.at("slot", e))
                        if a is not None:
                            pool.wait_ge(va.sem, va.at("var", a))
                            G.tensor_tensor(rs_a[:, :], var_a[:, :], mhalf[:, 0, :], ALU.pow).then_inc(pa.sem, 1)
                            pool.wait_ge(ld_x, a * 16 + 16)
                            if first(a):
                                pool.wait_ge(ld_w, 16 * 8)
                            else:
                                pool.wait_ge(va.sem, va.at("x1", a - 1))
                            G.tensor_tensor(xb[:, :, :], xt[:, :, :], gb[:, :].unsqueeze(1).broadcast_to([P, TG, C]),
                                            ALU.add).then_inc(pa.sem, 1)
                        for n in range(4):
                            scatter(n)
                        if first(a):
                            pool.wait_ge(act_w, 2)
                            G.tensor_tensor(w13_lo[:, :], stage, w13_hi[:, :].bitcast(f32), ALU.subtract).then_inc(pool_w, 1)
                        if b is not None:
                            add_rotated(q_rot, q_cos, q_sin, "q_sin")
                        for n in range(4, 8):
                            scatter(n)
                        if a is not None:
                            pool.wait_ge(va.sem, va.at("var2", a))
                            G.tensor_tensor(rs_b[:, :, :], var_b[:, :, :], mhalf[:, :, :], ALU.pow).then_inc(pa.sem, 1)
                        if d is not None:
                            pool.wait_ge(vd.sem, vd.at("ssv", d))
                            G.tensor_tensor(rr2[:, :], ssv[:, :], mhalf[:, 0, :], ALU.pow).then_inc(pd.sem, 1)
                        if a is not None:
                            pool.wait_ge(va.sem, va.at("f", a))
                        if b is not None:
                            add_rotated(k_rot, k_cos, k_sin, "k_sin")
                        if a is not None:
                            G.tensor_tensor(base_all[:, bass.ds(a * TG, TG), :], x1[:, :, :],
                                            f_all[:, bass.ds(a * TG, TG), :], ALU.add).then_inc(pa.sem, 1)
                    sweep(pool, body, 4)
                    pool.wait_ge(scattered, 16 * 2 * TG * NG)

                @block.scalar
                def _(act):
                    S.preload_act_table(ACT.Exp)
                    act.wait_ge(ld_w, 16 * 8)
                    act.wait_ge(ld_big, 32)
                    S.activation(stage, stage, ACT.Copy, scale=ln[:, 1:2]).then_inc(act_w, 1)
                    act.wait_ge(act_w, 1)
                    S.activation(w13_hi[:, :], stage, ACT.Copy).then_inc(act_w, 1)

                    def body(gs):
                        a, b, c, d, e = gs
                        if b is not None:
                            act.wait_ge(tb.sem, tb.at("hT", b))
                            if not first(b):
                                act.wait_ge(tb.sem, tb.at("v", b - 1))
                            S.activation(hT_hi[:, 0:GT], banks[0][:, :], ACT.Copy)
                            S.activation(hT_hi[:, GT:], banks[0][:, 0:NN], ACT.Copy).then_inc(ab.sem, 1)
                        if d is not None:
                            act.wait_ge(td.sem, td.at("yT", d))
                            if not first(d):
                                act.wait_ge(td.sem, td.at("wo", d - 1))
                            S.activation(yT[:, :, :], banks[1][:, :], ACT.Copy).then_inc(ad.sem, 1)
                        if a is not None:
                            act.wait_ge(ta.sem, ta.at("tT", a))
                            if not first(a):
                                act.wait_ge(ta.sem, ta.at("gnn", a - 1))
                            S.activation(tT[:, :, :], banks[0][:, :], ACT.Copy).then_inc(aa.sem, 1)
                        if c is not None:
                            act.wait_ge(vc.sem, vc.at("nmax", c))
                            if not first(c):
                                act.wait_ge(tc.sem, tc.at("prT", c - 1))
                            for t in range(TG):
                                for h in range(NH):
                                    last = S.activation(pr[:, t, h, :], sc[:, t, h, :], ACT.Exp, scale=SCALE,
                                                        bias=nmx[:, t * NH + h:t * NH + h + 1])
                            last.then_inc(ac.sem, 1)
                        if d is not None:
                            act.wait_ge(vd.sem, vd.at("f2", d))
                            if not first(d):
                                act.wait_ge(vd.sem, vd.at("ssv", d - 1))
                            for t in range(TG):
                                last = S.activation(junk[:, t, :], f2[:, t, :], ACT.Square, accum_out=ss[:, t:t + 1])
                            last.then_inc(ad.sem, 1)
                            act.wait_ge(td.sem, td.at("flatT", d))
                            if not first(d):
                                act.wait_ge(td.sem, td.at("logits", d - 1))
                            S.activation(flatT[:, :, :], banks[1][:, :], ACT.Copy).then_inc(ad.sem, 1)
                        if c is not None:
                            act.wait_ge(tc.sem, tc.at("prT", c))
                            if not first(c):
                                act.wait_ge(tc.sem, tc.at("y", c - 1))
                            for p in range(2):
                                last = S.activation(prT[:, p, :, :], banks[4 + p][:, :], ACT.Copy)
                            last.then_inc(ac.sem, 1)
                        if d is not None:
                            act.wait_ge(vr.sem, vr.at("dtop", d))
                            if not first(d):
                                act.wait_ge(vr.sem, vr.at("gate", d - 1))
                            S.activation(etop[:, :, :], dtop[:, :, :], ACT.Exp).then_inc(ar.sem, 1)
                        if b is not None:
                            act.wait_ge(tb.sem, tb.at("v", b))
                            act.wait_ge(pool_w, 5)
                            if not first(b):
                                act.wait_ge(tc.sem, tc.at("y", b - 1))
                            vp = banks[0][:, :].rearrange("p (g k d) -> p g k d", g=GR, k=2)
                            S.activation(v_diag[0:NN, :, :, 0:32], vp[0:NN], ACT.Copy)
                            S.activation(v_diag[NN:P, 1:GR, :, 33:65], vp[NN:P, 0:GR - 1], ACT.Copy)
                            S.activation(v_diag[NN:P, 0:1, :, 33:65], vp[NN:P, GR - 1:GR], ACT.Copy).then_inc(ab.sem, 1)
                    sweep(act, body, 4)

                @block.vector
                def _(dve):
                    dve.wait_ge(ld_w, 16 * 8)
                    V.tensor_copy(trib[:, :], cst[:, C_TRI:C_TRI + P]).then_inc(dve_w, 1)
                    V.tensor_copy(oneb[:, :], cst[:, C_ONE:C_ONE + P]).then_inc(dve_w, 1)
                    V.tensor_scalar(rws[:, :], rw[:, :], ln[:, 1:2], None, ALU.mult).then_inc(dve_w, 1)
                    V.tensor_scalar(wq_raw[:, :], wq_raw[:, :], ln[:, 0:1], None, ALU.mult).then_inc(dve_w, 1)
                    dve.wait_ge(dve_w, 4)
                    V.tensor_copy(wq_hi[:, :], wq_raw[:, :]).then_inc(dve_w, 1)
                    dve.wait_ge(dve_w, 5)
                    V.tensor_tensor(wq_lo[:, :], wq_raw[:, :], wq_hi[:, :].bitcast(f32), ALU.subtract).then_inc(dve_w, 1)

                    def held():
                        V.memset(spare[:, :], 0.0)

                    def layer_norm(steps, g, src, st, mv, eps_scale, names):
                        for t in range(TG):
                            last = V.bn_stats(st[:, t, :], src[:, t, :])
                        last.then_inc(steps.sem, 1)
                        dve.wait_ge(steps.sem, steps.at(names[0], g))
                        held()
                        for t in range(TG):
                            last = V.bn_aggr(mv[:, t, :], st[:, t, :])
                        last.then_inc(steps.sem, 1)
                        dve.wait_ge(steps.sem, steps.at(names[1], g))

                    def body(gs):
                        a, b, c, d, e = gs
                        if d is not None:
                            dve.wait_ge(tc.sem, tc.at("y", d))
                            ys = [banks[6 + j][:, 0:264].rearrange("p (t h e) -> p t h e", t=2, h=NH) for j in range(2)]
                            for j in range(2):
                                last = V.reciprocal(rden[:, 2 * j:2 * j + 2, :].unsqueeze(3), ys[j][:, :, :, 32:33])
                            last.then_inc(vy.sem, 1)
                            dve.wait_ge(vy.sem, vy.at("rden", d))
                            if not first(d):
                                dve.wait_ge(td.sem, td.at("yT", d - 1))
                            for j in range(2):
                                last = V.tensor_tensor(yn[:, 2 * j:2 * j + 2, :].rearrange("p t (h e) -> p t h e", h=NH),
                                                       ys[j][:, :, :, 0:32],
                                                       rden[:, 2 * j:2 * j + 2, :].unsqueeze(3).broadcast_to([P, 2, NH, HD]), ALU.mult)
                            last.then_inc(vy.sem, 1)
                        if b is not None:
                            dve.wait_ge(ab.sem, ab.at("hi", b))
                            if not first(b):
                                dve.wait_ge(tb.sem, tb.at("v", b - 1))
                            V.tensor_tensor(hT_lo[:, 0:GT], banks[0][:, :], hT_hi[:, 0:GT].bitcast(f32), ALU.subtract)
                            V.tensor_tensor(hT_lo[:, GT:], banks[0][:, 0:NN], hT_hi[:, GT:].bitcast(f32), ALU.subtract).then_inc(vb.sem, 1)
                        if a is not None:
                            dve.wait_ge(ld_x, a * 16 + 16)
                            layer_norm(va, a, xt, st_a, mv_a, None, ("stats", "moments"))
                            V.tensor_scalar(var_a[:, :], mv_a[:, :, 1], 1e-5, None, ALU.add).then_inc(va.sem, 1)
                            dve.wait_ge(pa.sem, pa.at("rstd", a))
                            if not first(a):
                                dve.wait_ge(ta.sem, ta.at("tT", a - 1))
                            for t in range(TG):
                                last = V.tensor_scalar(xn[:, t, :], xt[:, t, :], mv_a[:, t, 0:1], rs_a[:, t:t + 1],
                                                       ALU.subtract, ALU.mult)
                            last.then_inc(va.sem, 1)
                        if c is not None:
                            dve.wait_ge(tc.sem, tc.at("scores", c))
                            if not first(c):
                                dve.wait_ge(ac.sem, ac.at("exp", c - 1))
                            for h in range(NH):
                                last = V.tensor_tensor(sc[:, :, h, :], banks[4 + h][:, 0:TG * NN].rearrange("p (t s) -> p t s", t=TG),
                                                       cst[:, C_MASK:C_MASK + NN].unsqueeze(1).broadcast_to([P, TG, NN]), ALU.add)
                            last.then_inc(vc.sem, 1)
                            dve.wait_ge(vc.sem, vc.at("masked", c))
                            V.reduce_max(mx[:, :], sc[:, :, :, :].rearrange("p t h s -> p (t h) s"), AX.X).then_inc(vc.sem, 1)
                            dve.wait_ge(vc.sem, vc.at("max", c))
                            V.tensor_scalar(nmx[:, :], mx[:, :], -SCALE, None, ALU.mult).then_inc(vc.sem, 1)
                        if d is not None:
                            dve.wait_ge(td.sem, td.at("wo", d))
                            dve.wait_ge(pa.sem, pa.at("base", d))
                            if not first(d):
                                dve.wait_ge(vd.sem, vd.at("flat", d - 1))
                                dve.wait_ge(ad.sem, ad.at("sumsq", d - 1))
                            att = banks[1][:, :].rearrange("p (t c) -> p t c", t=TG)
                            V.tensor_tensor(f2[:, :, :], att, f_all[:, bass.ds(d * TG, TG), :], ALU.add).then_inc(vd.sem, 1)
                            V.tensor_tensor(base_all[:, bass.ds(d * TG, TG), :], att, base_all[:, bass.ds(d * TG, TG), :],
                                            ALU.add).then_inc(vd.sem, 1)

                        def rope(outs, names, swap):
                            for dst, bank, col, pe_step, step in outs:
                                dve.wait_ge(tb.sem, tb.at(pe_step, b))
                                if not first(b):
                                    dve.wait_ge(pb.sem, pb.at(names, b - 1))
                                V.tensor_tensor(dst[:, :].rearrange("p (g t) -> p g t", g=GR),
                                                banks[bank][:, :].rearrange("p (g t) -> p g t", g=GR),
                                                cst[:, col:col + NN].unsqueeze(1).broadcast_to([P, GR, NN]), ALU.mult).then_inc(vb.sem, 1)
                        if b is not None:
                            rope(((q_cos, 2, C_COS, "q", "q_cos"), (q_sin, 3, C_SIN, "q_swap", "q_sin")), "q", False)
                        if a is not None:
                            dve.wait_ge(ta.sem, ta.at("gnn", a))
                            dve.wait_ge(pa.sem, pa.at("xb", a))
                            if not first(a):
                                dve.wait_ge(pa.sem, pa.at("base", a - 1))
                            V.tensor_tensor(x1[:, :, :], banks[0][:, :].rearrange("p (t c) -> p t c", t=TG), xb[:, :, :],
                                            ALU.add).then_inc(va.sem, 1)
                            dve.wait_ge(va.sem, va.at("x1", a))
                            layer_norm(va, a, x1, st_b, mv_b, None, ("stats1", "moments1"))
                            V.tensor_scalar(var_b[:, 0, :], mv_b[:, :, 1], 1e-5, None, ALU.add).then_inc(va.sem, 1)
                            V.tensor_scalar(var_b[:, 1, :], mv_b[:, :, 1], 1.0 + 1e-6, 1e-11, ALU.mult, ALU.add).then_inc(va.sem, 1)
                            dve.wait_ge(pa.sem, pa.at("rstd1", a))
                            for t in range(TG):
                                last = V.tensor_scalar(f_all[:, bass.ds(a * TG + t, 1), :].rearrange("p o c -> p (o c)"), x1[:, t, :], mv_b[:, t, 0:1],
                                                       rs_b[:, 0, t:t + 1], ALU.subtract, ALU.mult)
                            last.then_inc(va.sem, 1)
                            if not first(a):
                                dve.wait_ge(tb.sem, tb.at("hT", a - 1))
                            for t in range(TG):
                                last = V.tensor_scalar(hp[:, t, :], x1[:, t, :], mv_b[:, t, 0:1], rs_b[:, 1, t:t + 1],
                                                       ALU.subtract, ALU.mult)
                            last.then_inc(va.sem, 1)
                        if d is not None:
                            dve.wait_ge(ad.sem, ad.at("sumsq", d))
                            V.tensor_scalar(ssv[:, :], ss[:, :], C * 1e-6, None, ALU.add).then_inc(vd.sem, 1)
                        if b is not None:
                            rope(((k_cos, 2, C_COS, "k", "k_cos"), (k_sin, 3, C_SIN, "k_swap", "k_sin")), "k", False)
                        if d is not None:
                            dve.wait_ge(pd.sem, pd.at("rms", d))
                            if not first(d):
                                dve.wait_ge(scattered, d * 16 * 2 * TG)
                            for t in range(TG):
                                last = V.tensor_scalar(flat[:, t, :], f2[:, t, :], rr2[:, t:t + 1], float(C) ** 0.5,
                                                       ALU.mult, ALU.mult)
                            last.then_inc(vd.sem, 1)
                        if d is not None:
                            router(d)

                    def router(d):
                        dve.wait_ge(td.sem, td.at("logits", d))
                        V.tensor_copy(lg[:, :, :], banks[1][:, 0:TG * 8].rearrange("p (t e) -> p t e", t=TG)).then_inc(vr.sem, 1)
                        dve.wait_ge(vr.sem, vr.at("lg", d))
                        held()
                        for t in range(TG):
                            last = V.max(top[:, t, :], lg[:, t, :])
                        last.then_inc(vr.sem, 1)
                        dve.wait_ge(vr.sem, vr.at("top", d))
                        held()
                        for t in range(TG):
                            last = V.max_index(topi[:, t, :], top[:, t, :], lg[:, t, :])
                        last.then_inc(vr.sem, 1)
                        dve.wait_ge(vr.sem, vr.at("topi", d))
                        V.tensor_copy(topf[:, :, :], topi[:, :, 0:2]).then_inc(vr.sem, 1)
                        dve.wait_ge(vr.sem, vr.at("topf", d))
                        V.tensor_tensor(oh[:, :, :, :], topf[:, :, :].unsqueeze(3).broadcast_to([P, TG, 2, 8]),
                                        iota8.unsqueeze(1).unsqueeze(1).broadcast_to([P, TG, 2, 8]), ALU.is_equal).then_inc(vr.sem, 1)
                        dve.wait_ge(vr.sem, vr.at("oh", d))
                        if not first(d):
                            dve.wait_ge(td.sem, td.at("rank", d - 1))
                        V.tensor_tensor(sel[:, :, :], oh[:, :, 0, :], oh[:, :, 1, :], ALU.add).then_inc(vr.sem, 1)
                        if first(d):
                            dve.wait_ge(pool_w, 2)
                        V.tensor_copy(carry_b[:, :], carry[:, :]).then_inc(vr.sem, 1)
                        dve.wait_ge(vr.sem, vr.at("carry_b", d))
                        V.reduce_sum(selsum[:, :], sel[:, :, :].rearrange("p t e -> p e t"), AX.X).then_inc(vr.sem, 1)
                        dve.wait_ge(vr.sem, vr.at("selsum", d))
                        V.tensor_tensor(carry[:, :], carry[:, :], selsum[:, :], ALU.add).then_inc(vr.sem, 1)
                        V.tensor_tensor(dtop[:, :, :], top[:, :, :], top[:, :, 0:1].broadcast_to([P, TG, 8]), ALU.subtract).then_inc(vr.sem, 1)
                        dve.wait_ge(ar.sem, ar.at("etop", d))
                        V.reduce_sum(z[:, :], etop[:, :, :], AX.X)
                        V.tensor_tensor(s2[:, :], etop[:, :, 0], etop[:, :, 1], ALU.add).then_inc(vr.sem, 1)
                        dve.wait_ge(vr.sem, vr.at("z", d))
                        V.scalar_tensor_tensor(den[:, :], z[:, :], 1e-9, s2[:, :], ALU.mult, ALU.add).then_inc(vr.sem, 1)
                        dve.wait_ge(vr.sem, vr.at("den", d))
                        V.reciprocal(rec[:, :], den[:, :]).then_inc(vr.sem, 1)
                        dve.wait_ge(vr.sem, vr.at("rec", d))
                        V.tensor_tensor(gates_all[:, bass.ds(d, 1), :].rearrange("p o (t k) -> p (o t) k", k=2), etop[:, :, 0:2],
                                        rec[:, :].unsqueeze(2).broadcast_to([P, TG, 2]), ALU.mult).then_inc(vr.sem, 1)
                        dve.wait_ge(td.sem, td.at("rank", d))
                        V.tensor_tensor(rank[:, :, :], banks[1][:, 0:TG * 8].rearrange("p (t e) -> p t e", t=TG),
                                        cst[:, C_BASE:C_BASE + 8].unsqueeze(1).broadcast_to([P, TG, 8]), ALU.add).then_inc(vr.sem, 1)
                        dve.wait_ge(vr.sem, vr.at("rank", d))
                        V.tensor_tensor(ohr[:, :, :, :], oh[:, :, :, :], rank[:, :, :].unsqueeze(2).broadcast_to([P, TG, 2, 8]),
                                        ALU.mult).then_inc(vr.sem, 1)
                        dve.wait_ge(vr.sem, vr.at("ohr", d))
                        V.reduce_sum(slotf[:, :], ohr[:, :, :, :].rearrange("p t k e -> p (t k) e"), AX.X).then_inc(vr.sem, 1)
                        dve.wait_ge(vr.sem, vr.at("slotf", d))
                        if not first(d):
                            dve.wait_ge(scattered, d * 16 * 2 * TG)
                        V.tensor_copy(slot_now[:, :], slotf[:, :]).then_inc(vr.sem, 1)
                        V.tensor_copy(slots_f[:, bass.ds(d, 1), :].rearrange("p o s -> p (o s)"), slotf[:, :]).then_inc(vr.sem, 1)

                    sweep(dve, body, 4)

                    n = [0]

                    def link(ins):
                        n[0] += 1
                        ins.then_inc(dve_t, 1)
                        dve.wait_ge(dve_t, n[0])

                    dve.wait_ge(vr.sem, vr.at("keep", NG - 1))
                    link(V.tensor_copy(carry_b[:, :], carry[:, :]))
                    dve.wait_ge(pe_t, 1)
                    link(V.tensor_scalar(cnti[:, :], banks[0][:, 0:8], float(P - 1), None, ALU.add))
                    link(V.tensor_tensor(fill[:, :], banks[0][0:1, 0:8], cst[0:1, C_BASE:C_BASE + 8], ALU.add))
                    link(V.tensor_scalar(cnti[:, :], cnti[:, :], 7, None, ALU.arith_shift_right))
                    link(V.tensor_copy(nblk[:, :], cnti[:, :]))
                    link(V.tensor_tensor(tri_nb[:, :, :], nblk[0:1, :].unsqueeze(1).broadcast_to([1, 8, 8]),
                                         cst[0:1, C_TRI8:C_TRI8 + 64].rearrange("p (a b) -> p a b", a=8), ALU.mult))
                    link(V.reduce_sum(cum[:, :], tri_nb[:, :, :], AX.X))
                    link(V.tensor_tensor(past[:, :, :], cst[0:1, C_BLK:C_BLK + NBLK].unsqueeze(2).broadcast_to([1, NBLK, 8]),
                                         cum[:, :].unsqueeze(1).broadcast_to([1, NBLK, 8]), ALU.is_ge))
                    link(V.tensor_tensor(pastn[:, :, :], past[:, :, :], nblk[0:1, :].unsqueeze(1).broadcast_to([1, NBLK, 8]), ALU.mult))
                    link(V.reduce_sum(bexp[:, :], past[:, :, :], AX.X))
                    link(V.reduce_sum(bprev[:, :], pastn[:, :, :], AX.X))
                    link(V.tensor_tensor(brow[:, :], cst[0:1, C_BLK:C_BLK + NBLK], bprev[:, :], ALU.subtract))
                    link(V.scalar_tensor_tensor(brow[:, :], bexp[:, :], float(REG), brow[:, :], ALU.mult, ALU.add))
                    link(V.tensor_scalar(table[:, 1, :], brow[:, :], float(P), None, ALU.mult))
                    link(V.tensor_scalar(table[:, 0, :], bexp[:, :], float(NE0 - 1), None, ALU.min))
                    link(V.tensor_scalar(gaps[:, :], nblk[:, :], -float(REG), float(P), ALU.add, ALU.mult))
                    slots = slots_f[:, :, :].rearrange("p g s -> p (g s)")
                    link(V.tensor_tensor(gap[:, :, :], slots.unsqueeze(2).broadcast_to([P, NG * 2 * TG, 7]),
                                         cst[:, C_BASE + 1:C_BASE + 8].unsqueeze(1).broadcast_to([P, NG * 2 * TG, 7]), ALU.is_ge))
                    link(V.tensor_tensor(gap[:, :, :], gap[:, :, :], gaps[:, 0:7].unsqueeze(1).broadcast_to([P, NG * 2 * TG, 7]), ALU.mult))
                    link(V.reduce_sum(back[:, :], gap[:, :, :], AX.X))
                    link(V.tensor_tensor(slots_all[:, :, :].rearrange("p g s -> p (g s)"), slots, back[:, :], ALU.add))

                @block.tensor
                def _(pe):
                    def body(gs):
                        a, b, c, d, e = gs
                        if b is not None:
                            pe.wait_ge(va.sem, va.at("hp", b))
                            if first(b):
                                pe.wait_ge(ld_w, 16 * 8)
                            else:
                                pe.wait_ge(ab.sem, ab.at("v", b - 1))
                            for t in range(TG):
                                last = T.transpose(banks[0][:, t * P:(t + 1) * P], hp[:, t, :], ident)
                            last.then_inc(tb.sem, 1)
                        if d is not None:
                            pe.wait_ge(vy.sem, vy.at("yn", d))
                            if not first(d):
                                pe.wait_ge(vr.sem, vr.at("rank", d - 1))
                            for t in range(TG):
                                last = T.transpose(banks[1][:, t * P:(t + 1) * P], yn[:, t, :], ident)
                            last.then_inc(td.sem, 1)
                        if c is not None:
                            pe.wait_ge(pb.sem, pb.at("k", c))
                            for t in range(TG):
                                for gi in range(2):
                                    tok = slice(t * P + gi * NN, t * P + (gi + 1) * NN)
                                    for h in range(NH):
                                        hs = slice(h * HD, (h + 1) * HD)
                                        last = T.matmul(banks[4 + h][gi * NN:(gi + 1) * NN, t * NN:(t + 1) * NN],
                                                        q_rot[hs, tok], k_rot[hs, tok], start=True, stop=True)
                            last.then_inc(tc.sem, 1)
                        if a is not None:
                            pe.wait_ge(ld_adj, a * 32 + 32)
                            pe.wait_ge(va.sem, va.at("xn", a))
                            if b is not None:
                                pe.wait_ge(vb.sem, vb.at("lo", b))
                            for t in range(TG):
                                last = T.matmul(banks[0][:, t * P:(t + 1) * P], xn[:, t, :], adjt[:, t, :], start=True, stop=True)
                            last.then_inc(ta.sem, 1)
                        if d is not None:
                            pe.wait_ge(ad.sem, ad.at("yT", d))
                            for t in range(TG):
                                last = T.matmul(banks[1][:, t * P:(t + 1) * P], yT[:, t, :], wo_sb[:, :], start=True, stop=True)
                            last.then_inc(td.sem, 1)

                        def project(n, bank, lo):
                            for q, (w, h) in enumerate(((wq_hi, hT_hi), (wq_hi, hT_lo), (wq_lo, hT_hi))):
                                last = T.matmul(banks[bank][:, :], w[:, n * P:(n + 1) * P], h[:, 0:GT], start=q == 0, stop=q == 2)
                            last.then_inc(tb.sem, 1)
                        if b is not None:
                            pe.wait_ge(vb.sem, vb.at("lo", b))
                            pe.wait_ge(dve_w, 6)
                            if not first(b):
                                pe.wait_ge(vb.sem, vb.at("k_sin", b - 1))
                            project(0, 2, None)
                            project(1, 3, None)
                        if a is not None:
                            if first(a):
                                pe.wait_ge(ld_w, 16 * 8)
                            pe.wait_ge(aa.sem, aa.at("tT", a))
                            for t in range(TG):
                                last = T.matmul(banks[0][:, t * P:(t + 1) * P], tT[:, t, :], gw[:, :], start=True, stop=True)
                            last.then_inc(ta.sem, 1)
                        if b is not None:
                            pe.wait_ge(vb.sem, vb.at("q_cos", b))
                            project(2, 2, None)
                            pe.wait_ge(vb.sem, vb.at("q_sin", b))
                            project(3, 3, None)
                        if d is not None:
                            pe.wait_ge(vd.sem, vd.at("flat", d))
                            for t in range(TG):
                                last = T.transpose(banks[1][:, t * P:(t + 1) * P], flat[:, t, :], ident)
                            last.then_inc(td.sem, 1)
                        if c is not None:
                            pe.wait_ge(ac.sem, ac.at("exp", c))
                            for p in range(2):
                                for t in range(TG):
                                    last = T.transpose(banks[4 + p][:, t * P:(t + 1) * P],
                                                       pr[:, t, 2 * p:2 * p + 2, :].rearrange("p h s -> p (h s)"), ident)
                            last.then_inc(tc.sem, 1)
                        if d is not None:
                            pe.wait_ge(ad.sem, ad.at("flatT", d))
                            for t in range(TG):
                                last = T.matmul(banks[1][:, t * 8:t * 8 + 8], flatT[:, t, :], rws[:, :], start=True, stop=True)
                            last.then_inc(td.sem, 1)
                        if d is not None:
                            pe.wait_ge(vr.sem, vr.at("carry_b", d))
                            T.matmul(banks[1][:, 0:TG * 8], trib[:, :], sel[:, :, :].rearrange("p t e -> p (t e)"), start=True, stop=False)
                            T.matmul(banks[1][:, 0:TG * 8], oneb[:, :], carry_b[:, :].unsqueeze(1).broadcast_to([P, TG, 8]),
                                     start=False, stop=False)
                            for t in range(TG - 1):
                                last = T.matmul(banks[1][:, (t + 1) * 8:TG * 8], oneb[:, :],
                                                sel[:, t:t + 1, :].broadcast_to([P, TG - 1 - t, 8]), start=False, stop=t == TG - 2)
                            last.then_inc(td.sem, 1)
                        if c is not None:
                            pe.wait_ge(ac.sem, ac.at("prT", c))
                            pe.wait_ge(ab.sem, ab.at("v", c))
                            for t in range(TG):
                                for gi in range(2):
                                    for p in range(2):
                                        last = T.matmul(banks[6 + t // 2][gi * NN:(gi + 1) * NN, (t % 2) * 132 + p * 66:(t % 2) * 132 + p * 66 + 66],
                                                        prT[:, p, t, gi * NN:(gi + 1) * NN], v_diag[:, 2 * t + gi, p, :],
                                                        start=True, stop=True)
                            last.then_inc(tc.sem, 1)
                        if b is not None:
                            if a is not None:
                                pe.wait_ge(va.sem, va.at("x1", a))
                            for gr in range(GR):
                                for q, (h, w) in enumerate(((hT_hi, wq_hi), (hT_hi, wq_lo), (hT_lo, wq_hi))):
                                    last = T.matmul(banks[0][:, gr * NN:(gr + 1) * NN],
                                                    h[:, gr * NN:gr * NN + P],
                                                    w[:, 512:576], start=q == 0, stop=q == 2)
                            last.then_inc(tb.sem, 1)
                    sweep(pe, body, 4)
                    pe.wait_ge(dve_t, 1)
                    T.matmul(banks[0][:, 0:8], oneb[:, :], carry_b[:, :], start=True, stop=True).then_inc(pe_t, 1)

        with ExitStack() as ctx:
            sb, sem = sb_in(ctx), sem_in(ctx)
            xs, ys = sb("xs", [P, 4, C]), sb("ys", [P, 4, C])
            xT_hi, xT_lo = sb("xT_hi", [P, 2, P], f32r), sb("xT_lo", [P, 2, P], f32r)
            act1, prod = sb("act1", [P, 2, HIDP]), sb("prod", [P, 2, KC * P])
            prodT = sb("prodT", [P, 2, KC * P])
            ld = [sem(f"ld_slots{u}") for u in range(4)]
            st = [sem(f"st_slots{u}") for u in range(4)]
            padded = sem("padded")
            pt = [sem(n) for n in ("pe_xT", "pe_h", "pe_prodT", "pe_y")]
            xT_done, h_done, prodT_done, y_done = pt
            hi_done, silu_done, prodT_copied = sem("hi_done"), sem("silu_done"), sem("prodT_copied")
            lo_done, prod_done, y_copied = sem("lo_done"), sem("prod_done"), sem("y_copied")

            def quarter(k, u):
                return (k // 4 + 1) * 16 if isinstance(k, int) else (k - u) * 4 + 16

            def blocks(engine, body, skew):
                for k in range(8):
                    body(k, k % 4)
                with engine.Fori(2, NBLK // 4) as j:
                    for u in range(4):
                        body(j * 4 + u, u)
                for k in range(NBLK, NBLK + skew):
                    body(k, k % 4)

            def live(k, back):
                return not isinstance(k, int) or 0 <= k - back < NBLK

            def live_prior(k, back):
                return not isinstance(k, int) or k - back >= 0

            with nc.Block() as block:
                @block.sync
                def _(sp):
                    def row_of(k):
                        return sp.value_load(table[0:1, 1, bass.ds(k, 1)], min_val=0, max_val=ROWS - P)

                    def body(k, u):
                        if live(k, 0):
                            row = row_of(k)
                            if live_prior(k, 4):
                                sp.wait_ge(xT_done, k - 3)
                            sp.dma_start(xs[:, u, :], slots_in[bass.ds(row, P), :]).then_inc(ld[u], 16)
                        if live(k, 7):
                            sp.wait_ge(y_copied, k - 6)
                            sp.dma_start(slots_out[bass.ds((k - 7) * P, P), :], ys[:, (u - 7) % 4, :]).then_inc(st[(u - 7) % 4], 16)
                    blocks(sp, body, 7)
                    for u in range(4):
                        sp.wait_ge(st[u], NBLK // 4 * 16)

                @block.gpsimd
                def _(pool):
                    G.memset(prod[:, :, :], 0.0).then_inc(padded, 1)

                @block.scalar
                def _(act):
                    S.preload_act_table(ACT.Silu)

                    def body(k, u):
                        if live(k, 0):
                            act.wait_ge(xT_done, k + 1)
                            if live_prior(k, 2):
                                act.wait_ge(h_done, k - 1)
                            S.activation(xT_hi[:, u % 2, :], banks[0][:, 0:P], ACT.Copy).then_inc(hi_done, 1)
                        if live(k, 1):
                            act.wait_ge(h_done, k)
                            if live_prior(k, 3):
                                act.wait_ge(prod_done, k - 2)
                            S.activation(act1[:, (u - 1) % 2, :], banks[1 + (u - 1) % 2][:, 0:HIDP], ACT.Silu).then_inc(silu_done, 1)
                        if live(k, 2):
                            act.wait_ge(prodT_done, k - 1)
                            if live_prior(k, 4):
                                act.wait_ge(y_done, k - 3)
                            S.activation(prodT[:, u % 2, :], banks[5 + u % 2][:, 0:KC * P], ACT.Copy).then_inc(prodT_copied, 1)
                    blocks(act, body, 2)

                @block.vector
                def _(dve):
                    dve.wait_ge(padded, 1)

                    def body(k, u):
                        if live(k, 0):
                            dve.wait_ge(hi_done, k + 1)
                            if live_prior(k, 2):
                                dve.wait_ge(h_done, k - 1)
                            V.tensor_tensor(xT_lo[:, u % 2, :], banks[0][:, 0:P], xT_hi[:, u % 2, :].bitcast(f32), ALU.subtract).then_inc(lo_done, 1)
                        if live(k, 1):
                            dve.wait_ge(silu_done, k)
                            if live_prior(k, 3):
                                dve.wait_ge(prodT_done, k - 2)
                            V.tensor_tensor(prod[:, (u - 1) % 2, 0:HIDP], banks[3 + (u - 1) % 2][:, 0:HIDP], act1[:, (u - 1) % 2, :],
                                            ALU.mult).then_inc(prod_done, 1)
                        if live(k, 3):
                            dve.wait_ge(y_done, k - 2)
                            if live_prior(k, 7):
                                dve.wait_ge(st[(u - 3) % 4], quarter(k - 7, (u - 3) % 4))
                            V.tensor_copy(ys[:, (u - 3) % 4, :], banks[7][:, 0:C]).then_inc(y_copied, 1)
                    blocks(dve, body, 3)

                @block.tensor
                def _(pe):
                    def expert(k):
                        return pe.value_load(table[0:1, 0, bass.ds(k, 1)], min_val=0, max_val=NE0 - 1)

                    def body(k, u):
                        if live(k, 0):
                            pe.wait_ge(ld[u], quarter(k, u))
                            if live_prior(k, 1):
                                pe.wait_ge(lo_done, k)
                            T.transpose(banks[0][:, 0:P], xs[:, u, :], ident).then_inc(xT_done, 1)
                        if live(k, 1):
                            e, par = expert(k - 1), (u - 1) % 2
                            pe.wait_ge(lo_done, k)
                            if live_prior(k, 3):
                                pe.wait_ge(prod_done, k - 2)
                            for n in range(2):
                                for q, (xx, ww) in enumerate(((xT_hi, w13_hi), (xT_hi, w13_lo), (xT_lo, w13_hi))):
                                    last = T.matmul(banks[1 + 2 * n + par][:, 0:HIDP], xx[:, par, :],
                                                    ww[:, bass.ds(e * (2 * HIDP) + n * HIDP, HIDP)], start=q == 0, stop=q == 2)
                            last.then_inc(h_done, 1)
                        if live(k, 2):
                            pe.wait_ge(prod_done, k - 1)
                            if live_prior(k, 4):
                                pe.wait_ge(prodT_copied, k - 3)
                            for n in range(KC):
                                last = T.transpose(banks[5 + u % 2][:, n * P:(n + 1) * P], prod[:, u % 2, n * P:(n + 1) * P], ident)
                            last.then_inc(prodT_done, 1)
                        if live(k, 3):
                            e = expert(k - 3)
                            pe.wait_ge(prodT_copied, k - 2)
                            if live_prior(k, 4):
                                pe.wait_ge(y_copied, k - 3)
                            for n in range(KC):
                                last = T.matmul(banks[7][:, 0:C], prodT[:, (u - 3) % 2, n * P:(n + 1) * P],
                                                w2_sb[:, bass.ds(e * (KC * C) + n * C, C)], start=n == 0, stop=n == KC - 1)
                            last.then_inc(y_done, 1)
                    blocks(pe, body, 3)

        with ExitStack() as ctx:
            sb, sem = sb_in(ctx), sem_in(ctx)
            gw, gb = sb("gw1", [P, C]), sb("gb1", [P, C])
            rw1, rw1_hi, rw1_lo = sb("rw1", [P, RH]), sb("rw1_hi", [P, RH], f32r), sb("rw1_lo", [P, RH], f32r)
            rb1, rw2, rb2 = sb("rb1", [RH, 1]), sb("rw2", [RH, 8]), sb("rb2", [P, 8])
            ew1_hi, ew1_lo = sb("ew1_hi", [P, NE1 * C], f32r), sb("ew1_lo", [P, NE1 * C], f32r)
            ew1, ew2, ew3 = (sb(n, [P, NE1 * C]) for n in ("ew1", "ew2", "ew3"))
            eb1, eb2, eb3 = sb("eb1", [P, NE1]), sb("eb2", [P, NE1]), sb("eb3", [NE1, C])
            mhalf = sb("mhalf1", [P, TG])
            adjt = [sb(f"adjt_c{i}", [P, TG, C]) for i in range(2)]
            rows = [sb(f"expert_rows{i}", [P, 2 * TG, C]) for i in range(2)]
            slot_now = [sb(f"slot_c{i}", [P, 2 * TG], u32) for i in range(2)]
            gate_now = [sb(f"gate_c{i}", [P, 2 * TG]) for i in range(2)]
            deg = [sb(f"deg{i}", [P, TG]) for i in range(2)]
            f3_hi = [sb(f"f3_hi{i}", [P, GT], f32r) for i in range(2)]
            f3_lo = [sb(f"f3_lo{i}", [P, GT], f32r) for i in range(2)]
            gateT = [sb(f"gateT{i}", [8, GT]) for i in range(2)]
            gate_bc = [sb(f"gate_bc{i}", [P, NE1, GT]) for i in range(2)]
            x2a, x2, xn, xb, tT, f3, ob = (sb(n, [P, TG, C]) for n in ("x2a", "x2", "xn_c", "xb_c", "tT_c", "f3", "ob"))
            degv, dscale, xscale = sb("degv", [P, TG]), sb("dscale", [P, TG]), sb("xscale", [P, TG])
            st_a, mv_a, var_a, rs_a = sb("st_c", [P, TG, 6]), sb("mv_c", [P, TG, 2]), sb("var_c", [P, TG]), sb("rs_c", [P, TG])
            st_b, mv_b, var_b, rs_b = sb("st_d", [P, TG, 6]), sb("mv_d", [P, TG, 2]), sb("var_d", [P, TG]), sb("rs_d", [P, TG])
            rhT = sb("rhT", [RH, GT])
            lg, top, topi = sb("lg_c", [P, TG, 8]), sb("top_c", [P, TG, 8]), sb("topi_c", [P, TG, 8], u32)
            topf, oh, dtop, etop = sb("topf_c", [P, TG, 2]), sb("oh_c", [P, TG, 2, 8]), sb("dtop_c", [P, TG, 8]), sb("etop_c", [P, TG, 8])
            z, zr, pk, dp, ep, e1 = sb("z_c", [P, TG]), sb("zr", [P, TG]), sb("pk", [P, TG, 2]), sb("dp", [P, TG]), sb("ep", [P, TG]), sb("e1", [P, TG])
            rk, ohr, gate = sb("rk", [P, TG, 2]), sb("ohr_c", [P, TG, 2, 8]), sb("gate", [P, TG, 8])
            h1 = [sb(f"h1_{i}", [P, GT]) for i in range(2)]
            h2 = [sb(f"h2_{i}", [P, GT]) for i in range(2)]
            h2g = [sb(f"h2g_{i}", [P, GT]) for i in range(2)]
            oT = sb("oT", [P, GT])
            spare, spare2 = sb("spare_c", [P, 1]), sb("spare_d", [P, 1])

            ld_w, ld_adj = sem("ld_w1"), [sem(f"ld_adj_c{i}") for i in range(2)]
            zeroed, dve_w = sem("zeroed1"), sem("dve_w1")
            gathered = [sem(f"gathered{i}") for i in range(2)]
            gates_loaded = [sem(f"gates_loaded{i}") for i in range(2)]
            gates_stored, stored = sem("gates_stored"), sem("stored")
            NW = 13
            vs = Steps(sem("vs"), "pick")
            va = Steps(sem("va1"), "degv add0 add1 stats moments var scale xn")
            vb = Steps(sem("vb1"), "x3 stats moments var f3")
            vc = Steps(sem("vc1"), "lo lg top topi topf oh dtop z zr pk dp e1 rk0 rk1 ohr gate")
            vd = Steps(sem("vd1"), "g0 g1 g2 g3 g4 g5 out")
            ab = Steps(sem("ab1"), "tT")
            ac = Steps(sem("ac1"), "hi rh etop ep gateT")
            ad = Steps(sem("ad1"), "a0 a1 b0 a2 b1 a3 b2 a4 b3 a5 b4 b5 oT")
            pa = Steps(sem("pa1"), "deg rstd")
            pb = Steps(sem("pb1"), "xb rstd")
            ta = Steps(sem("ta1"), "deg")
            tb = Steps(sem("tb1"), "tT gnn")
            tc = Steps(sem("tc1"), "f3T rh logits gateT")
            td = Steps(sem("td1"), "a0 a1 b0 a2 b1 c0 a3 b2 c1 a4 b3 c2 a5 b4 c3 b5 c4 c5 oT")

            def sweep(engine, body):
                def step(i, u):
                    gs = [i - k for k in range(4)]
                    if isinstance(i, int):
                        gs = [g if 0 <= g < NG else None for g in gs]
                    body(gs, [(u - k) % 2 for k in range(4)])
                for i in range(4):
                    step(i, i)
                with engine.Fori(2, NG // 2) as j:
                    for u in range(2):
                        step(j * 2 + u, u)
                for i in range(NG, NG + 3):
                    step(i, i)

            def pair(g, p):
                return (g // 2 + 1) * 16 if isinstance(g, int) else (g - p) * 8 + 16

            with nc.Block() as block:
                @block.sync
                def _(sp):
                    for dst, src in ((gw[:, :], gnn1_w), (gb[:, :], gnn1_b.partition_broadcast(P)), (rw1[:, :], r1_w1),
                                     (rb1[:, :], r1_b1), (rw2[:, :], r1_w2), (ew1[:, :], e_w1), (ew2[:, :], e_w2), (ew3[:, :], e_w3),
                                     (eb1[:, :], e_b1), (eb2[:, :], e_b2), (eb3[:, :], e_b3)):
                        sp.dma_start(dst, src).then_inc(ld_w, 16)
                    sp.wait_ge(zeroed, 4)
                    sp.dma_start(rb2[:, 0:NE1], r1_b2.partition_broadcast(P)).then_inc(ld_w, 16)
                    sp.dma_start(cst[:, :], consts).then_inc(ld_w, 16)

                    def body(gs, ps):
                        a, b, c, d = gs
                        if a is not None:
                            if not (isinstance(a, int) and a < 2):
                                sp.wait_ge(tb.sem, tb.at("tT", a - 2))
                            src = adj_t[bass.ds(a * GT, GT), :].rearrange("(t b m) n -> b m t n", b=2, m=NN)
                            for k in range(2):
                                sp.dma_start(adjt[ps[0]][k * NN:(k + 1) * NN, :, k * NN:(k + 1) * NN], src[k]).then_inc(ld_adj[ps[0]], 16)
                        if c is not None:
                            if not (isinstance(c, int) and c < 2):
                                sp.wait_ge(vd.sem, vd.at("g5", c - 2))
                            sp.wait_ge(ac.sem, ac.at("gateT", c))
                            sp.dma_start(gates_dram[ps[2]], gateT[ps[2]][0:NE1, :]).then_inc(gates_stored, 16)
                            sp.wait_ge(gates_stored, c * 16 + 16)
                            sp.dma_start(gate_bc[ps[2]][:, :, :], gates_dram[ps[2]].partition_broadcast(P)).then_inc(gates_loaded[ps[2]], 16)
                        if d is not None:
                            sp.wait_ge(vd.sem, vd.at("out", d))
                            sp.dma_start(out[bass.ds(d * GT, GT), :].rearrange("(t p) c -> p t c", p=P), ob[:, :, :]).then_inc(stored, 16)
                    sweep(sp, body)
                    sp.wait_ge(stored, 16 * NG)

                @block.gpsimd
                def _(pool):
                    G.memset(adjt[0][:, :, :], 0.0).then_inc(zeroed, 1)
                    G.memset(adjt[1][:, :, :], 0.0).then_inc(zeroed, 1)
                    G.memset(rb2[:, :], -1e30).then_inc(zeroed, 1)
                    G.memset(mhalf[:, :], -0.5).then_inc(zeroed, 1)
                    pool.wait_ge(ld_w, 16 * NW)

                    def body(gs, ps):
                        a, b, c, d = gs
                        if b is not None:
                            if not first(b):
                                pool.wait_ge(vb.sem, vb.at("x3", b - 1))
                            pool.wait_ge(va.sem, va.at("add1", b))
                            G.tensor_tensor(xb[:, :, :], x2[:, :, :], gb[:, :].unsqueeze(1).broadcast_to([P, TG, C]),
                                            ALU.add).then_inc(pb.sem, 1)
                        if a is not None:
                            pool.wait_ge(vs.sem, vs.at("pick", a))
                            if not (isinstance(a, int) and a < 2):
                                pool.wait_ge(va.sem, va.at("add1", a - 2))
                            G.tensor_tensor(spare[:, :], mhalf[:, 0:1], mhalf[:, 0:1], ALU.add)
                            for n in range(2 * TG):
                                G.indirect_dma_start(out=rows[ps[0]][:, n, :], out_offset=None, in_=slots_out,
                                                     in_offset=bass.IndirectOffsetOnAxis(ap=slot_now[ps[0]][:, n:n + 1], axis=0),
                                                     bounds_check=NBLK * P - 1).then_inc(gathered[ps[0]], 16)
                        if b is not None:
                            pool.wait_ge(vb.sem, vb.at("var", b))
                            G.tensor_tensor(rs_b[:, :], var_b[:, :], mhalf[:, :], ALU.pow).then_inc(pb.sem, 1)
                        if a is not None:
                            pool.wait_ge(va.sem, va.at("degv", a))
                            G.tensor_tensor(deg[ps[0]][:, :], degv[:, :], mhalf[:, :], ALU.pow).then_inc(pa.sem, 1)
                            pool.wait_ge(va.sem, va.at("var", a))
                            G.tensor_tensor(rs_a[:, :], var_a[:, :], mhalf[:, :], ALU.pow).then_inc(pa.sem, 1)
                    sweep(pool, body)

                @block.scalar
                def _(act):
                    S.preload_act_table(ACT.Exp)
                    act.wait_ge(ld_w, 16 * NW)

                    def body(gs, ps):
                        a, b, c, d = gs

                        def relu_a(n):
                            if d is None:
                                return
                            act.wait_ge(td.sem, td.at(f"a{n}", d))
                            if n >= 2:
                                act.wait_ge(td.sem, td.at(f"b{n - 2}", d))
                            S.activation(h1[n % 2][:, :], banks[n % 2][:, :], ACT.Relu, bias=eb1[:, n:n + 1]).then_inc(ad.sem, 1)

                        def relu_b(n):
                            if d is None:
                                return
                            act.wait_ge(td.sem, td.at(f"b{n}", d))
                            if n >= 2:
                                act.wait_ge(vd.sem, vd.at(f"g{n - 2}", d))
                            S.activation(h2[n % 2][:, :], banks[2 + n % 2][:, :], ACT.Relu, bias=eb2[:, n:n + 1]).then_inc(ad.sem, 1)

                        if c is not None:
                            act.wait_ge(tc.sem, tc.at("f3T", c))
                            if not (isinstance(c, int) and c < 2):
                                act.wait_ge(td.sem, td.at("a5", c - 2))
                            S.activation(f3_hi[ps[2]][:, :], banks[6][:, :], ACT.Copy).then_inc(ac.sem, 1)
                        relu_a(0)
                        relu_a(1)
                        if b is not None:
                            act.wait_ge(tb.sem, tb.at("tT", b))
                            if not first(b):
                                act.wait_ge(tb.sem, tb.at("gnn", b - 1))
                            S.activation(tT[:, :, :], banks[5][:, :], ACT.Copy).then_inc(ab.sem, 1)
                        relu_b(0)
                        if c is not None:
                            act.wait_ge(tc.sem, tc.at("rh", c))
                            if not first(c):
                                act.wait_ge(tc.sem, tc.at("logits", c - 1))
                            S.activation(rhT[:, :], banks[6][0:RH, :], ACT.Relu, bias=rb1[:, :]).then_inc(ac.sem, 1)
                        relu_a(2)
                        relu_b(1)
                        relu_a(3)
                        relu_b(2)
                        relu_a(4)
                        if c is not None:
                            act.wait_ge(vc.sem, vc.at("dtop", c))
                            if not first(c):
                                act.wait_ge(vc.sem, vc.at("pk", c - 1))
                            S.activation(etop[:, :, :], dtop[:, :, :], ACT.Exp).then_inc(ac.sem, 1)
                        relu_b(3)
                        relu_a(5)
                        if c is not None:
                            act.wait_ge(vc.sem, vc.at("dp", c))
                            if not first(c):
                                act.wait_ge(vc.sem, vc.at("rk1", c - 1))
                            S.activation(ep[:, :], dp[:, :], ACT.Exp).then_inc(ac.sem, 1)
                        relu_b(4)
                        relu_b(5)
                        if c is not None:
                            act.wait_ge(tc.sem, tc.at("gateT", c))
                            if not (isinstance(c, int) and c < 2):
                                act.wait_ge(gates_stored, c * 16 - 16)
                                act.wait_ge(td.sem, td.at("c5", c - 2))
                            S.activation(gateT[ps[2]][:, :], banks[6][0:8, :], ACT.Copy).then_inc(ac.sem, 1)
                        if d is not None:
                            act.wait_ge(td.sem, td.at("c5", d))
                            if not first(d):
                                act.wait_ge(td.sem, td.at("oT", d - 1))
                            S.activation(oT[:, :], banks[4][:, :], ACT.Copy).then_inc(ad.sem, 1)
                    sweep(act, body)

                @block.vector
                def _(dve):
                    dve.wait_ge(ld_w, 16 * NW)
                    for hi, lo, w in ((ew1_hi, ew1_lo, ew1), (rw1_hi, rw1_lo, rw1)):
                        V.tensor_copy(hi[:, :], w[:, :]).then_inc(dve_w, 1)
                    dve.wait_ge(dve_w, 2)
                    for hi, lo, w in ((ew1_hi, ew1_lo, ew1), (rw1_hi, rw1_lo, rw1)):
                        V.tensor_tensor(lo[:, :], w[:, :], hi[:, :].bitcast(f32), ALU.subtract).then_inc(dve_w, 1)

                    def held():
                        V.memset(spare2[:, :], 0.0)

                    def all8(ap):
                        return ap.unsqueeze(2).broadcast_to([P, TG, 8])

                    def moments(steps, g, st, mv, var, src):
                        for t in range(TG):
                            last = V.bn_stats(st[:, t, :], src(t))
                        last.then_inc(steps.sem, 1)
                        dve.wait_ge(steps.sem, steps.at("stats", g))
                        held()
                        for t in range(TG):
                            last = V.bn_aggr(mv[:, t, :], st[:, t, :])
                        last.then_inc(steps.sem, 1)
                        dve.wait_ge(steps.sem, steps.at("moments", g))
                        V.tensor_scalar(var[:, :], mv[:, :, 1], 1e-5, None, ALU.add).then_inc(steps.sem, 1)

                    def body(gs, ps):
                        a, b, c, d = gs

                        def gated(n):
                            if d is None:
                                return
                            dve.wait_ge(ad.sem, ad.at(f"b{n}", d))
                            if n == 0:
                                dve.wait_ge(gates_loaded[ps[3]], pair(d, ps[3]))
                            if n >= 2:
                                dve.wait_ge(td.sem, td.at(f"c{n - 2}", d))
                            elif not first(d):
                                dve.wait_ge(td.sem, td.at(f"c{n + 4}", d - 1))
                            V.tensor_tensor(h2g[n % 2][:, :], h2[n % 2][:, :], gate_bc[ps[3]][:, n, :], ALU.mult).then_inc(vd.sem, 1)

                        if a is not None:
                            if not (isinstance(a, int) and a < 2):
                                dve.wait_ge(gathered[ps[0]], pair(a, ps[0]) * (2 * TG) - 16 * 2 * TG)
                            V.tensor_copy(slot_now[ps[0]][:, :], slots_all[:, bass.ds(a, 1), :].rearrange("p o s -> p (o s)"))
                            V.tensor_copy(gate_now[ps[0]][:, :], gates_all[:, bass.ds(a, 1), :].rearrange("p o s -> p (o s)")).then_inc(vs.sem, 1)
                        if c is not None:
                            dve.wait_ge(ac.sem, ac.at("hi", c))
                            if not (isinstance(c, int) and c < 2):
                                dve.wait_ge(td.sem, td.at("a5", c - 2))
                            V.tensor_tensor(f3_lo[ps[2]][:, :], banks[6][:, :], f3_hi[ps[2]][:, :].bitcast(f32), ALU.subtract).then_inc(vc.sem, 1)
                        gated(0)
                        gated(1)
                        if b is not None:
                            dve.wait_ge(tb.sem, tb.at("gnn", b))
                            dve.wait_ge(pb.sem, pb.at("xb", b))
                            for t in range(TG):
                                last = V.scalar_tensor_tensor(base_all[:, bass.ds(b * TG + t, 1), :].rearrange("p o c -> p (o c)"),
                                                              banks[5][:, t * P:(t + 1) * P], deg[ps[1]][:, t:t + 1], xb[:, t, :], ALU.mult, ALU.add)
                            last.then_inc(vb.sem, 1)
                            dve.wait_ge(vb.sem, vb.at("x3", b))
                            held()
                            moments(vb, b, st_b, mv_b, var_b, lambda t: base_all[:, bass.ds(b * TG + t, 1), :].rearrange("p o c -> p (o c)"))
                        gated(2)
                        if c is not None:
                            dve.wait_ge(tc.sem, tc.at("logits", c))
                            V.tensor_tensor(lg[:, :, :], banks[6][:, 0:TG * 8].rearrange("p (t e) -> p t e", t=TG),
                                            rb2[:, :].unsqueeze(1).broadcast_to([P, TG, 8]), ALU.add).then_inc(vc.sem, 1)
                            dve.wait_ge(vc.sem, vc.at("lg", c))
                            held()
                            for t in range(TG):
                                last = V.max(top[:, t, :], lg[:, t, :])
                            last.then_inc(vc.sem, 1)
                            dve.wait_ge(vc.sem, vc.at("top", c))
                            held()
                            for t in range(TG):
                                last = V.max_index(topi[:, t, :], top[:, t, :], lg[:, t, :])
                            last.then_inc(vc.sem, 1)
                            dve.wait_ge(vc.sem, vc.at("topi", c))
                            V.tensor_copy(topf[:, :, :], topi[:, :, 0:2]).then_inc(vc.sem, 1)
                            dve.wait_ge(vc.sem, vc.at("topf", c))
                            V.tensor_tensor(oh[:, :, :, :], topf[:, :, :].unsqueeze(3).broadcast_to([P, TG, 2, 8]),
                                            iota8.unsqueeze(1).unsqueeze(1).broadcast_to([P, TG, 2, 8]), ALU.is_equal).then_inc(vc.sem, 1)
                            if not first(c):
                                dve.wait_ge(ac.sem, ac.at("etop", c - 1))
                            V.tensor_tensor(dtop[:, :, :], top[:, :, :], top[:, :, 0:1].broadcast_to([P, TG, 8]), ALU.subtract).then_inc(vc.sem, 1)
                        if b is not None:
                            dve.wait_ge(pb.sem, pb.at("rstd", b))
                            if not first(b):
                                dve.wait_ge(tc.sem, tc.at("f3T", b - 1))
                            for t in range(TG):
                                last = V.tensor_scalar(f3[:, t, :], base_all[:, bass.ds(b * TG + t, 1), :].rearrange("p o c -> p (o c)"),
                                                       mv_b[:, t, 0:1], rs_b[:, t:t + 1], ALU.subtract, ALU.mult)
                            last.then_inc(vb.sem, 1)
                        gated(3)
                        if a is not None:
                            dve.wait_ge(ta.sem, ta.at("deg", a))
                            V.tensor_scalar(degv[:, :], banks[7][:, 0:TG], 1e-5, None, ALU.add).then_inc(va.sem, 1)
                        if c is not None:
                            dve.wait_ge(ac.sem, ac.at("etop", c))
                            V.reduce_sum(z[:, :], etop[:, :, :], AX.X).then_inc(vc.sem, 1)
                            dve.wait_ge(vc.sem, vc.at("z", c))
                            V.reciprocal(zr[:, :], z[:, :]).then_inc(vc.sem, 1)
                            dve.wait_ge(vc.sem, vc.at("zr", c))
                            V.tensor_tensor(pk[:, :, :], etop[:, :, 0:2], zr[:, :].unsqueeze(2).broadcast_to([P, TG, 2]), ALU.mult).then_inc(vc.sem, 1)
                            dve.wait_ge(vc.sem, vc.at("pk", c))
                            V.tensor_tensor(dp[:, :], pk[:, :, 1], pk[:, :, 0], ALU.subtract).then_inc(vc.sem, 1)
                        gated(4)
                        if a is not None:
                            dve.wait_ge(gathered[ps[0]], pair(a, ps[0]) * (2 * TG))
                            for t in range(TG):
                                last = V.scalar_tensor_tensor(x2a[:, t, :], rows[ps[0]][:, 2 * t, :], gate_now[ps[0]][:, 2 * t:2 * t + 1],
                                                              base_all[:, bass.ds(a * TG + t, 1), :].rearrange("p o c -> p (o c)"), ALU.mult, ALU.add)
                            last.then_inc(va.sem, 1)
                            dve.wait_ge(va.sem, va.at("add0", a))
                            if not first(a):
                                dve.wait_ge(pb.sem, pb.at("xb", a - 1))
                            for t in range(TG):
                                last = V.scalar_tensor_tensor(x2[:, t, :], rows[ps[0]][:, 2 * t + 1, :], gate_now[ps[0]][:, 2 * t + 1:2 * t + 2],
                                                              x2a[:, t, :], ALU.mult, ALU.add)
                            last.then_inc(va.sem, 1)
                            dve.wait_ge(va.sem, va.at("add1", a))
                            held()
                            moments(va, a, st_a, mv_a, var_a, lambda t: x2[:, t, :])
                        if c is not None:
                            dve.wait_ge(ac.sem, ac.at("ep", c))
                            V.tensor_scalar(e1[:, :], ep[:, :], 1.0, None, ALU.add).then_inc(vc.sem, 1)
                            dve.wait_ge(vc.sem, vc.at("e1", c))
                            V.reciprocal(rk[:, :, 0], e1[:, :]).then_inc(vc.sem, 1)
                            dve.wait_ge(vc.sem, vc.at("rk0", c))
                            V.tensor_tensor(rk[:, :, 1], ep[:, :], rk[:, :, 0], ALU.mult).then_inc(vc.sem, 1)
                            dve.wait_ge(vc.sem, vc.at("rk1", c))
                            V.tensor_tensor(ohr[:, :, :, :], oh[:, :, :, :], rk[:, :, :].unsqueeze(3).broadcast_to([P, TG, 2, 8]), ALU.mult).then_inc(vc.sem, 1)
                            dve.wait_ge(vc.sem, vc.at("ohr", c))
                            if not first(c):
                                dve.wait_ge(tc.sem, tc.at("gateT", c - 1))
                            V.tensor_tensor(gate[:, :, :], ohr[:, :, 0, :], ohr[:, :, 1, :], ALU.add).then_inc(vc.sem, 1)
                        gated(5)
                        if a is not None:
                            dve.wait_ge(pa.sem, pa.at("rstd", a))
                            V.tensor_tensor(xscale[:, :], rs_a[:, :], deg[ps[0]][:, :], ALU.mult).then_inc(va.sem, 1)
                            dve.wait_ge(va.sem, va.at("scale", a))
                            if not first(a):
                                dve.wait_ge(tb.sem, tb.at("tT", a - 1))
                            for t in range(TG):
                                last = V.tensor_scalar(xn[:, t, :], x2[:, t, :], mv_a[:, t, 0:1], xscale[:, t:t + 1], ALU.subtract, ALU.mult)
                            last.then_inc(va.sem, 1)
                        if d is not None:
                            dve.wait_ge(td.sem, td.at("oT", d))
                            if not first(d):
                                dve.wait_ge(stored, d * 16)
                            V.tensor_tensor(ob[:, :, :], banks[7][:, :].rearrange("p (t c) -> p t c", t=TG),
                                            base_all[:, bass.ds(d * TG, TG), :], ALU.add).then_inc(vd.sem, 1)
                    sweep(dve, body)

                @block.tensor
                def _(pe):
                    pe.wait_ge(ld_w, 16 * NW)
                    pe.wait_ge(dve_w, 4)

                    def body(gs, ps):
                        a, b, c, d = gs
                        par = ps[3]

                        def layer_a(n):
                            if d is None:
                                return
                            if n >= 2:
                                pe.wait_ge(ad.sem, ad.at(f"a{n - 2}", d))
                            elif not first(d):
                                pe.wait_ge(ad.sem, ad.at(f"a{n + 4}", d - 1))
                            w = slice(n * C, (n + 1) * C)
                            for q, (ww, ff) in enumerate(((ew1_hi, f3_hi), (ew1_hi, f3_lo), (ew1_lo, f3_hi))):
                                last = T.matmul(banks[n % 2][:, :], ww[:, w], ff[par][:, :], start=q == 0, stop=q == 2)
                            last.then_inc(td.sem, 1)

                        def layer_b(n):
                            if d is None:
                                return
                            pe.wait_ge(ad.sem, ad.at(f"a{n}", d))
                            if n >= 2:
                                pe.wait_ge(ad.sem, ad.at(f"b{n - 2}", d))
                            elif not first(d):
                                pe.wait_ge(ad.sem, ad.at(f"b{n + 4}", d - 1))
                            T.matmul(banks[2 + n % 2][:, :], ew2[:, n * C:(n + 1) * C], h1[n % 2][:, :], start=True, stop=True).then_inc(td.sem, 1)

                        def layer_c(n):
                            if d is None:
                                return
                            pe.wait_ge(vd.sem, vd.at(f"g{n}", d))
                            if n == 0 and not first(d):
                                pe.wait_ge(ad.sem, ad.at("oT", d - 1))
                            last = T.matmul(banks[4][:, :], ew3[:, n * C:(n + 1) * C], h2g[n % 2][:, :], start=n == 0, stop=False)
                            if n == NE1 - 1:
                                last = T.matmul(banks[4][:, :], eb3[:, :], gateT[par][0:NE1, :], start=False, stop=True)
                            last.then_inc(td.sem, 1)

                        if c is not None:
                            pe.wait_ge(vb.sem, vb.at("f3", c))
                            if not first(c):
                                pe.wait_ge(ac.sem, ac.at("gateT", c - 1))
                            for t in range(TG):
                                last = T.transpose(banks[6][:, t * P:(t + 1) * P], f3[:, t, :], ident)
                            last.then_inc(tc.sem, 1)
                        layer_a(0)
                        layer_a(1)
                        if b is not None:
                            pe.wait_ge(va.sem, va.at("xn", b))
                            if not first(b):
                                pe.wait_ge(vb.sem, vb.at("x3", b - 1))
                            for t in range(TG):
                                last = T.matmul(banks[5][:, t * P:(t + 1) * P], xn[:, t, :], adjt[ps[1]][:, t, :], start=True, stop=True)
                            last.then_inc(tb.sem, 1)
                        layer_b(0)
                        if c is not None:
                            pe.wait_ge(vc.sem, vc.at("lo", c))
                            for q, (ww, ff) in enumerate(((rw1_hi, f3_hi), (rw1_hi, f3_lo), (rw1_lo, f3_hi))):
                                last = T.matmul(banks[6][0:RH, :], ww[:, :], ff[ps[2]][:, :], start=q == 0, stop=q == 2)
                            last.then_inc(tc.sem, 1)
                        layer_a(2)
                        layer_b(1)
                        if b is not None:
                            pe.wait_ge(ab.sem, ab.at("tT", b))
                            for t in range(TG):
                                last = T.matmul(banks[5][:, t * P:(t + 1) * P], tT[:, t, :], gw[:, :], start=True, stop=True)
                            last.then_inc(tb.sem, 1)
                        layer_c(0)
                        layer_a(3)
                        layer_b(2)
                        if c is not None:
                            pe.wait_ge(ac.sem, ac.at("rh", c))
                            for t in range(TG):
                                last = T.matmul(banks[6][:, t * 8:t * 8 + 8], rhT[:, t * P:(t + 1) * P], rw2[:, :], start=True, stop=True)
                            last.then_inc(tc.sem, 1)
                        layer_c(1)
                        layer_a(4)
                        if a is not None:
                            pe.wait_ge(ld_adj[ps[0]], pair(a, ps[0]) * 2)
                            if d is not None and not first(d):
                                pe.wait_ge(vd.sem, vd.at("out", d - 1))
                            for t in range(TG):
                                last = T.matmul(banks[7][:, t:t + 1], adjt[ps[0]][:, t, :], cst[:, C_ONE:C_ONE + 1], start=True, stop=True)
                            last.then_inc(ta.sem, 1)
                        layer_b(3)
                        layer_c(2)
                        layer_a(5)
                        layer_b(4)
                        layer_c(3)
                        layer_b(5)
                        layer_c(4)
                        if c is not None:
                            pe.wait_ge(vc.sem, vc.at("gate", c))
                            for t in range(TG):
                                last = T.transpose(banks[6][0:8, t * P:(t + 1) * P], gate[:, t, :], ident)
                            last.then_inc(tc.sem, 1)
                        layer_c(5)
                        if d is not None:
                            pe.wait_ge(ad.sem, ad.at("oT", d))
                            if a is not None:
                                pe.wait_ge(va.sem, va.at("degv", a))
                            elif not first(d):
                                pe.wait_ge(vd.sem, vd.at("out", d - 1))
                            for t in range(TG):
                                last = T.transpose(banks[7][:, t * P:(t + 1) * P], oT[:, t * P:(t + 1) * P], ident)
                            last.then_inc(td.sem, 1)
                    sweep(pe, body)


def laid_out(inp):
    a = {k: np.ascontiguousarray(v) for k, v in inp.items()}
    half = HD // 2

    def swapped(w):
        return w.reshape(-1, 2, half, C)[:, ::-1].reshape(-1, C)

    def repeated(w):
        return np.repeat(w.reshape(NH // 2, 1, HD, C), 2, 1).reshape(-1, C)

    wq, wk, wv = a["L0_ffn_wq"], repeated(a["L0_ffn_wk"]), a["L0_ffn_wv"]
    w13 = np.zeros((C, NE0, 2, HIDP), np.float32)
    w13[:, :, 0, :HID] = a["L0_ffn_w1"].transpose(2, 0, 1)
    w13[:, :, 1, :HID] = a["L0_ffn_w3"].transpose(2, 0, 1)
    w2 = np.zeros((NE0, KC * P, C), np.float32)
    w2[:, :HID] = a["L0_ffn_w2"].transpose(0, 2, 1)
    r2 = np.zeros((RH, 8), np.float32)
    r2[:, :NE1] = a["L1_ffn_router_w2"]
    return dict(
        x=a["x"].reshape(TOK, C),
        adj_t=a["adj"].transpose(0, 2, 1).reshape(TOK, NN),
        gnn0_w=a["L0_gnn_weight"], gnn0_b=a["L0_gnn_bias"],
        ln1=a["L0_ffn_ln1_w"].reshape(C, 1), ln2=a["L0_ffn_ln2_w"].reshape(C, 1),
        wqkv=np.concatenate([wq, swapped(wq), wk, swapped(wk), wv], 0).T,
        wo=a["L0_ffn_wo"].T, router0=a["L0_ffn_router_w"].T,
        w13=w13.reshape(C, -1), w2=w2.reshape(NE0, KC, P, C).transpose(2, 0, 1, 3).reshape(P, -1),
        gnn1_w=a["L1_gnn_weight"], gnn1_b=a["L1_gnn_bias"],
        r1_w1=a["L1_ffn_router_w1"], r1_b1=a["L1_ffn_router_b1"].reshape(RH, 1),
        r1_w2=r2, r1_b2=a["L1_ffn_router_b2"],
        e_w1=a["L1_ffn_expert_w1"].transpose(1, 0, 2).reshape(C, -1), e_b1=a["L1_ffn_expert_b1"].T,
        e_w2=a["L1_ffn_expert_w2"].transpose(1, 0, 2).reshape(C, -1), e_b2=a["L1_ffn_expert_b2"].T,
        e_w3=a["L1_ffn_expert_w3"].transpose(1, 0, 2).reshape(C, -1), e_b3=a["L1_ffn_expert_b3"],
        consts=constants(),
    )


def kernel(**inputs):
    import concourse.bacc as _bacc
    from concourse.bass_utils import run_bass_kernel_spmd as _run

    nc = _bacc.Bacc("TRN2", target_bir_lowering=False, num_devices=1)
    arrays = {f"in_{k}": np.ascontiguousarray(v) for k, v in laid_out(inputs).items()}
    args = {k[3:]: nc.dram_tensor(k, v.shape, mybir.dt.float32, kind="ExternalInput").ap() for k, v in arrays.items()}
    out = nc.dram_tensor("out_0", (TOK, C), mybir.dt.float32, kind="ExternalOutput").ap()
    build(nc, out=out, **args)
    r = _run(nc, [arrays], core_ids=[0])
    return r.results[0]["out_0"].reshape(NB, NN, C)
```

```python
from contextlib import ExitStack

import numpy as np
import concourse.bass as bass
from concourse import mybir

P = 128
NB, NN, C = 128, 64, 128
TOK = NB * NN
TG = 4
GT = TG * P
NG = TOK // GT
GR = GT // NN
NH, HD = 4, 32
NE0, HID = 8, 341
HIDP = HID + 1
KC = 3
NE1, RH = 6, 64
MB = TOK // P
REG = MB + 1
DUM = NE0 * REG
NBLK = 2 * TOK // P + NE0
NDUM = NE0
ROWS = (DUM + NDUM) * P

C_ID, C_COS, C_SIN, C_MASK = 0, 128, 192, 256
C_TRI, C_ONE, C_IOTA, C_BASE = 320, 448, 576, 584
C_BLK, C_TRI8 = 592, 592 + NBLK
C_N = C_TRI8 + 64


def constants():
    c = np.zeros((P, C_N), np.float32)
    c[:, C_ID:C_ID + P] = np.eye(P)
    inv = 1.0 / 10000.0 ** (np.arange(0, HD, 2, dtype=np.float32) / HD)
    fr = np.outer(np.arange(NN, dtype=np.float32), inv)
    emb = np.concatenate([fr, fr], -1)
    sign = np.where(np.arange(HD) < HD // 2, -1.0, 1.0)
    c[:, C_COS:C_COS + NN] = np.tile(np.cos(emb).T, (NH, 1))
    c[:, C_SIN:C_SIN + NN] = np.tile((np.sin(emb) * sign).T, (NH, 1))
    t = np.arange(P) % NN
    c[:, C_MASK:C_MASK + NN] = np.where(np.arange(NN)[None] <= t[:, None], 0.0, -1e30)
    c[:, C_TRI:C_TRI + P] = np.arange(P)[:, None] < np.arange(P)[None]
    c[:, C_ONE:C_ONE + P] = 1.0
    c[:, C_IOTA:C_IOTA + 8] = np.arange(8)
    c[:, C_BASE:C_BASE + 8] = np.arange(8) * REG * P
    c[:, C_BLK:C_BLK + NBLK] = np.arange(NBLK)
    c[:, C_TRI8:C_TRI8 + 64] = (np.arange(8)[None] <= np.arange(8)[:, None]).reshape(-1)
    return c


class Steps:

    def __init__(self, sem, names):
        self.sem, self.names = sem, names.split()

    def at(self, name, g):
        return g * len(self.names) + (self.names.index(name) + 1)


def signals(sem, names):
    return {n: sem(n) for n in names.split()}


def has(g):
    return not isinstance(g, int) or g >= 0


def upto(g):
    return min(g, NG - 1) + 1 if isinstance(g, int) else g + 1


def build(nc, x, adj_t, gnn0_w, gnn0_b, ln1, ln2, wqkv, wo, router0, w13, w2, gnn1_w, gnn1_b,
          r1_w1, r1_b1, r1_w2, r1_b2, e_w1, e_b1, e_w2, e_b2, e_w3, e_b3, consts, out):
    f32, f32r, bf16 = mybir.dt.float32, mybir.dt.float32r, mybir.dt.bfloat16
    u32, i32 = mybir.dt.uint32, mybir.dt.int32
    ALU, ACT, AX = mybir.AluOpType, mybir.ActivationFunctionType, mybir.AxisListType
    V, S, T, G = nc.vector, nc.scalar, nc.tensor, nc.gpsimd
    SCALE = float(HD) ** -0.5

    slots_in = nc.dram_tensor("slots_in", (ROWS, C), f32, kind="Internal").ap()
    slots_out = nc.dram_tensor("slots_out", (NBLK * P, C), f32, kind="Internal").ap()
    gates_dram = [nc.dram_tensor(f"gates_dram{i}", (NE1, GT), f32, kind="Internal").ap() for i in range(2)]

    def first(g):
        return isinstance(g, int) and g == 0

    with ExitStack() as whole:
        def sb_in(ctx):
            return lambda name, shape, dt=f32: ctx.enter_context(nc.sbuf_tensor(name, shape, dt))

        def sem_in(ctx):
            return lambda name: ctx.enter_context(nc.semaphore(name))

        sb, sem = sb_in(whole), sem_in(whole)
        banks = [whole.enter_context(nc.psum_tensor(f"bank{i}", [P, 512], f32)) for i in range(8)]

        cst = sb("cst", [P, C_N])
        ident = cst[:, C_ID:C_ID + P]
        iota8 = cst[:, C_IOTA:C_IOTA + 8]
        base_all = sb("base_all", [P, NG * TG, C])
        slots_all = sb("slots_all", [P, NG, 2 * TG], u32)
        gates_all = sb("gates_all", [P, NG, 2 * TG])
        w13_hi = sb("w13_hi", [P, NE0 * 2 * HIDP], f32r)
        w13_lo = sb("w13_lo", [P, NE0 * 2 * HIDP], f32r)
        w2_sb = sb("w2_sb", [P, NE0 * KC * C])
        table = sb("table", [1, 2, NBLK], i32)

        with ExitStack() as ctx:
            sb, sem = sb_in(ctx), sem_in(ctx)
            f_all = sb("f_all", [P, NG * TG, C])
            stage = f_all[:, NG * TG - 43:, :].rearrange("p t c -> p (t c)")[:, 0:NE0 * 2 * HIDP]
            gw, gb, wo_sb = sb("gw", [P, C]), sb("gb", [P, C]), sb("wo_sb", [P, C])
            rw, ln = sb("rw", [P, NE0]), sb("ln", [P, 2])
            rws = sb("rws", [P, NE0])
            wq_raw = sb("wq_raw", [P, 576])
            wq_hi, wq_lo = sb("wq_hi", [P, 576], f32r), sb("wq_lo", [P, 576], f32r)
            trib, oneb = sb("trib", [P, P], bf16), sb("oneb", [P, P], bf16)
            xt, xb, xn, adjt = (sb(n, [P, TG, C]) for n in ("xt", "xb", "xn", "adjt"))
            tT, x1, hp = (sb(n, [P, TG, C]) for n in ("tT", "x1", "hp"))
            hT_hi, hT_lo = sb("hT_hi", [P, GT + NN], f32r), sb("hT_lo", [P, GT + NN], f32r)
            q_cos, q_sin, k_cos, k_sin = (sb(n, [P, GT]) for n in ("q_cos", "q_sin", "k_cos", "k_sin"))
            q_rot, k_rot = sb("q_rot", [P, GT]), sb("k_rot", [P, GT])
            v_diag = sb("v_diag", [P, GR, 2, 66])
            sc, pr = sb("sc", [P, TG, NH, NN]), sb("pr", [P, TG, NH, NN])
            prT = sb("prT", [P, 2, TG, P])
            yn, yT, f2, flat, flatT = (sb(n, [P, TG, C]) for n in ("yn", "yT", "f2", "flat", "flatT"))
            junk = sb("junk", [P, TG, C])
            zrow = sb("zrow", [P, C])
            st_a, mv_a, rs_a = sb("st_a", [P, TG, 6]), sb("mv_a", [P, TG, 2]), sb("rs_a", [P, TG])
            var_a, var_b, mhalf = sb("var_a", [P, TG]), sb("var_b", [P, 2, TG]), sb("mhalf", [P, 2, TG])
            st_b, mv_b = sb("st_b", [P, TG, 6]), sb("mv_b", [P, TG, 2])
            rs_b = sb("rs_b", [P, 2, TG])
            mx, nmx = sb("mx", [P, TG * NH]), sb("nmx", [P, TG * NH])
            rden = sb("rden", [P, TG, NH])
            ss, ssv, rr2 = sb("ss", [P, TG]), sb("ssv", [P, TG]), sb("rr2", [P, TG])
            lg, top, topi = sb("lg", [P, TG, 8]), sb("top", [P, TG, 8]), sb("topi", [P, TG, 8], u32)
            topf, oh = sb("topf", [P, TG, 2]), sb("oh", [P, TG, 2, 8])
            sel, carry, carry_b = sb("sel", [P, TG, 8], bf16), sb("carry", [P, 8]), sb("carry_b", [P, 8], bf16)
            selsum = sb("selsum", [P, 8])
            dtop, etop = sb("dtop", [P, TG, 8]), sb("etop", [P, TG, 8])
            z, s2, den, rec = (sb(n, [P, TG]) for n in ("z", "s2", "den", "rec"))
            rank, ohr, slotf = sb("rank", [P, TG, 8]), sb("ohr", [P, TG, 2, 8]), sb("slotf", [P, TG * 2])
            slot_now = sb("slot_now", [P, 2 * TG], u32)
            cnti, nblk = sb("cnti", [P, 8], i32), sb("nblk", [P, 8])
            slots_f, gaps = sb("slots_f", [P, NG, 2 * TG]), sb("gaps", [P, 8])
            tri_nb, cum = sb("tri_nb", [1, 8, 8]), sb("cum", [1, 8])
            left = f_all[:, :, :].rearrange("p t c -> p (t c)")
            past, pastn = (left[0:1, i * NBLK * 8:(i + 1) * NBLK * 8].rearrange("p (k e) -> p k e", e=8) for i in range(2))
            gap = left[:, 2 * NBLK * 8:2 * NBLK * 8 + NG * 2 * TG * 7].rearrange("p (s e) -> p s e", e=7)
            back = left[:, 3 * NBLK * 8:3 * NBLK * 8 + NG * 2 * TG]
            bexp, bprev, brow = sb("bexp", [1, NBLK]), sb("bprev", [1, NBLK]), sb("brow", [1, NBLK])
            fill = sb("fill", [1, 8], i32)
            spare, spare2, nmr = sb("spare", [P, 1]), sb("spare2", [P, 1]), sb("nmr", [P, TG])

            ld_x, ld_adj, ld_w, ld_big, ld_w2 = (sem(n) for n in ("ld_x", "ld_adj", "ld_w", "ld_big", "ld_w2"))
            zeroed, zero_fill, scattered = sem("zeroed"), sem("zero_fill"), sem("scattered")
            act_w, dve_w, pool_w = sem("act_w"), sem("dve_w"), sem("pool_w")
            dve_t, pe_t = sem("dve_t"), sem("pe_t")
            B_GNNT, B_GNN, B_HT, B_V = 2, 2, 3, 1
            B_PQ, B_PQS, B_PK, B_PKS = 3, 7, 7, 6
            B_PRT, B_Y = (4, 5), (4, 5)
            B_YT, B_WO, B_FLATT, B_LOGITS, B_RANK = 6, 2, 5, 5, 0
            DEEP = 5
            at = signals(sem, "st0 mv0 var0 rstd0 xb xn gnnT tT gnn x1 st1 mv1 var1 rstd1 nmr hp f base0 "
                             "hT hi lo pq pqs pk pks qc qs kc ks qr kr v vd "
                             "scores mask max nmax exp prT prTc y rden yn yT yTc wo f2 base1 ssq ssv rms flat flatT flatTc logits "
                             "lg top topi topf oh sel carb ssum car dtop etop z den rec gate rank rk ohr slotf slot keep")

            def sweep(engine, body):
                for i in range(DEEP):
                    body([i - k if i >= k else None for k in range(DEEP + 1)])
                with engine.Fori(DEEP, NG) as i:
                    body([i - k for k in range(DEEP + 1)])
                for i in range(NG, NG + DEEP):
                    body([i - k if i - k < NG else None for k in range(DEEP + 1)])

            with nc.Block() as block:
                @block.sync
                def _(sp):
                    def load_x(g):
                        if g is None:
                            return
                        if has(g - 1):
                            sp.wait_ge(at["xn"], g)
                            sp.wait_ge(at["xb"], g)
                        sp.dma_start(xt[:, :, :], x[bass.ds(g * GT, GT), :].rearrange("(t p) c -> p t c", p=P)).then_inc(ld_x, 16)

                    def load_adj(g):
                        if g is None:
                            return
                        if has(g - 1):
                            sp.wait_ge(at["gnnT"], g)
                        rows = adj_t[bass.ds(g * GT, GT), :].rearrange("(t b m) n -> b m t n", b=2, m=NN)
                        if first(g):
                            sp.wait_ge(zeroed, 1)
                        for b in range(2):
                            sp.dma_start(adjt[b * NN:(b + 1) * NN, :, b * NN:(b + 1) * NN], rows[b]).then_inc(ld_adj, 16)

                    load_x(0)
                    sp.dma_start(cst[:, :], consts).then_inc(ld_w, 16)
                    load_adj(0)
                    for dst, src in ((gw[:, :], gnn0_w), (gb[:, :], gnn0_b.partition_broadcast(P)),
                                     (ln[:, 0:1], ln1), (ln[:, 1:2], ln2), (wo_sb[:, :], wo), (rw[:, :], router0),
                                     (wq_raw[:, :], wqkv)):
                        sp.dma_start(dst, src).then_inc(ld_w, 16)
                    sp.dma_start(stage, w13).then_inc(ld_big, 16)
                    load_x(1)
                    load_adj(1)
                    sp.dma_start(w2_sb[:, :], w2).then_inc(ld_w2, 16)
                    sp.wait_ge(zeroed, 2)
                    for k in range(NDUM):
                        sp.dma_start(slots_in[(DUM + k) * P:(DUM + k + 1) * P, :], zrow[:, :]).then_inc(zero_fill, 16)
                    with sp.Fori(2, NG) as g:
                        load_x(g)
                        load_adj(g)
                    sp.wait_ge(dve_t, 3)
                    for e in range(NE0):
                        row = sp.value_load(fill[0:1, e:e + 1], min_val=0, max_val=ROWS - P)
                        sp.dma_start(slots_in[bass.ds(row, P), :], zrow[:, :]).then_inc(zero_fill, 16)
                    sp.wait_ge(zero_fill, 16 * (NDUM + NE0))
                    sp.wait_ge(ld_w2, 16)

                @block.gpsimd
                def _(pool):
                    G.memset(adjt[:, :, :], 0.0).then_inc(zeroed, 1)
                    G.memset(mhalf[:, :, :], -0.5).then_inc(pool_w, 1)
                    G.memset(zrow[:, :], 0.0).then_inc(zeroed, 1)
                    G.memset(v_diag[:, :, :, :], 0.0).then_inc(pool_w, 1)
                    G.memset(carry[:, :], 0.0).then_inc(pool_w, 1)
                    pool.wait_ge(pool_w, 3)
                    G.memset(v_diag[0:NN, :, :, 32:33], 1.0).then_inc(pool_w, 1)
                    pool.wait_ge(pool_w, 4)
                    G.memset(v_diag[NN:P, :, :, 65:66], 1.0).then_inc(pool_w, 1)
                    pool.wait_ge(pool_w, 5)

                    def rstd0(g):
                        if g is not None:
                            pool.wait_ge(at["var0"], g + 1)
                            if has(g - 1):
                                pool.wait_ge(at["xn"], g)
                            G.tensor_tensor(rs_a[:, :], var_a[:, :], mhalf[:, 0, :], ALU.pow).then_inc(at["rstd0"], 1)

                    def xb_(g):
                        if g is not None:
                            pool.wait_ge(ld_x, g * 16 + 16)
                            if first(g):
                                pool.wait_ge(ld_w, 16 * 8)
                            if has(g - 1):
                                pool.wait_ge(at["x1"], g)
                            G.tensor_tensor(xb[:, :, :], xt[:, :, :], gb[:, :].unsqueeze(1).broadcast_to([P, TG, C]), ALU.add).then_inc(at["xb"], 1)

                    def rstd1(g):
                        if g is not None:
                            pool.wait_ge(at["var1"], g + 1)
                            if has(g - 1):
                                pool.wait_ge(at["f"], g)
                                pool.wait_ge(at["hp"], g)
                            G.tensor_tensor(rs_b[:, :, :], var_b[:, :, :], mhalf[:, :, :], ALU.pow).then_inc(at["rstd1"], 1)

                    def base0(g):
                        if g is not None:
                            pool.wait_ge(at["f"], g + 1)
                            G.tensor_tensor(base_all[:, bass.ds(g * TG, TG), :], x1[:, :, :], f_all[:, bass.ds(g * TG, TG), :], ALU.add).then_inc(at["base0"], 1)

                    def qr(g):
                        if g is not None:
                            pool.wait_ge(at["qc"], g + 1)
                            pool.wait_ge(at["qs"], g + 1)
                            if has(g - 1):
                                pool.wait_ge(at["scores"], g)
                            G.tensor_tensor(q_rot[:, :], q_cos[:, :], q_sin[:, :], ALU.add).then_inc(at["qr"], 1)

                    def kr(g):
                        if g is not None:
                            pool.wait_ge(at["kc"], g + 1)
                            pool.wait_ge(at["ks"], g + 1)
                            if has(g - 1):
                                pool.wait_ge(at["scores"], g)
                            G.tensor_tensor(k_rot[:, :], k_cos[:, :], k_sin[:, :], ALU.add).then_inc(at["kr"], 1)

                    def rms(g):
                        if g is not None:
                            pool.wait_ge(at["ssv"], g + 1)
                            if has(g - 1):
                                pool.wait_ge(at["flat"], g)
                            G.tensor_tensor(rr2[:, :], ssv[:, :], mhalf[:, 0, :], ALU.pow).then_inc(at["rms"], 1)

                    def sc(n, g):
                        if g is not None:
                            if n == 0:
                                pool.wait_ge(at["slot"], g + 1)
                                G.tensor_tensor(spare2[:, :], mhalf[:, 0, 0:1], mhalf[:, 0, 0:1], ALU.add)
                            G.indirect_dma_start(
                                out=slots_in, out_offset=bass.IndirectOffsetOnAxis(ap=slot_now[:, n:n + 1], axis=0),
                                in_=flat[:, n // 2, :], in_offset=None, bounds_check=ROWS - 1).then_inc(scattered, 16)

                    def weights_lo():
                        pool.wait_ge(act_w, 2)
                        G.tensor_tensor(w13_lo[:, :], stage, w13_hi[:, :].bitcast(f32), ALU.subtract).then_inc(pool_w, 1)

                    def body(g):
                        sc(7, g[5])
                        rms(g[4])
                        base0(g[2])
                        rstd0(g[0])
                        xb_(g[0])
                        kr(g[2])
                        rstd1(g[1])
                        sc(0, g[4])
                        sc(1, g[4])
                        sc(2, g[4])
                        sc(3, g[4])
                        qr(g[2])
                        sc(4, g[4])
                        sc(5, g[4])
                        sc(6, g[4])
                        if first(g[4]):
                            weights_lo()
                    sweep(pool, body)
                    pool.wait_ge(scattered, 16 * 2 * TG * NG)

                @block.scalar
                def _(act):
                    S.preload_act_table(ACT.Exp)

                    def weights_hi():
                        act.wait_ge(ld_w, 16 * 8)
                        act.wait_ge(ld_big, 16)
                        S.activation(stage, stage, ACT.Copy, scale=ln[:, 1:2]).then_inc(act_w, 1)
                        act.wait_ge(act_w, 1)
                        S.activation(w13_hi[:, :], stage, ACT.Copy).then_inc(act_w, 1)

                    def tT_(g):
                        if g is not None:
                            act.wait_ge(at["gnnT"], g + 1)
                            if has(g - 1):
                                act.wait_ge(at["gnn"], g)
                            S.activation(tT[:, :, :], banks[B_GNNT][:, :], ACT.Copy).then_inc(at["tT"], 1)

                    def hp_(g):
                        if g is not None:
                            act.wait_ge(at["nmr"], g + 1)
                            if has(g - 1):
                                act.wait_ge(at["hT"], g)
                            for t in range(TG):
                                last = S.activation(hp[:, t, :], x1[:, t, :], ACT.Identity, scale=rs_b[:, 1, t:t + 1], bias=nmr[:, t:t + 1])
                            last.then_inc(at["hp"], 1)

                    def hi(g):
                        if g is not None:
                            act.wait_ge(at["hT"], g + 1)
                            if has(g - 1):
                                act.wait_ge(at["pks"], g)
                                act.wait_ge(at["v"], g)
                            S.activation(hT_hi[:, 0:GT], banks[B_HT][:, :], ACT.Copy)
                            S.activation(hT_hi[:, GT:], banks[B_HT][:, 0:NN], ACT.Copy).then_inc(at["hi"], 1)

                    def vd(g):
                        if g is not None:
                            act.wait_ge(at["v"], g + 1)
                            if first(g):
                                act.wait_ge(pool_w, 5)
                            if has(g - 1):
                                act.wait_ge(at["y"], g)
                            vp = banks[B_V][:, :].rearrange("p (g k d) -> p g k d", g=GR, k=2)
                            S.activation(v_diag[0:NN, :, :, 0:32], vp[0:NN], ACT.Copy)
                            S.activation(v_diag[NN:P, 1:GR, :, 33:65], vp[NN:P, 0:GR - 1], ACT.Copy)
                            S.activation(v_diag[NN:P, 0:1, :, 33:65], vp[NN:P, GR - 1:GR], ACT.Copy).then_inc(at["vd"], 1)

                    def exp(g):
                        if g is not None:
                            act.wait_ge(at["nmax"], g + 1)
                            if has(g - 1):
                                act.wait_ge(at["prT"], g)
                            for t in range(TG):
                                for h in range(NH):
                                    last = S.activation(pr[:, t, h, :], sc[:, t, h, :], ACT.Exp, scale=SCALE,
                                                        bias=nmx[:, t * NH + h:t * NH + h + 1])
                            last.then_inc(at["exp"], 1)

                    def prTc(g):
                        if g is not None:
                            act.wait_ge(at["prT"], g + 1)
                            if has(g - 1):
                                act.wait_ge(at["y"], g)
                            for p in range(2):
                                last = S.activation(prT[:, p, :, :], banks[B_PRT[p]][:, :], ACT.Copy)
                            last.then_inc(at["prTc"], 1)

                    def yTc(g):
                        if g is not None:
                            act.wait_ge(at["yT"], g + 1)
                            if has(g - 1):
                                act.wait_ge(at["wo"], g)
                            S.activation(yT[:, :, :], banks[B_YT][:, :], ACT.Copy).then_inc(at["yTc"], 1)

                    def ssq(g):
                        if g is not None:
                            act.wait_ge(at["f2"], g + 1)
                            if has(g - 1):
                                act.wait_ge(at["ssv"], g)
                            for t in range(TG):
                                last = S.activation(junk[:, t, :], f2[:, t, :], ACT.Square, accum_out=ss[:, t:t + 1])
                            last.then_inc(at["ssq"], 1)

                    def flat_(g):
                        if g is not None:
                            act.wait_ge(at["rms"], g + 1)
                            if has(g - 1):
                                act.wait_ge(scattered, g * 16 * 2 * TG)
                                act.wait_ge(at["flatT"], g)
                            for t in range(TG):
                                last = S.activation(flat[:, t, :], f2[:, t, :], ACT.Copy, scale=rr2[:, t:t + 1])
                            last.then_inc(at["flat"], 1)

                    def flatTc(g):
                        if g is not None:
                            act.wait_ge(at["flatT"], g + 1)
                            if has(g - 1):
                                act.wait_ge(at["logits"], g)
                            S.activation(flatT[:, :, :], banks[B_FLATT][:, :], ACT.Copy).then_inc(at["flatTc"], 1)

                    def etop_(g):
                        if g is not None:
                            act.wait_ge(at["dtop"], g + 1)
                            if has(g - 1):
                                act.wait_ge(at["gate"], g)
                            S.activation(etop[:, :, :], dtop[:, :, :], ACT.Exp).then_inc(at["etop"], 1)

                    def body(g):
                        prTc(g[4])
                        hp_(g[2])
                        hi(g[2])
                        tT_(g[1])
                        yTc(g[4])
                        vd(g[3])
                        etop_(g[5])
                        ssq(g[4])
                        flat_(g[4])
                        flatTc(g[4])
                        exp(g[3])
                        if first(g[4]):
                            weights_hi()
                    sweep(act, body)

                @block.vector
                def _(dve):
                    def weights():
                        dve.wait_ge(ld_w, 16 * 8)
                        V.tensor_copy(trib[:, :], cst[:, C_TRI:C_TRI + P]).then_inc(dve_w, 1)
                        V.tensor_copy(oneb[:, :], cst[:, C_ONE:C_ONE + P]).then_inc(dve_w, 1)
                        V.tensor_scalar(rws[:, :], rw[:, :], ln[:, 1:2], None, ALU.mult).then_inc(dve_w, 1)
                        V.tensor_scalar(wq_raw[:, :], wq_raw[:, :], ln[:, 0:1], None, ALU.mult).then_inc(dve_w, 1)
                        dve.wait_ge(dve_w, 4)
                        V.tensor_copy(wq_hi[:, :], wq_raw[:, :]).then_inc(dve_w, 1)
                        dve.wait_ge(dve_w, 5)
                        V.tensor_tensor(wq_lo[:, :], wq_raw[:, :], wq_hi[:, :].bitcast(f32), ALU.subtract).then_inc(dve_w, 1)

                    def held():
                        V.memset(spare[:, :], 0.0)

                    def st0(g):
                        if g is not None:
                            dve.wait_ge(ld_x, g * 16 + 16)
                            for t in range(TG):
                                last = V.bn_stats(st_a[:, t, :], xt[:, t, :])
                            last.then_inc(at["st0"], 1)

                    def mv0(g):
                        if g is not None:
                            dve.wait_ge(at["st0"], g + 1)
                            held()
                            for t in range(TG):
                                last = V.bn_aggr(mv_a[:, t, :], st_a[:, t, :])
                            last.then_inc(at["mv0"], 1)

                    def var0(g):
                        if g is not None:
                            dve.wait_ge(at["mv0"], g + 1)
                            if has(g - 1):
                                dve.wait_ge(at["rstd0"], g)
                            V.tensor_scalar(var_a[:, :], mv_a[:, :, 1], 1e-5, None, ALU.add).then_inc(at["var0"], 1)

                    def xn_(g):
                        if g is not None:
                            dve.wait_ge(at["rstd0"], g + 1)
                            if has(g - 1):
                                dve.wait_ge(at["gnnT"], g)
                            for t in range(TG):
                                last = V.tensor_scalar(xn[:, t, :], xt[:, t, :], mv_a[:, t, 0:1], rs_a[:, t:t + 1], ALU.subtract, ALU.mult)
                            last.then_inc(at["xn"], 1)

                    def x1_(g):
                        if g is not None:
                            dve.wait_ge(at["gnn"], g + 1)
                            dve.wait_ge(at["xb"], g + 1)
                            if has(g - 1):
                                dve.wait_ge(at["base0"], g)
                                dve.wait_ge(at["hp"], g)
                            V.tensor_tensor(x1[:, :, :], banks[B_GNN][:, :].rearrange("p (t c) -> p t c", t=TG), xb[:, :, :], ALU.add).then_inc(at["x1"], 1)

                    def st1(g):
                        if g is not None:
                            dve.wait_ge(at["x1"], g + 1)
                            for t in range(TG):
                                last = V.bn_stats(st_b[:, t, :], x1[:, t, :])
                            last.then_inc(at["st1"], 1)

                    def mv1(g):
                        if g is not None:
                            dve.wait_ge(at["st1"], g + 1)
                            held()
                            for t in range(TG):
                                last = V.bn_aggr(mv_b[:, t, :], st_b[:, t, :])
                            last.then_inc(at["mv1"], 1)

                    def var1(g):
                        if g is not None:
                            dve.wait_ge(at["mv1"], g + 1)
                            if has(g - 1):
                                dve.wait_ge(at["rstd1"], g)
                            V.tensor_scalar(var_b[:, 0, :], mv_b[:, :, 1], 1e-5, None, ALU.add)
                            V.tensor_scalar(var_b[:, 1, :], mv_b[:, :, 1], 1.0 + 1e-6, 1e-11, ALU.mult, ALU.add).then_inc(at["var1"], 1)

                    def nmr_(g):
                        if g is not None:
                            dve.wait_ge(at["rstd1"], g + 1)
                            if has(g - 1):
                                dve.wait_ge(at["hp"], g)
                            V.scalar_tensor_tensor(nmr[:, :], mv_b[:, :, 0], -1.0, rs_b[:, 1, :], ALU.mult, ALU.mult).then_inc(at["nmr"], 1)

                    def f_(g):
                        if g is not None:
                            dve.wait_ge(at["rstd1"], g + 1)
                            for t in range(TG):
                                last = V.tensor_scalar(f_all[:, bass.ds(g * TG + t, 1), :].rearrange("p o c -> p (o c)"), x1[:, t, :],
                                                       mv_b[:, t, 0:1], rs_b[:, 0, t:t + 1], ALU.subtract, ALU.mult)
                            last.then_inc(at["f"], 1)

                    def lo(g):
                        if g is not None:
                            dve.wait_ge(at["hi"], g + 1)
                            if has(g - 1):
                                dve.wait_ge(at["pks"], g)
                                dve.wait_ge(at["v"], g)
                            V.tensor_tensor(hT_lo[:, 0:GT], banks[B_HT][:, :], hT_hi[:, 0:GT].bitcast(f32), ALU.subtract)
                            V.tensor_tensor(hT_lo[:, GT:], banks[B_HT][:, 0:NN], hT_hi[:, GT:].bitcast(f32), ALU.subtract).then_inc(at["lo"], 1)

                    def rope(g, dst, bank, col, projected, done, used):
                        if g is not None:
                            dve.wait_ge(projected, g + 1)
                            if has(g - 1):
                                dve.wait_ge(used, g)
                            V.tensor_tensor(dst[:, :].rearrange("p (g t) -> p g t", g=GR),
                                            banks[bank][:, :].rearrange("p (g t) -> p g t", g=GR),
                                            cst[:, col:col + NN].unsqueeze(1).broadcast_to([P, GR, NN]), ALU.mult).then_inc(done, 1)

                    def qc(g):
                        rope(g, q_cos, B_PQ, C_COS, at["pq"], at["qc"], at["qr"])

                    def qs(g):
                        rope(g, q_sin, B_PQS, C_SIN, at["pqs"], at["qs"], at["qr"])

                    def kc(g):
                        rope(g, k_cos, B_PK, C_COS, at["pk"], at["kc"], at["kr"])

                    def ks(g):
                        rope(g, k_sin, B_PKS, C_SIN, at["pks"], at["ks"], at["kr"])

                    def mask(g):
                        if g is not None:
                            dve.wait_ge(at["scores"], g + 1)
                            if has(g - 1):
                                dve.wait_ge(at["exp"], g)
                            for h in range(NH):
                                last = V.tensor_tensor(sc[:, :, h, :], banks[4 + h][:, 0:TG * NN].rearrange("p (t s) -> p t s", t=TG),
                                                       cst[:, C_MASK:C_MASK + NN].unsqueeze(1).broadcast_to([P, TG, NN]), ALU.add)
                            last.then_inc(at["mask"], 1)

                    def max_(g):
                        if g is not None:
                            dve.wait_ge(at["mask"], g + 1)
                            V.reduce_max(mx[:, :], sc[:, :, :, :].rearrange("p t h s -> p (t h) s"), AX.X).then_inc(at["max"], 1)

                    def nmax(g):
                        if g is not None:
                            dve.wait_ge(at["max"], g + 1)
                            if has(g - 1):
                                dve.wait_ge(at["exp"], g)
                            V.tensor_scalar(nmx[:, :], mx[:, :], -SCALE, None, ALU.mult).then_inc(at["nmax"], 1)

                    def ys(j):
                        return banks[B_Y[j]][:, 0:264].rearrange("p (t h e) -> p t h e", t=2, h=NH)

                    def rden_(g):
                        if g is not None:
                            dve.wait_ge(at["y"], g + 1)
                            for j in range(2):
                                last = V.reciprocal(rden[:, 2 * j:2 * j + 2, :].unsqueeze(3), ys(j)[:, :, :, 32:33])
                            last.then_inc(at["rden"], 1)

                    def yn_(g):
                        if g is not None:
                            dve.wait_ge(at["rden"], g + 1)
                            if has(g - 1):
                                dve.wait_ge(at["yT"], g)
                            for j in range(2):
                                last = V.tensor_tensor(yn[:, 2 * j:2 * j + 2, :].rearrange("p t (h e) -> p t h e", h=NH),
                                                       ys(j)[:, :, :, 0:32],
                                                       rden[:, 2 * j:2 * j + 2, :].unsqueeze(3).broadcast_to([P, 2, NH, HD]), ALU.mult)
                            last.then_inc(at["yn"], 1)

                    att = banks[B_WO][:, :].rearrange("p (t c) -> p t c", t=TG)

                    def f2_(g):
                        if g is not None:
                            dve.wait_ge(at["wo"], g + 1)
                            dve.wait_ge(at["f"], g + 1)
                            if has(g - 1):
                                dve.wait_ge(at["flat"], g)
                            V.tensor_tensor(f2[:, :, :], att, f_all[:, bass.ds(g * TG, TG), :], ALU.add).then_inc(at["f2"], 1)

                    def base1(g):
                        if g is not None:
                            dve.wait_ge(at["wo"], g + 1)
                            dve.wait_ge(at["base0"], g + 1)
                            V.tensor_tensor(base_all[:, bass.ds(g * TG, TG), :], att, base_all[:, bass.ds(g * TG, TG), :], ALU.add).then_inc(at["base1"], 1)

                    def ssv_(g):
                        if g is not None:
                            dve.wait_ge(at["ssq"], g + 1)
                            if has(g - 1):
                                dve.wait_ge(at["rms"], g)
                            V.tensor_scalar(ssv[:, :], ss[:, :], 1.0 / C, 1e-6, ALU.mult, ALU.add).then_inc(at["ssv"], 1)

                    def lg_(g):
                        if g is not None:
                            dve.wait_ge(at["logits"], g + 1)
                            V.tensor_copy(lg[:, :, :], banks[B_LOGITS][:, 0:TG * 8].rearrange("p (t e) -> p t e", t=TG)).then_inc(at["lg"], 1)

                    def top_(g):
                        if g is not None:
                            dve.wait_ge(at["lg"], g + 1)
                            held()
                            for t in range(TG):
                                last = V.max(top[:, t, :], lg[:, t, :])
                            last.then_inc(at["top"], 1)

                    def topi_(g):
                        if g is not None:
                            dve.wait_ge(at["top"], g + 1)
                            held()
                            for t in range(TG):
                                last = V.max_index(topi[:, t, :], top[:, t, :], lg[:, t, :])
                            last.then_inc(at["topi"], 1)

                    def topf_(g):
                        if g is not None:
                            dve.wait_ge(at["topi"], g + 1)
                            V.tensor_copy(topf[:, :, :], topi[:, :, 0:2]).then_inc(at["topf"], 1)

                    def oh_(g):
                        if g is not None:
                            dve.wait_ge(at["topf"], g + 1)
                            V.tensor_tensor(oh[:, :, :, :], topf[:, :, :].unsqueeze(3).broadcast_to([P, TG, 2, 8]),
                                            iota8.unsqueeze(1).unsqueeze(1).broadcast_to([P, TG, 2, 8]), ALU.is_equal).then_inc(at["oh"], 1)

                    def sel_(g):
                        if g is not None:
                            dve.wait_ge(at["oh"], g + 1)
                            if has(g - 1):
                                dve.wait_ge(at["rank"], g)
                            V.tensor_tensor(sel[:, :, :], oh[:, :, 0, :], oh[:, :, 1, :], ALU.add).then_inc(at["sel"], 1)

                    def carb(g):
                        if g is not None:
                            if first(g):
                                dve.wait_ge(pool_w, 3)
                            if has(g - 1):
                                dve.wait_ge(at["car"], g)
                                dve.wait_ge(at["rank"], g)
                            V.tensor_copy(carry_b[:, :], carry[:, :]).then_inc(at["carb"], 1)

                    def ssum(g):
                        if g is not None:
                            dve.wait_ge(at["sel"], g + 1)
                            V.reduce_sum(selsum[:, :], sel[:, :, :].rearrange("p t e -> p e t"), AX.X).then_inc(at["ssum"], 1)

                    def car(g):
                        if g is not None:
                            dve.wait_ge(at["carb"], g + 1)
                            dve.wait_ge(at["ssum"], g + 1)
                            V.tensor_tensor(carry[:, :], carry[:, :], selsum[:, :], ALU.add).then_inc(at["car"], 1)

                    def dtop_(g):
                        if g is not None:
                            dve.wait_ge(at["top"], g + 1)
                            if has(g - 1):
                                dve.wait_ge(at["etop"], g)
                            V.tensor_tensor(dtop[:, :, :], top[:, :, :], top[:, :, 0:1].broadcast_to([P, TG, 8]), ALU.subtract).then_inc(at["dtop"], 1)

                    def z_(g):
                        if g is not None:
                            dve.wait_ge(at["etop"], g + 1)
                            V.reduce_sum(z[:, :], etop[:, :, :], AX.X)
                            V.tensor_tensor(s2[:, :], etop[:, :, 0], etop[:, :, 1], ALU.add).then_inc(at["z"], 1)

                    def den_(g):
                        if g is not None:
                            dve.wait_ge(at["z"], g + 1)
                            V.scalar_tensor_tensor(den[:, :], z[:, :], 1e-9, s2[:, :], ALU.mult, ALU.add).then_inc(at["den"], 1)

                    def rec_(g):
                        if g is not None:
                            dve.wait_ge(at["den"], g + 1)
                            V.reciprocal(rec[:, :], den[:, :]).then_inc(at["rec"], 1)

                    def gate(g):
                        if g is not None:
                            dve.wait_ge(at["rec"], g + 1)
                            V.tensor_tensor(gates_all[:, bass.ds(g, 1), :].rearrange("p o (t k) -> p (o t) k", k=2), etop[:, :, 0:2],
                                            rec[:, :].unsqueeze(2).broadcast_to([P, TG, 2]), ALU.mult).then_inc(at["gate"], 1)

                    def rk(g):
                        if g is not None:
                            dve.wait_ge(at["rank"], g + 1)
                            V.tensor_tensor(rank[:, :, :], banks[B_RANK][:, 0:TG * 8].rearrange("p (t e) -> p t e", t=TG),
                                            cst[:, C_BASE:C_BASE + 8].unsqueeze(1).broadcast_to([P, TG, 8]), ALU.add).then_inc(at["rk"], 1)

                    def ohr_(g):
                        if g is not None:
                            dve.wait_ge(at["rk"], g + 1)
                            V.tensor_tensor(ohr[:, :, :, :], oh[:, :, :, :], rank[:, :, :].unsqueeze(2).broadcast_to([P, TG, 2, 8]), ALU.mult).then_inc(at["ohr"], 1)

                    def slotf_(g):
                        if g is not None:
                            dve.wait_ge(at["ohr"], g + 1)
                            V.reduce_sum(slotf[:, :], ohr[:, :, :, :].rearrange("p t k e -> p (t k) e"), AX.X).then_inc(at["slotf"], 1)

                    def slot(g):
                        if g is not None:
                            dve.wait_ge(at["slotf"], g + 1)
                            if has(g - 1):
                                dve.wait_ge(scattered, g * 16 * 2 * TG)
                            V.tensor_copy(slot_now[:, :], slotf[:, :]).then_inc(at["slot"], 1)
                            V.tensor_copy(slots_f[:, bass.ds(g, 1), :].rearrange("p o s -> p (o s)"), slotf[:, :]).then_inc(at["keep"], 1)

                    def body(g):
                        z_(g[5])
                        st0(g[0])
                        ssv_(g[4])
                        mv0(g[0])
                        mask(g[3])
                        max_(g[3])
                        nmax(g[3])
                        x1_(g[1])
                        lg_(g[4])
                        var0(g[0])
                        top_(g[4])
                        topi_(g[4])
                        den_(g[5])
                        topf_(g[4])
                        kc(g[2])
                        oh_(g[4])
                        ks(g[2])
                        carb(g[4])
                        sel_(g[4])
                        st1(g[1])
                        ssum(g[4])
                        mv1(g[1])
                        rk(g[4])
                        var1(g[1])
                        ohr_(g[4])
                        slotf_(g[4])
                        slot(g[4])
                        qc(g[2])
                        nmr_(g[1])
                        xn_(g[0])
                        qs(g[2])
                        rden_(g[3])
                        yn_(g[3])
                        dtop_(g[4])
                        f_(g[1])
                        rec_(g[5])
                        car(g[4])
                        lo(g[1])
                        gate(g[5])
                        f2_(g[3])
                        base1(g[3])
                        if first(g[0]):
                            weights()
                    sweep(dve, body)

                    n = [0]

                    def link(ins):
                        n[0] += 1
                        ins.then_inc(dve_t, 1)
                        dve.wait_ge(dve_t, n[0])

                    dve.wait_ge(at["keep"], NG)
                    link(V.tensor_copy(carry_b[:, :], carry[:, :]))
                    dve.wait_ge(pe_t, 1)
                    link(V.tensor_scalar(cnti[:, :], banks[0][:, 0:8], float(P - 1), None, ALU.add))
                    link(V.tensor_tensor(fill[:, :], banks[0][0:1, 0:8], cst[0:1, C_BASE:C_BASE + 8], ALU.add))
                    link(V.tensor_scalar(cnti[:, :], cnti[:, :], 7, None, ALU.arith_shift_right))
                    link(V.tensor_copy(nblk[:, :], cnti[:, :]))
                    link(V.tensor_tensor(tri_nb[:, :, :], nblk[0:1, :].unsqueeze(1).broadcast_to([1, 8, 8]),
                                         cst[0:1, C_TRI8:C_TRI8 + 64].rearrange("p (a b) -> p a b", a=8), ALU.mult))
                    link(V.reduce_sum(cum[:, :], tri_nb[:, :, :], AX.X))
                    link(V.tensor_tensor(past[:, :, :], cst[0:1, C_BLK:C_BLK + NBLK].unsqueeze(2).broadcast_to([1, NBLK, 8]),
                                         cum[:, :].unsqueeze(1).broadcast_to([1, NBLK, 8]), ALU.is_ge))
                    link(V.tensor_tensor(pastn[:, :, :], past[:, :, :], nblk[0:1, :].unsqueeze(1).broadcast_to([1, NBLK, 8]), ALU.mult))
                    link(V.reduce_sum(bexp[:, :], past[:, :, :], AX.X))
                    link(V.reduce_sum(bprev[:, :], pastn[:, :, :], AX.X))
                    link(V.tensor_tensor(brow[:, :], cst[0:1, C_BLK:C_BLK + NBLK], bprev[:, :], ALU.subtract))
                    link(V.scalar_tensor_tensor(brow[:, :], bexp[:, :], float(REG), brow[:, :], ALU.mult, ALU.add))
                    link(V.tensor_scalar(table[:, 1, :], brow[:, :], float(P), None, ALU.mult))
                    link(V.tensor_scalar(table[:, 0, :], bexp[:, :], float(NE0 - 1), None, ALU.min))
                    link(V.tensor_scalar(gaps[:, :], nblk[:, :], -float(REG), float(P), ALU.add, ALU.mult))
                    slots = slots_f[:, :, :].rearrange("p g s -> p (g s)")
                    link(V.tensor_tensor(gap[:, :, :], slots.unsqueeze(2).broadcast_to([P, NG * 2 * TG, 7]),
                                         cst[:, C_BASE + 1:C_BASE + 8].unsqueeze(1).broadcast_to([P, NG * 2 * TG, 7]), ALU.is_ge))
                    link(V.tensor_tensor(gap[:, :, :], gap[:, :, :], gaps[:, 0:7].unsqueeze(1).broadcast_to([P, NG * 2 * TG, 7]), ALU.mult))
                    link(V.reduce_sum(back[:, :], gap[:, :, :], AX.X))
                    link(V.tensor_tensor(slots_all[:, :, :].rearrange("p g s -> p (g s)"), slots, back[:, :], ALU.add))
                @block.tensor
                def _(pe):
                    def gnnT(g):
                        if g is not None:
                            pe.wait_ge(ld_adj, g * 32 + 32)
                            pe.wait_ge(at["xn"], g + 1)
                            if has(g - 1):
                                pe.wait_ge(at["x1"], upto(g - 1))
                            for t in range(TG):
                                last = T.matmul(banks[B_GNNT][:, t * P:(t + 1) * P], xn[:, t, :], adjt[:, t, :], start=True, stop=True)
                            last.then_inc(at["gnnT"], 1)

                    def gnn(g):
                        if g is not None:
                            if first(g):
                                pe.wait_ge(ld_w, 16 * 8)
                            pe.wait_ge(at["tT"], g + 1)
                            if has(g - 3):
                                pe.wait_ge(at["f2"], upto(g - 3))
                            if has(g - 3):
                                pe.wait_ge(at["base1"], upto(g - 3))
                            for t in range(TG):
                                last = T.matmul(banks[B_GNN][:, t * P:(t + 1) * P], tT[:, t, :], gw[:, :], start=True, stop=True)
                            last.then_inc(at["gnn"], 1)

                    def hT(g):
                        if g is not None:
                            pe.wait_ge(at["hp"], g + 1)
                            if has(g - 1):
                                pe.wait_ge(at["qc"], upto(g - 1))
                            for t in range(TG):
                                last = T.transpose(banks[B_HT][:, t * P:(t + 1) * P], hp[:, t, :], ident)
                            last.then_inc(at["hT"], 1)

                    def project(g, n, bank, done):
                        for q, (w, h) in enumerate(((wq_hi, hT_hi), (wq_hi, hT_lo), (wq_lo, hT_hi))):
                            last = T.matmul(banks[bank][:, :], w[:, n * P:(n + 1) * P], h[:, 0:GT], start=q == 0, stop=q == 2)
                        last.then_inc(done, 1)

                    def pq(g):
                        if g is not None:
                            pe.wait_ge(at["lo"], g + 1)
                            if first(g):
                                pe.wait_ge(dve_w, 6)
                            if has(g):
                                pe.wait_ge(at["hi"], upto(g))
                            project(g, 0, B_PQ, at["pq"])

                    def pqs(g):
                        if g is not None:
                            pe.wait_ge(at["lo"], g + 1)
                            if first(g):
                                pe.wait_ge(dve_w, 6)
                            if has(g):
                                pe.wait_ge(at["kc"], upto(g))
                            project(g, 1, B_PQS, at["pqs"])

                    def pk(g):
                        if g is not None:
                            pe.wait_ge(at["lo"], g + 1)
                            if first(g):
                                pe.wait_ge(dve_w, 6)
                            if has(g - 1):
                                pe.wait_ge(at["mask"], upto(g - 1))
                            project(g, 2, B_PK, at["pk"])

                    def pks(g):
                        if g is not None:
                            pe.wait_ge(at["lo"], g + 1)
                            if first(g):
                                pe.wait_ge(dve_w, 6)
                            if has(g - 1):
                                pe.wait_ge(at["mask"], upto(g - 1))
                            project(g, 3, B_PKS, at["pks"])

                    def v(g):
                        if g is not None:
                            pe.wait_ge(at["lo"], g + 1)
                            if first(g):
                                pe.wait_ge(dve_w, 6)
                            if has(g - 1):
                                pe.wait_ge(at["vd"], upto(g - 1))
                            for gr in range(GR):
                                for q, (h, w) in enumerate(((hT_hi, wq_hi), (hT_hi, wq_lo), (hT_lo, wq_hi))):
                                    last = T.matmul(banks[B_V][:, gr * NN:(gr + 1) * NN], h[:, gr * NN:gr * NN + P],
                                                    w[:, 512:576], start=q == 0, stop=q == 2)
                            last.then_inc(at["v"], 1)

                    def scores(g):
                        if g is not None:
                            pe.wait_ge(at["qr"], g + 1)
                            pe.wait_ge(at["kr"], g + 1)
                            if has(g - 1):
                                pe.wait_ge(at["rden"], upto(g - 1))
                            if has(g - 1):
                                pe.wait_ge(at["yn"], upto(g - 1))
                            if has(g - 1):
                                pe.wait_ge(at["yTc"], upto(g - 1))
                            if has(g):
                                pe.wait_ge(at["qs"], upto(g))
                            for t in range(TG):
                                for gi in range(2):
                                    tok = slice(t * P + gi * NN, t * P + (gi + 1) * NN)
                                    for h in range(NH):
                                        hs = slice(h * HD, (h + 1) * HD)
                                        last = T.matmul(banks[4 + h][gi * NN:(gi + 1) * NN, t * NN:(t + 1) * NN],
                                                        q_rot[hs, tok], k_rot[hs, tok], start=True, stop=True)
                            last.then_inc(at["scores"], 1)

                    def prT_(g):
                        if g is not None:
                            pe.wait_ge(at["exp"], g + 1)
                            if has(g):
                                pe.wait_ge(at["mask"], upto(g))
                            if has(g - 1):
                                pe.wait_ge(at["lg"], upto(g - 1))
                            for p in range(2):
                                for t in range(TG):
                                    last = T.transpose(banks[B_PRT[p]][:, t * P:(t + 1) * P],
                                                       pr[:, t, 2 * p:2 * p + 2, :].rearrange("p h s -> p (h s)"), ident)
                            last.then_inc(at["prT"], 1)

                    def y(g):
                        if g is not None:
                            pe.wait_ge(at["prTc"], g + 1)
                            pe.wait_ge(at["vd"], g + 1)
                            for t in range(TG):
                                for gi in range(2):
                                    for p in range(2):
                                        last = T.matmul(banks[B_Y[t // 2]][gi * NN:(gi + 1) * NN, (t % 2) * 132 + p * 66:(t % 2) * 132 + p * 66 + 66],
                                                        prT[:, p, t, gi * NN:(gi + 1) * NN], v_diag[:, 2 * t + gi, p, :],
                                                        start=True, stop=True)
                            last.then_inc(at["y"], 1)

                    def yT_(g):
                        if g is not None:
                            pe.wait_ge(at["yn"], g + 1)
                            if has(g + 1):
                                pe.wait_ge(at["ks"], upto(g + 1))
                            for t in range(TG):
                                last = T.transpose(banks[B_YT][:, t * P:(t + 1) * P], yn[:, t, :], ident)
                            last.then_inc(at["yT"], 1)

                    def wo_(g):
                        if g is not None:
                            pe.wait_ge(at["yTc"], g + 1)
                            if has(g + 3):
                                pe.wait_ge(at["tT"], upto(g + 3))
                            for t in range(TG):
                                last = T.matmul(banks[B_WO][:, t * P:(t + 1) * P], yT[:, t, :], wo_sb[:, :], start=True, stop=True)
                            last.then_inc(at["wo"], 1)

                    def flatT_(g):
                        if g is not None:
                            pe.wait_ge(at["flat"], g + 1)
                            if has(g + 1):
                                pe.wait_ge(at["mask"], upto(g + 1))
                            for t in range(TG):
                                last = T.transpose(banks[B_FLATT][:, t * P:(t + 1) * P], flat[:, t, :], ident)
                            last.then_inc(at["flatT"], 1)

                    def logits(g):
                        if g is not None:
                            pe.wait_ge(at["flatTc"], g + 1)
                            for t in range(TG):
                                last = T.matmul(banks[B_LOGITS][:, t * 8:t * 8 + 8], flatT[:, t, :], rws[:, :], start=True, stop=True)
                            last.then_inc(at["logits"], 1)

                    def rank(g):
                        if g is not None:
                            pe.wait_ge(at["sel"], g + 1)
                            pe.wait_ge(at["carb"], g + 1)
                            if has(g - 1):
                                pe.wait_ge(at["rk"], upto(g - 1))
                            bank = banks[B_RANK]
                            T.matmul(bank[:, 0:TG * 8], trib[:, :], sel[:, :, :].rearrange("p t e -> p (t e)"), start=True, stop=False)
                            T.matmul(bank[:, 0:TG * 8], oneb[:, :], carry_b[:, :].unsqueeze(1).broadcast_to([P, TG, 8]), start=False, stop=False)
                            for t in range(TG - 1):
                                last = T.matmul(bank[:, (t + 1) * 8:TG * 8], oneb[:, :],
                                                sel[:, t:t + 1, :].broadcast_to([P, TG - 1 - t, 8]), start=False, stop=t == TG - 2)
                            last.then_inc(at["rank"], 1)

                    def body(g):
                        scores(g[3])
                        gnn(g[1])
                        pq(g[2])
                        flatT_(g[4])
                        pk(g[2])
                        logits(g[4])
                        pks(g[2])
                        v(g[2])
                        rank(g[4])
                        prT_(g[3])
                        pqs(g[2])
                        y(g[3])
                        hT(g[1])
                        gnnT(g[0])
                        yT_(g[3])
                        wo_(g[3])
                    sweep(pe, body)
                    pe.wait_ge(dve_t, 1)
                    T.matmul(banks[0][:, 0:8], oneb[:, :], carry_b[:, :], start=True, stop=True).then_inc(pe_t, 1)

        with ExitStack() as ctx:
            sb, sem = sb_in(ctx), sem_in(ctx)
            xs, ys = sb("xs", [P, 4, C]), sb("ys", [P, 4, C])
            xT_hi, xT_lo = sb("xT_hi", [P, 2, P], f32r), sb("xT_lo", [P, 2, P], f32r)
            act1, prod = sb("act1", [P, 2, HIDP]), sb("prod", [P, 2, KC * P])
            prodT = sb("prodT", [P, 2, KC * P])
            ld = [sem(f"ld_slots{u}") for u in range(4)]
            st = [sem(f"st_slots{u}") for u in range(4)]
            padded = sem("padded")
            pt = [sem(n) for n in ("pe_xT", "pe_h", "pe_prodT", "pe_y")]
            xT_done, h_done, prodT_done, y_done = pt
            hi_done, silu_done, prodT_copied = sem("hi_done"), sem("silu_done"), sem("prodT_copied")
            lo_done, prod_done, y_copied = sem("lo_done"), sem("prod_done"), sem("y_copied")

            def quarter(k, u):
                return (k // 4 + 1) * 16 if isinstance(k, int) else (k - u) * 4 + 16

            def blocks(engine, body, skew):
                for k in range(8):
                    body(k, k % 4)
                with engine.Fori(2, NBLK // 4) as j:
                    for u in range(4):
                        body(j * 4 + u, u)
                for k in range(NBLK, NBLK + skew):
                    body(k, k % 4)

            def live(k, back):
                return not isinstance(k, int) or 0 <= k - back < NBLK

            def live_prior(k, back):
                return not isinstance(k, int) or k - back >= 0

            with nc.Block() as block:
                @block.sync
                def _(sp):
                    def row_of(k):
                        return sp.value_load(table[0:1, 1, bass.ds(k, 1)], min_val=0, max_val=ROWS - P)

                    def body(k, u):
                        if live(k, 0):
                            row = row_of(k)
                            if live_prior(k, 4):
                                sp.wait_ge(xT_done, k - 3)
                            sp.dma_start(xs[:, u, :], slots_in[bass.ds(row, P), :]).then_inc(ld[u], 16)
                        if live(k, 7):
                            sp.wait_ge(y_copied, k - 6)
                            sp.dma_start(slots_out[bass.ds((k - 7) * P, P), :], ys[:, (u - 7) % 4, :]).then_inc(st[(u - 7) % 4], 16)
                    blocks(sp, body, 7)
                    for u in range(4):
                        sp.wait_ge(st[u], NBLK // 4 * 16)

                @block.gpsimd
                def _(pool):
                    G.memset(prod[:, :, :], 0.0).then_inc(padded, 1)

                @block.scalar
                def _(act):
                    S.preload_act_table(ACT.Silu)

                    def body(k, u):
                        if live(k, 0):
                            act.wait_ge(xT_done, k + 1)
                            if live_prior(k, 2):
                                act.wait_ge(h_done, k - 1)
                            S.activation(xT_hi[:, u % 2, :], banks[0][:, 0:P], ACT.Copy).then_inc(hi_done, 1)
                        if live(k, 1):
                            act.wait_ge(h_done, k)
                            if live_prior(k, 3):
                                act.wait_ge(prod_done, k - 2)
                            S.activation(act1[:, (u - 1) % 2, :], banks[1 + (u - 1) % 2][:, 0:HIDP], ACT.Silu).then_inc(silu_done, 1)
                        if live(k, 2):
                            act.wait_ge(prodT_done, k - 1)
                            if live_prior(k, 4):
                                act.wait_ge(y_done, k - 3)
                            S.activation(prodT[:, u % 2, :], banks[5 + u % 2][:, 0:KC * P], ACT.Copy).then_inc(prodT_copied, 1)
                    blocks(act, body, 2)

                @block.vector
                def _(dve):
                    dve.wait_ge(padded, 1)

                    def body(k, u):
                        if live(k, 0):
                            dve.wait_ge(hi_done, k + 1)
                            if live_prior(k, 2):
                                dve.wait_ge(h_done, k - 1)
                            V.tensor_tensor(xT_lo[:, u % 2, :], banks[0][:, 0:P], xT_hi[:, u % 2, :].bitcast(f32), ALU.subtract).then_inc(lo_done, 1)
                        if live(k, 1):
                            dve.wait_ge(silu_done, k)
                            if live_prior(k, 3):
                                dve.wait_ge(prodT_done, k - 2)
                            V.tensor_tensor(prod[:, (u - 1) % 2, 0:HIDP], banks[3 + (u - 1) % 2][:, 0:HIDP], act1[:, (u - 1) % 2, :],
                                            ALU.mult).then_inc(prod_done, 1)
                        if live(k, 3):
                            dve.wait_ge(y_done, k - 2)
                            if live_prior(k, 7):
                                dve.wait_ge(st[(u - 3) % 4], quarter(k - 7, (u - 3) % 4))
                            V.tensor_copy(ys[:, (u - 3) % 4, :], banks[7][:, 0:C]).then_inc(y_copied, 1)
                    blocks(dve, body, 3)

                @block.tensor
                def _(pe):
                    def expert(k):
                        return pe.value_load(table[0:1, 0, bass.ds(k, 1)], min_val=0, max_val=NE0 - 1)

                    def body(k, u):
                        if live(k, 0):
                            pe.wait_ge(ld[u], quarter(k, u))
                            if live_prior(k, 1):
                                pe.wait_ge(lo_done, k)
                            T.transpose(banks[0][:, 0:P], xs[:, u, :], ident).then_inc(xT_done, 1)
                        if live(k, 1):
                            e, par = expert(k - 1), (u - 1) % 2
                            pe.wait_ge(lo_done, k)
                            if live_prior(k, 3):
                                pe.wait_ge(prod_done, k - 2)
                            for n in range(2):
                                for q, (xx, ww) in enumerate(((xT_hi, w13_hi), (xT_hi, w13_lo), (xT_lo, w13_hi))):
                                    last = T.matmul(banks[1 + 2 * n + par][:, 0:HIDP], xx[:, par, :],
                                                    ww[:, bass.ds(e * (2 * HIDP) + n * HIDP, HIDP)], start=q == 0, stop=q == 2)
                            last.then_inc(h_done, 1)
                        if live(k, 2):
                            pe.wait_ge(prod_done, k - 1)
                            if live_prior(k, 4):
                                pe.wait_ge(prodT_copied, k - 3)
                            for n in range(KC):
                                last = T.transpose(banks[5 + u % 2][:, n * P:(n + 1) * P], prod[:, u % 2, n * P:(n + 1) * P], ident)
                            last.then_inc(prodT_done, 1)
                        if live(k, 3):
                            e = expert(k - 3)
                            pe.wait_ge(prodT_copied, k - 2)
                            if live_prior(k, 4):
                                pe.wait_ge(y_copied, k - 3)
                            for n in range(KC):
                                last = T.matmul(banks[7][:, 0:C], prodT[:, (u - 3) % 2, n * P:(n + 1) * P],
                                                w2_sb[:, bass.ds(e * (KC * C) + n * C, C)], start=n == 0, stop=n == KC - 1)
                            last.then_inc(y_done, 1)
                    blocks(pe, body, 3)

        with ExitStack() as ctx:
            sb, sem = sb_in(ctx), sem_in(ctx)
            gw, gb = sb("gw1", [P, C]), sb("gb1", [P, C])
            rw1, rw1_hi, rw1_lo = sb("rw1", [P, RH]), sb("rw1_hi", [P, RH], f32r), sb("rw1_lo", [P, RH], f32r)
            rb1, rw2, rb2 = sb("rb1", [RH, 1]), sb("rw2", [RH, 8]), sb("rb2", [P, 8])
            ew1_hi, ew1_lo = sb("ew1_hi", [P, NE1 * C], f32r), sb("ew1_lo", [P, NE1 * C], f32r)
            ew1, ew2, ew3 = (sb(n, [P, NE1 * C]) for n in ("ew1", "ew2", "ew3"))
            eb1, eb2, eb3 = sb("eb1", [P, NE1]), sb("eb2", [P, NE1]), sb("eb3", [NE1, C])
            mhalf = sb("mhalf1", [P, TG])
            adjt = [sb(f"adjt_c{i}", [P, TG, C]) for i in range(2)]
            rows = [sb(f"expert_rows{i}", [P, 2 * TG, C]) for i in range(2)]
            slot_now = [sb(f"slot_c{i}", [P, 2 * TG], u32) for i in range(2)]
            gate_now = [sb(f"gate_c{i}", [P, 2 * TG]) for i in range(2)]
            deg = [sb(f"deg{i}", [P, TG]) for i in range(2)]
            f3_hi = [sb(f"f3_hi{i}", [P, GT], f32r) for i in range(2)]
            f3_lo = [sb(f"f3_lo{i}", [P, GT], f32r) for i in range(2)]
            gateT = [sb(f"gateT{i}", [8, GT]) for i in range(2)]
            gate_bc = [sb(f"gate_bc{i}", [P, NE1, GT]) for i in range(2)]
            x2a, x2, xn, xb, tT, f3, ob = (sb(n, [P, TG, C]) for n in ("x2a", "x2", "xn_c", "xb_c", "tT_c", "f3", "ob"))
            degv, dscale, xscale = sb("degv", [P, TG]), sb("dscale", [P, TG]), sb("xscale", [P, TG])
            st_a, mv_a, var_a, rs_a = sb("st_c", [P, TG, 6]), sb("mv_c", [P, TG, 2]), sb("var_c", [P, TG]), sb("rs_c", [P, TG])
            st_b, mv_b, var_b, rs_b = sb("st_d", [P, TG, 6]), sb("mv_d", [P, TG, 2]), sb("var_d", [P, TG]), sb("rs_d", [P, TG])
            rhT = sb("rhT", [RH, GT])
            lg, top, topi = sb("lg_c", [P, TG, 8]), sb("top_c", [P, TG, 8]), sb("topi_c", [P, TG, 8], u32)
            topf, oh, dtop, etop = sb("topf_c", [P, TG, 2]), sb("oh_c", [P, TG, 2, 8]), sb("dtop_c", [P, TG, 8]), sb("etop_c", [P, TG, 8])
            z, zr, pk, dp, ep, e1 = sb("z_c", [P, TG]), sb("zr", [P, TG]), sb("pk", [P, TG, 2]), sb("dp", [P, TG]), sb("ep", [P, TG]), sb("e1", [P, TG])
            rk, ohr, gate = sb("rk", [P, TG, 2]), sb("ohr_c", [P, TG, 2, 8]), sb("gate", [P, TG, 8])
            h1 = [sb(f"h1_{i}", [P, GT]) for i in range(2)]
            h2 = [sb(f"h2_{i}", [P, GT]) for i in range(2)]
            h2g = [sb(f"h2g_{i}", [P, GT]) for i in range(2)]
            oT = sb("oT", [P, GT])
            spare, spare2 = sb("spare_c", [P, 1]), sb("spare_d", [P, 1])

            ld_w, ld_adj = sem("ld_w1"), [sem(f"ld_adj_c{i}") for i in range(2)]
            zeroed, dve_w = sem("zeroed1"), sem("dve_w1")
            gathered = [sem(f"gathered{i}") for i in range(2)]
            gates_loaded = [sem(f"gates_loaded{i}") for i in range(2)]
            gates_stored, stored = sem("gates_stored"), sem("stored")
            NW = 13
            vs = Steps(sem("vs"), "pick")
            va = Steps(sem("va1"), "degv add0 add1 stats moments var scale xn")
            vb = Steps(sem("vb1"), "x3 stats moments var f3")
            vc = Steps(sem("vc1"), "lo lg top topi topf oh dtop z zr pk dp e1 rk0 rk1 ohr gate")
            vd = Steps(sem("vd1"), "g0 g1 g2 g3 g4 g5 out")
            ab = Steps(sem("ab1"), "tT")
            ac = Steps(sem("ac1"), "hi rh etop ep gateT")
            ad = Steps(sem("ad1"), "a0 a1 b0 a2 b1 a3 b2 a4 b3 a5 b4 b5 oT")
            pa = Steps(sem("pa1"), "deg rstd")
            pb = Steps(sem("pb1"), "xb rstd")
            ta = Steps(sem("ta1"), "deg")
            tb = Steps(sem("tb1"), "tT gnn")
            tc = Steps(sem("tc1"), "f3T rh logits gateT")
            td = Steps(sem("td1"), "a0 a1 b0 a2 b1 c0 a3 b2 c1 a4 b3 c2 a5 b4 c3 b5 c4 c5 oT")

            def sweep(engine, body):
                def step(i, u):
                    gs = [i - k for k in range(4)]
                    if isinstance(i, int):
                        gs = [g if 0 <= g < NG else None for g in gs]
                    body(gs, [(u - k) % 2 for k in range(4)])
                for i in range(4):
                    step(i, i)
                with engine.Fori(2, NG // 2) as j:
                    for u in range(2):
                        step(j * 2 + u, u)
                for i in range(NG, NG + 3):
                    step(i, i)

            def pair(g, p):
                return (g // 2 + 1) * 16 if isinstance(g, int) else (g - p) * 8 + 16

            with nc.Block() as block:
                @block.sync
                def _(sp):
                    for dst, src in ((gw[:, :], gnn1_w), (gb[:, :], gnn1_b.partition_broadcast(P)), (rw1[:, :], r1_w1),
                                     (rb1[:, :], r1_b1), (rw2[:, :], r1_w2), (ew1[:, :], e_w1), (ew2[:, :], e_w2), (ew3[:, :], e_w3),
                                     (eb1[:, :], e_b1), (eb2[:, :], e_b2), (eb3[:, :], e_b3)):
                        sp.dma_start(dst, src).then_inc(ld_w, 16)
                    sp.wait_ge(zeroed, 4)
                    sp.dma_start(rb2[:, 0:NE1], r1_b2.partition_broadcast(P)).then_inc(ld_w, 16)
                    sp.dma_start(cst[:, :], consts).then_inc(ld_w, 16)

                    def body(gs, ps):
                        a, b, c, d = gs
                        if a is not None:
                            if not (isinstance(a, int) and a < 2):
                                sp.wait_ge(tb.sem, tb.at("tT", a - 2))
                            src = adj_t[bass.ds(a * GT, GT), :].rearrange("(t b m) n -> b m t n", b=2, m=NN)
                            for k in range(2):
                                sp.dma_start(adjt[ps[0]][k * NN:(k + 1) * NN, :, k * NN:(k + 1) * NN], src[k]).then_inc(ld_adj[ps[0]], 16)
                        if c is not None:
                            if not (isinstance(c, int) and c < 2):
                                sp.wait_ge(vd.sem, vd.at("g5", c - 2))
                            sp.wait_ge(ac.sem, ac.at("gateT", c))
                            sp.dma_start(gates_dram[ps[2]], gateT[ps[2]][0:NE1, :]).then_inc(gates_stored, 16)
                            sp.wait_ge(gates_stored, c * 16 + 16)
                            sp.dma_start(gate_bc[ps[2]][:, :, :], gates_dram[ps[2]].partition_broadcast(P)).then_inc(gates_loaded[ps[2]], 16)
                        if d is not None:
                            sp.wait_ge(vd.sem, vd.at("out", d))
                            sp.dma_start(out[bass.ds(d * GT, GT), :].rearrange("(t p) c -> p t c", p=P), ob[:, :, :]).then_inc(stored, 16)
                    sweep(sp, body)
                    sp.wait_ge(stored, 16 * NG)

                @block.gpsimd
                def _(pool):
                    G.memset(adjt[0][:, :, :], 0.0).then_inc(zeroed, 1)
                    G.memset(adjt[1][:, :, :], 0.0).then_inc(zeroed, 1)
                    G.memset(rb2[:, :], -1e30).then_inc(zeroed, 1)
                    G.memset(mhalf[:, :], -0.5).then_inc(zeroed, 1)
                    pool.wait_ge(ld_w, 16 * NW)

                    def body(gs, ps):
                        a, b, c, d = gs
                        if b is not None:
                            if not first(b):
                                pool.wait_ge(vb.sem, vb.at("x3", b - 1))
                            pool.wait_ge(va.sem, va.at("add1", b))
                            G.tensor_tensor(xb[:, :, :], x2[:, :, :], gb[:, :].unsqueeze(1).broadcast_to([P, TG, C]),
                                            ALU.add).then_inc(pb.sem, 1)
                        if a is not None:
                            pool.wait_ge(vs.sem, vs.at("pick", a))
                            if not (isinstance(a, int) and a < 2):
                                pool.wait_ge(va.sem, va.at("add1", a - 2))
                            G.tensor_tensor(spare[:, :], mhalf[:, 0:1], mhalf[:, 0:1], ALU.add)
                            for n in range(2 * TG):
                                G.indirect_dma_start(out=rows[ps[0]][:, n, :], out_offset=None, in_=slots_out,
                                                     in_offset=bass.IndirectOffsetOnAxis(ap=slot_now[ps[0]][:, n:n + 1], axis=0),
                                                     bounds_check=NBLK * P - 1).then_inc(gathered[ps[0]], 16)
                        if b is not None:
                            pool.wait_ge(vb.sem, vb.at("var", b))
                            G.tensor_tensor(rs_b[:, :], var_b[:, :], mhalf[:, :], ALU.pow).then_inc(pb.sem, 1)
                        if a is not None:
                            pool.wait_ge(va.sem, va.at("degv", a))
                            G.tensor_tensor(deg[ps[0]][:, :], degv[:, :], mhalf[:, :], ALU.pow).then_inc(pa.sem, 1)
                            pool.wait_ge(va.sem, va.at("var", a))
                            G.tensor_tensor(rs_a[:, :], var_a[:, :], mhalf[:, :], ALU.pow).then_inc(pa.sem, 1)
                    sweep(pool, body)

                @block.scalar
                def _(act):
                    S.preload_act_table(ACT.Exp)
                    act.wait_ge(ld_w, 16 * NW)

                    def body(gs, ps):
                        a, b, c, d = gs

                        def relu_a(n):
                            if d is None:
                                return
                            act.wait_ge(td.sem, td.at(f"a{n}", d))
                            if n >= 2:
                                act.wait_ge(td.sem, td.at(f"b{n - 2}", d))
                            S.activation(h1[n % 2][:, :], banks[n % 2][:, :], ACT.Relu, bias=eb1[:, n:n + 1]).then_inc(ad.sem, 1)

                        def relu_b(n):
                            if d is None:
                                return
                            act.wait_ge(td.sem, td.at(f"b{n}", d))
                            if n >= 2:
                                act.wait_ge(vd.sem, vd.at(f"g{n - 2}", d))
                            S.activation(h2[n % 2][:, :], banks[2 + n % 2][:, :], ACT.Relu, bias=eb2[:, n:n + 1]).then_inc(ad.sem, 1)

                        if c is not None:
                            act.wait_ge(tc.sem, tc.at("f3T", c))
                            if not (isinstance(c, int) and c < 2):
                                act.wait_ge(td.sem, td.at("a5", c - 2))
                            S.activation(f3_hi[ps[2]][:, :], banks[6][:, :], ACT.Copy).then_inc(ac.sem, 1)
                        relu_a(0)
                        relu_a(1)
                        if b is not None:
                            act.wait_ge(tb.sem, tb.at("tT", b))
                            if not first(b):
                                act.wait_ge(tb.sem, tb.at("gnn", b - 1))
                            S.activation(tT[:, :, :], banks[5][:, :], ACT.Copy).then_inc(ab.sem, 1)
                        relu_b(0)
                        if c is not None:
                            act.wait_ge(tc.sem, tc.at("rh", c))
                            if not first(c):
                                act.wait_ge(tc.sem, tc.at("logits", c - 1))
                            S.activation(rhT[:, :], banks[6][0:RH, :], ACT.Relu, bias=rb1[:, :]).then_inc(ac.sem, 1)
                        relu_a(2)
                        relu_b(1)
                        relu_a(3)
                        relu_b(2)
                        relu_a(4)
                        if c is not None:
                            act.wait_ge(vc.sem, vc.at("dtop", c))
                            if not first(c):
                                act.wait_ge(vc.sem, vc.at("pk", c - 1))
                            S.activation(etop[:, :, :], dtop[:, :, :], ACT.Exp).then_inc(ac.sem, 1)
                        relu_b(3)
                        relu_a(5)
                        if c is not None:
                            act.wait_ge(vc.sem, vc.at("dp", c))
                            if not first(c):
                                act.wait_ge(vc.sem, vc.at("rk1", c - 1))
                            S.activation(ep[:, :], dp[:, :], ACT.Exp).then_inc(ac.sem, 1)
                        relu_b(4)
                        relu_b(5)
                        if c is not None:
                            act.wait_ge(tc.sem, tc.at("gateT", c))
                            if not (isinstance(c, int) and c < 2):
                                act.wait_ge(gates_stored, c * 16 - 16)
                                act.wait_ge(td.sem, td.at("c5", c - 2))
                            S.activation(gateT[ps[2]][:, :], banks[6][0:8, :], ACT.Copy).then_inc(ac.sem, 1)
                        if d is not None:
                            act.wait_ge(td.sem, td.at("c5", d))
                            if not first(d):
                                act.wait_ge(td.sem, td.at("oT", d - 1))
                            S.activation(oT[:, :], banks[4][:, :], ACT.Copy).then_inc(ad.sem, 1)
                    sweep(act, body)

                @block.vector
                def _(dve):
                    dve.wait_ge(ld_w, 16 * NW)
                    for hi, lo, w in ((ew1_hi, ew1_lo, ew1), (rw1_hi, rw1_lo, rw1)):
                        V.tensor_copy(hi[:, :], w[:, :]).then_inc(dve_w, 1)
                    dve.wait_ge(dve_w, 2)
                    for hi, lo, w in ((ew1_hi, ew1_lo, ew1), (rw1_hi, rw1_lo, rw1)):
                        V.tensor_tensor(lo[:, :], w[:, :], hi[:, :].bitcast(f32), ALU.subtract).then_inc(dve_w, 1)

                    def held():
                        V.memset(spare2[:, :], 0.0)

                    def all8(ap):
                        return ap.unsqueeze(2).broadcast_to([P, TG, 8])

                    def moments(steps, g, st, mv, var, src):
                        for t in range(TG):
                            last = V.bn_stats(st[:, t, :], src(t))
                        last.then_inc(steps.sem, 1)
                        dve.wait_ge(steps.sem, steps.at("stats", g))
                        held()
                        for t in range(TG):
                            last = V.bn_aggr(mv[:, t, :], st[:, t, :])
                        last.then_inc(steps.sem, 1)
                        dve.wait_ge(steps.sem, steps.at("moments", g))
                        V.tensor_scalar(var[:, :], mv[:, :, 1], 1e-5, None, ALU.add).then_inc(steps.sem, 1)

                    def body(gs, ps):
                        a, b, c, d = gs

                        def gated(n):
                            if d is None:
                                return
                            dve.wait_ge(ad.sem, ad.at(f"b{n}", d))
                            if n == 0:
                                dve.wait_ge(gates_loaded[ps[3]], pair(d, ps[3]))
                            if n >= 2:
                                dve.wait_ge(td.sem, td.at(f"c{n - 2}", d))
                            elif not first(d):
                                dve.wait_ge(td.sem, td.at(f"c{n + 4}", d - 1))
                            V.tensor_tensor(h2g[n % 2][:, :], h2[n % 2][:, :], gate_bc[ps[3]][:, n, :], ALU.mult).then_inc(vd.sem, 1)

                        if a is not None:
                            if not (isinstance(a, int) and a < 2):
                                dve.wait_ge(gathered[ps[0]], pair(a, ps[0]) * (2 * TG) - 16 * 2 * TG)
                            V.tensor_copy(slot_now[ps[0]][:, :], slots_all[:, bass.ds(a, 1), :].rearrange("p o s -> p (o s)"))
                            V.tensor_copy(gate_now[ps[0]][:, :], gates_all[:, bass.ds(a, 1), :].rearrange("p o s -> p (o s)")).then_inc(vs.sem, 1)
                        if c is not None:
                            dve.wait_ge(ac.sem, ac.at("hi", c))
                            if not (isinstance(c, int) and c < 2):
                                dve.wait_ge(td.sem, td.at("a5", c - 2))
                            V.tensor_tensor(f3_lo[ps[2]][:, :], banks[6][:, :], f3_hi[ps[2]][:, :].bitcast(f32), ALU.subtract).then_inc(vc.sem, 1)
                        gated(0)
                        gated(1)
                        if b is not None:
                            dve.wait_ge(tb.sem, tb.at("gnn", b))
                            dve.wait_ge(pb.sem, pb.at("xb", b))
                            for t in range(TG):
                                last = V.scalar_tensor_tensor(base_all[:, bass.ds(b * TG + t, 1), :].rearrange("p o c -> p (o c)"),
                                                              banks[5][:, t * P:(t + 1) * P], deg[ps[1]][:, t:t + 1], xb[:, t, :], ALU.mult, ALU.add)
                            last.then_inc(vb.sem, 1)
                            dve.wait_ge(vb.sem, vb.at("x3", b))
                            held()
                            moments(vb, b, st_b, mv_b, var_b, lambda t: base_all[:, bass.ds(b * TG + t, 1), :].rearrange("p o c -> p (o c)"))
                        gated(2)
                        if c is not None:
                            dve.wait_ge(tc.sem, tc.at("logits", c))
                            V.tensor_tensor(lg[:, :, :], banks[6][:, 0:TG * 8].rearrange("p (t e) -> p t e", t=TG),
                                            rb2[:, :].unsqueeze(1).broadcast_to([P, TG, 8]), ALU.add).then_inc(vc.sem, 1)
                            dve.wait_ge(vc.sem, vc.at("lg", c))
                            held()
                            for t in range(TG):
                                last = V.max(top[:, t, :], lg[:, t, :])
                            last.then_inc(vc.sem, 1)
                            dve.wait_ge(vc.sem, vc.at("top", c))
                            held()
                            for t in range(TG):
                                last = V.max_index(topi[:, t, :], top[:, t, :], lg[:, t, :])
                            last.then_inc(vc.sem, 1)
                            dve.wait_ge(vc.sem, vc.at("topi", c))
                            V.tensor_copy(topf[:, :, :], topi[:, :, 0:2]).then_inc(vc.sem, 1)
                            dve.wait_ge(vc.sem, vc.at("topf", c))
                            V.tensor_tensor(oh[:, :, :, :], topf[:, :, :].unsqueeze(3).broadcast_to([P, TG, 2, 8]),
                                            iota8.unsqueeze(1).unsqueeze(1).broadcast_to([P, TG, 2, 8]), ALU.is_equal).then_inc(vc.sem, 1)
                            if not first(c):
                                dve.wait_ge(ac.sem, ac.at("etop", c - 1))
                            V.tensor_tensor(dtop[:, :, :], top[:, :, :], top[:, :, 0:1].broadcast_to([P, TG, 8]), ALU.subtract).then_inc(vc.sem, 1)
                        if b is not None:
                            dve.wait_ge(pb.sem, pb.at("rstd", b))
                            if not first(b):
                                dve.wait_ge(tc.sem, tc.at("f3T", b - 1))
                            for t in range(TG):
                                last = V.tensor_scalar(f3[:, t, :], base_all[:, bass.ds(b * TG + t, 1), :].rearrange("p o c -> p (o c)"),
                                                       mv_b[:, t, 0:1], rs_b[:, t:t + 1], ALU.subtract, ALU.mult)
                            last.then_inc(vb.sem, 1)
                        gated(3)
                        if a is not None:
                            dve.wait_ge(ta.sem, ta.at("deg", a))
                            V.tensor_scalar(degv[:, :], banks[7][:, 0:TG], 1e-5, None, ALU.add).then_inc(va.sem, 1)
                        if c is not None:
                            dve.wait_ge(ac.sem, ac.at("etop", c))
                            V.reduce_sum(z[:, :], etop[:, :, :], AX.X).then_inc(vc.sem, 1)
                            dve.wait_ge(vc.sem, vc.at("z", c))
                            V.reciprocal(zr[:, :], z[:, :]).then_inc(vc.sem, 1)
                            dve.wait_ge(vc.sem, vc.at("zr", c))
                            V.tensor_tensor(pk[:, :, :], etop[:, :, 0:2], zr[:, :].unsqueeze(2).broadcast_to([P, TG, 2]), ALU.mult).then_inc(vc.sem, 1)
                            dve.wait_ge(vc.sem, vc.at("pk", c))
                            V.tensor_tensor(dp[:, :], pk[:, :, 1], pk[:, :, 0], ALU.subtract).then_inc(vc.sem, 1)
                        gated(4)
                        if a is not None:
                            dve.wait_ge(gathered[ps[0]], pair(a, ps[0]) * (2 * TG))
                            for t in range(TG):
                                last = V.scalar_tensor_tensor(x2a[:, t, :], rows[ps[0]][:, 2 * t, :], gate_now[ps[0]][:, 2 * t:2 * t + 1],
                                                              base_all[:, bass.ds(a * TG + t, 1), :].rearrange("p o c -> p (o c)"), ALU.mult, ALU.add)
                            last.then_inc(va.sem, 1)
                            dve.wait_ge(va.sem, va.at("add0", a))
                            if not first(a):
                                dve.wait_ge(pb.sem, pb.at("xb", a - 1))
                            for t in range(TG):
                                last = V.scalar_tensor_tensor(x2[:, t, :], rows[ps[0]][:, 2 * t + 1, :], gate_now[ps[0]][:, 2 * t + 1:2 * t + 2],
                                                              x2a[:, t, :], ALU.mult, ALU.add)
                            last.then_inc(va.sem, 1)
                            dve.wait_ge(va.sem, va.at("add1", a))
                            held()
                            moments(va, a, st_a, mv_a, var_a, lambda t: x2[:, t, :])
                        if c is not None:
                            dve.wait_ge(ac.sem, ac.at("ep", c))
                            V.tensor_scalar(e1[:, :], ep[:, :], 1.0, None, ALU.add).then_inc(vc.sem, 1)
                            dve.wait_ge(vc.sem, vc.at("e1", c))
                            V.reciprocal(rk[:, :, 0], e1[:, :]).then_inc(vc.sem, 1)
                            dve.wait_ge(vc.sem, vc.at("rk0", c))
                            V.tensor_tensor(rk[:, :, 1], ep[:, :], rk[:, :, 0], ALU.mult).then_inc(vc.sem, 1)
                            dve.wait_ge(vc.sem, vc.at("rk1", c))
                            V.tensor_tensor(ohr[:, :, :, :], oh[:, :, :, :], rk[:, :, :].unsqueeze(3).broadcast_to([P, TG, 2, 8]), ALU.mult).then_inc(vc.sem, 1)
                            dve.wait_ge(vc.sem, vc.at("ohr", c))
                            if not first(c):
                                dve.wait_ge(tc.sem, tc.at("gateT", c - 1))
                            V.tensor_tensor(gate[:, :, :], ohr[:, :, 0, :], ohr[:, :, 1, :], ALU.add).then_inc(vc.sem, 1)
                        gated(5)
                        if a is not None:
                            dve.wait_ge(pa.sem, pa.at("rstd", a))
                            V.tensor_tensor(xscale[:, :], rs_a[:, :], deg[ps[0]][:, :], ALU.mult).then_inc(va.sem, 1)
                            dve.wait_ge(va.sem, va.at("scale", a))
                            if not first(a):
                                dve.wait_ge(tb.sem, tb.at("tT", a - 1))
                            for t in range(TG):
                                last = V.tensor_scalar(xn[:, t, :], x2[:, t, :], mv_a[:, t, 0:1], xscale[:, t:t + 1], ALU.subtract, ALU.mult)
                            last.then_inc(va.sem, 1)
                        if d is not None:
                            dve.wait_ge(td.sem, td.at("oT", d))
                            if not first(d):
                                dve.wait_ge(stored, d * 16)
                            V.tensor_tensor(ob[:, :, :], banks[7][:, :].rearrange("p (t c) -> p t c", t=TG),
                                            base_all[:, bass.ds(d * TG, TG), :], ALU.add).then_inc(vd.sem, 1)
                    sweep(dve, body)

                @block.tensor
                def _(pe):
                    pe.wait_ge(ld_w, 16 * NW)
                    pe.wait_ge(dve_w, 4)

                    def body(gs, ps):
                        a, b, c, d = gs
                        par = ps[3]

                        def layer_a(n):
                            if d is None:
                                return
                            if n >= 2:
                                pe.wait_ge(ad.sem, ad.at(f"a{n - 2}", d))
                            elif not first(d):
                                pe.wait_ge(ad.sem, ad.at(f"a{n + 4}", d - 1))
                            w = slice(n * C, (n + 1) * C)
                            for q, (ww, ff) in enumerate(((ew1_hi, f3_hi), (ew1_hi, f3_lo), (ew1_lo, f3_hi))):
                                last = T.matmul(banks[n % 2][:, :], ww[:, w], ff[par][:, :], start=q == 0, stop=q == 2)
                            last.then_inc(td.sem, 1)

                        def layer_b(n):
                            if d is None:
                                return
                            pe.wait_ge(ad.sem, ad.at(f"a{n}", d))
                            if n >= 2:
                                pe.wait_ge(ad.sem, ad.at(f"b{n - 2}", d))
                            elif not first(d):
                                pe.wait_ge(ad.sem, ad.at(f"b{n + 4}", d - 1))
                            T.matmul(banks[2 + n % 2][:, :], ew2[:, n * C:(n + 1) * C], h1[n % 2][:, :], start=True, stop=True).then_inc(td.sem, 1)

                        def layer_c(n):
                            if d is None:
                                return
                            pe.wait_ge(vd.sem, vd.at(f"g{n}", d))
                            if n == 0 and not first(d):
                                pe.wait_ge(ad.sem, ad.at("oT", d - 1))
                            last = T.matmul(banks[4][:, :], ew3[:, n * C:(n + 1) * C], h2g[n % 2][:, :], start=n == 0, stop=False)
                            if n == NE1 - 1:
                                last = T.matmul(banks[4][:, :], eb3[:, :], gateT[par][0:NE1, :], start=False, stop=True)
                            last.then_inc(td.sem, 1)

                        if c is not None:
                            pe.wait_ge(vb.sem, vb.at("f3", c))
                            if not first(c):
                                pe.wait_ge(ac.sem, ac.at("gateT", c - 1))
                            for t in range(TG):
                                last = T.transpose(banks[6][:, t * P:(t + 1) * P], f3[:, t, :], ident)
                            last.then_inc(tc.sem, 1)
                        layer_a(0)
                        layer_a(1)
                        if b is not None:
                            pe.wait_ge(va.sem, va.at("xn", b))
                            if not first(b):
                                pe.wait_ge(vb.sem, vb.at("x3", b - 1))
                            for t in range(TG):
                                last = T.matmul(banks[5][:, t * P:(t + 1) * P], xn[:, t, :], adjt[ps[1]][:, t, :], start=True, stop=True)
                            last.then_inc(tb.sem, 1)
                        layer_b(0)
                        if c is not None:
                            pe.wait_ge(vc.sem, vc.at("lo", c))
                            for q, (ww, ff) in enumerate(((rw1_hi, f3_hi), (rw1_hi, f3_lo), (rw1_lo, f3_hi))):
                                last = T.matmul(banks[6][0:RH, :], ww[:, :], ff[ps[2]][:, :], start=q == 0, stop=q == 2)
                            last.then_inc(tc.sem, 1)
                        layer_a(2)
                        layer_b(1)
                        if b is not None:
                            pe.wait_ge(ab.sem, ab.at("tT", b))
                            for t in range(TG):
                                last = T.matmul(banks[5][:, t * P:(t + 1) * P], tT[:, t, :], gw[:, :], start=True, stop=True)
                            last.then_inc(tb.sem, 1)
                        layer_c(0)
                        layer_a(3)
                        layer_b(2)
                        if c is not None:
                            pe.wait_ge(ac.sem, ac.at("rh", c))
                            for t in range(TG):
                                last = T.matmul(banks[6][:, t * 8:t * 8 + 8], rhT[:, t * P:(t + 1) * P], rw2[:, :], start=True, stop=True)
                            last.then_inc(tc.sem, 1)
                        layer_c(1)
                        layer_a(4)
                        if a is not None:
                            pe.wait_ge(ld_adj[ps[0]], pair(a, ps[0]) * 2)
                            if d is not None and not first(d):
                                pe.wait_ge(vd.sem, vd.at("out", d - 1))
                            for t in range(TG):
                                last = T.matmul(banks[7][:, t:t + 1], adjt[ps[0]][:, t, :], cst[:, C_ONE:C_ONE + 1], start=True, stop=True)
                            last.then_inc(ta.sem, 1)
                        layer_b(3)
                        layer_c(2)
                        layer_a(5)
                        layer_b(4)
                        layer_c(3)
                        layer_b(5)
                        layer_c(4)
                        if c is not None:
                            pe.wait_ge(vc.sem, vc.at("gate", c))
                            for t in range(TG):
                                last = T.transpose(banks[6][0:8, t * P:(t + 1) * P], gate[:, t, :], ident)
                            last.then_inc(tc.sem, 1)
                        layer_c(5)
                        if d is not None:
                            pe.wait_ge(ad.sem, ad.at("oT", d))
                            if a is not None:
                                pe.wait_ge(va.sem, va.at("degv", a))
                            elif not first(d):
                                pe.wait_ge(vd.sem, vd.at("out", d - 1))
                            for t in range(TG):
                                last = T.transpose(banks[7][:, t * P:(t + 1) * P], oT[:, t * P:(t + 1) * P], ident)
                            last.then_inc(td.sem, 1)
                    sweep(pe, body)


def laid_out(inp):
    a = {k: np.ascontiguousarray(v) for k, v in inp.items()}
    half = HD // 2

    def swapped(w):
        return w.reshape(-1, 2, half, C)[:, ::-1].reshape(-1, C)

    def repeated(w):
        return np.repeat(w.reshape(NH // 2, 1, HD, C), 2, 1).reshape(-1, C)

    wq, wk, wv = a["L0_ffn_wq"], repeated(a["L0_ffn_wk"]), a["L0_ffn_wv"]
    w13 = np.zeros((C, NE0, 2, HIDP), np.float32)
    w13[:, :, 0, :HID] = a["L0_ffn_w1"].transpose(2, 0, 1)
    w13[:, :, 1, :HID] = a["L0_ffn_w3"].transpose(2, 0, 1)
    w2 = np.zeros((NE0, KC * P, C), np.float32)
    w2[:, :HID] = a["L0_ffn_w2"].transpose(0, 2, 1)
    r2 = np.zeros((RH, 8), np.float32)
    r2[:, :NE1] = a["L1_ffn_router_w2"]
    return dict(
        x=a["x"].reshape(TOK, C),
        adj_t=a["adj"].transpose(0, 2, 1).reshape(TOK, NN),
        gnn0_w=a["L0_gnn_weight"], gnn0_b=a["L0_gnn_bias"],
        ln1=a["L0_ffn_ln1_w"].reshape(C, 1), ln2=a["L0_ffn_ln2_w"].reshape(C, 1),
        wqkv=np.concatenate([wq, swapped(wq), wk, swapped(wk), wv], 0).T,
        wo=a["L0_ffn_wo"].T, router0=a["L0_ffn_router_w"].T,
        w13=w13.reshape(C, -1), w2=w2.reshape(NE0, KC, P, C).transpose(2, 0, 1, 3).reshape(P, -1),
        gnn1_w=a["L1_gnn_weight"], gnn1_b=a["L1_gnn_bias"],
        r1_w1=a["L1_ffn_router_w1"], r1_b1=a["L1_ffn_router_b1"].reshape(RH, 1),
        r1_w2=r2, r1_b2=a["L1_ffn_router_b2"],
        e_w1=a["L1_ffn_expert_w1"].transpose(1, 0, 2).reshape(C, -1), e_b1=a["L1_ffn_expert_b1"].T,
        e_w2=a["L1_ffn_expert_w2"].transpose(1, 0, 2).reshape(C, -1), e_b2=a["L1_ffn_expert_b2"].T,
        e_w3=a["L1_ffn_expert_w3"].transpose(1, 0, 2).reshape(C, -1), e_b3=a["L1_ffn_expert_b3"],
        consts=constants(),
    )


def kernel(**inputs):
    import concourse.bacc as _bacc
    from concourse.bass_utils import run_bass_kernel_spmd as _run

    nc = _bacc.Bacc("TRN2", target_bir_lowering=False, num_devices=1)
    arrays = {f"in_{k}": np.ascontiguousarray(v) for k, v in laid_out(inputs).items()}
    args = {k[3:]: nc.dram_tensor(k, v.shape, mybir.dt.float32, kind="ExternalInput").ap() for k, v in arrays.items()}
    out = nc.dram_tensor("out_0", (TOK, C), mybir.dt.float32, kind="ExternalOutput").ap()
    build(nc, out=out, **args)
    r = _run(nc, [arrays], core_ids=[0])
    return r.results[0]["out_0"].reshape(NB, NN, C)
```

```python
from contextlib import ExitStack

import numpy as np
import concourse.bass as bass
from concourse import mybir

P = 128
NB, NN, C = 128, 64, 128
TOK = NB * NN
TG = 4
GT = TG * P
NG = TOK // GT
GR = GT // NN
NH, HD = 4, 32
NE0, HID = 8, 341
HIDP = HID + 1
KC = 3
NE1, RH = 6, 64
MB = TOK // P
REG = MB + 1
DUM = NE0 * REG
NBLK = 2 * TOK // P + NE0
NDUM = NE0
ROWS = (DUM + NDUM) * P

C_ID, C_COS, C_SIN, C_MASK = 0, 128, 192, 256
C_TRI, C_ONE, C_IOTA, C_BASE = 320, 448, 576, 584
C_BLK, C_TRI8 = 592, 592 + NBLK
C_N = C_TRI8 + 64


def constants():
    c = np.zeros((P, C_N), np.float32)
    c[:, C_ID:C_ID + P] = np.eye(P)
    inv = 1.0 / 10000.0 ** (np.arange(0, HD, 2, dtype=np.float32) / HD)
    fr = np.outer(np.arange(NN, dtype=np.float32), inv)
    emb = np.concatenate([fr, fr], -1)
    sign = np.where(np.arange(HD) < HD // 2, -1.0, 1.0)
    c[:, C_COS:C_COS + NN] = np.tile(np.cos(emb).T, (NH, 1))
    c[:, C_SIN:C_SIN + NN] = np.tile((np.sin(emb) * sign).T, (NH, 1))
    t = np.arange(P) % NN
    c[:, C_MASK:C_MASK + NN] = np.where(np.arange(NN)[None] <= t[:, None], 0.0, -1e30)
    c[:, C_TRI:C_TRI + P] = np.arange(P)[:, None] < np.arange(P)[None]
    c[:, C_ONE:C_ONE + P] = 1.0
    c[:, C_IOTA:C_IOTA + 8] = np.arange(8)
    c[:, C_BASE:C_BASE + 8] = np.arange(8) * REG * P
    c[:, C_BLK:C_BLK + NBLK] = np.arange(NBLK)
    c[:, C_TRI8:C_TRI8 + 64] = (np.arange(8)[None] <= np.arange(8)[:, None]).reshape(-1)
    return c


class Steps:

    def __init__(self, sem, names):
        self.sem, self.names = sem, names.split()

    def at(self, name, g):
        return g * len(self.names) + (self.names.index(name) + 1)


def signals(sem, names):
    return {n: sem(n) for n in names.split()}


def has(g):
    return not isinstance(g, int) or g >= 0


def exists(g):
    return not isinstance(g, int) or 0 <= g < NG


def build(nc, x, adj_t, gnn0_w, gnn0_b, ln1, ln2, wqkv, wo, router0, w13, w2, gnn1_w, gnn1_b,
          r1_w1, r1_b1, r1_w2, r1_b2, e_w1, e_b1, e_w2, e_b2, e_w3, e_b3, consts, out):
    f32, f32r, bf16 = mybir.dt.float32, mybir.dt.float32r, mybir.dt.bfloat16
    u32, i32 = mybir.dt.uint32, mybir.dt.int32
    ALU, ACT, AX = mybir.AluOpType, mybir.ActivationFunctionType, mybir.AxisListType
    V, S, T, G = nc.vector, nc.scalar, nc.tensor, nc.gpsimd
    SCALE = float(HD) ** -0.5

    slots_in = nc.dram_tensor("slots_in", (ROWS, C), f32, kind="Internal").ap()
    slots_out = nc.dram_tensor("slots_out", (NBLK * P, C), f32, kind="Internal").ap()
    gates_dram = [nc.dram_tensor(f"gates_dram{i}", (NE1, GT), f32, kind="Internal").ap() for i in range(2)]

    def first(g):
        return isinstance(g, int) and g == 0

    with ExitStack() as whole:
        def sb_in(ctx):
            return lambda name, shape, dt=f32: ctx.enter_context(nc.sbuf_tensor(name, shape, dt))

        def sem_in(ctx):
            return lambda name: ctx.enter_context(nc.semaphore(name))

        sb, sem = sb_in(whole), sem_in(whole)
        banks = [whole.enter_context(nc.psum_tensor(f"bank{i}", [P, 512], f32)) for i in range(8)]

        cst = sb("cst", [P, C_N])
        ident = cst[:, C_ID:C_ID + P]
        iota8 = cst[:, C_IOTA:C_IOTA + 8]
        base_all = sb("base_all", [P, NG * TG, C])
        slots_all = sb("slots_all", [P, NG, 2 * TG], u32)
        gates_all = sb("gates_all", [P, NG, 2 * TG])
        w13_hi = sb("w13_hi", [P, NE0 * 2 * HIDP], f32r)
        w13_lo = sb("w13_lo", [P, NE0 * 2 * HIDP], f32r)
        w2_sb = sb("w2_sb", [P, NE0 * KC * C])
        table = sb("table", [1, 2, NBLK], i32)

        with ExitStack() as ctx:
            sb, sem = sb_in(ctx), sem_in(ctx)
            f_all = sb("f_all", [P, NG * TG, C])
            stage = f_all[:, NG * TG - 43:, :].rearrange("p t c -> p (t c)")[:, 0:NE0 * 2 * HIDP]
            gw, gb, wo_sb = sb("gw", [P, C]), sb("gb", [P, C]), sb("wo_sb", [P, C])
            rw, ln = sb("rw", [P, NE0]), sb("ln", [P, 2])
            rws = sb("rws", [P, NE0])
            wq_raw = sb("wq_raw", [P, 576])
            wq_hi, wq_lo = sb("wq_hi", [P, 576], f32r), sb("wq_lo", [P, 576], f32r)
            trib, oneb = sb("trib", [P, P], bf16), sb("oneb", [P, P], bf16)
            xt, xb, xn, adjt = (sb(n, [P, TG, C]) for n in ("xt", "xb", "xn", "adjt"))
            tT, x1, hp = (sb(n, [P, TG, C]) for n in ("tT", "x1", "hp"))
            hT_hi, hT_lo = sb("hT_hi", [P, GT + NN], f32r), sb("hT_lo", [P, GT + NN], f32r)
            q_cos, q_sin, k_cos, k_sin = (sb(n, [P, GT]) for n in ("q_cos", "q_sin", "k_cos", "k_sin"))
            q_rot, k_rot = sb("q_rot", [P, GT]), sb("k_rot", [P, GT])
            v_diag = sb("v_diag", [P, GR, 2, 66])
            sc, pr = sb("sc", [P, TG, NH, NN]), sb("pr", [P, TG, NH, NN])
            prT = sb("prT", [P, 2, TG, P])
            yn, yT, f2, flat, flatT = (sb(n, [P, TG, C]) for n in ("yn", "yT", "f2", "flat", "flatT"))
            junk = sb("junk", [P, TG, C])
            zrow = sb("zrow", [P, C])
            st_a, mv_a, rs_a = sb("st_a", [P, TG, 6]), sb("mv_a", [P, TG, 2]), sb("rs_a", [P, TG])
            var_a, var_b, mhalf = sb("var_a", [P, TG]), sb("var_b", [P, 2, TG]), sb("mhalf", [P, 2, TG])
            st_b, mv_b = sb("st_b", [P, TG, 6]), sb("mv_b", [P, TG, 2])
            rs_b = sb("rs_b", [P, 2, TG])
            mx, nmx = sb("mx", [P, TG * NH]), sb("nmx", [P, TG * NH])
            rden = sb("rden", [P, TG, NH])
            ss, ssv, rr2 = sb("ss", [P, TG]), sb("ssv", [P, TG]), sb("rr2", [P, TG])
            lg, top, topi = sb("lg", [P, TG, 8]), sb("top", [P, TG, 8]), sb("topi", [P, TG, 8], u32)
            topf, oh = sb("topf", [P, TG, 2]), sb("oh", [P, TG, 2, 8])
            sel, carry, carry_b = sb("sel", [P, TG, 8], bf16), sb("carry", [P, 8]), sb("carry_b", [P, 8], bf16)
            selsum = sb("selsum", [P, 8])
            dtop, etop = sb("dtop", [P, TG, 8]), sb("etop", [P, TG, 8])
            z, s2, den, rec = (sb(n, [P, TG]) for n in ("z", "s2", "den", "rec"))
            rank, ohr, slotf = sb("rank", [P, TG, 8]), sb("ohr", [P, TG, 2, 8]), sb("slotf", [P, TG * 2])
            slot_now = sb("slot_now", [P, 2 * TG], u32)
            cnti, nblk = sb("cnti", [P, 8], i32), sb("nblk", [P, 8])
            slots_f, gaps = sb("slots_f", [P, NG, 2 * TG]), sb("gaps", [P, 8])
            tri_nb, cum = sb("tri_nb", [1, 8, 8]), sb("cum", [1, 8])
            left = f_all[:, :, :].rearrange("p t c -> p (t c)")
            past, pastn = (left[0:1, i * NBLK * 8:(i + 1) * NBLK * 8].rearrange("p (k e) -> p k e", e=8) for i in range(2))
            gap = left[:, 2 * NBLK * 8:2 * NBLK * 8 + NG * 2 * TG * 7].rearrange("p (s e) -> p s e", e=7)
            back = left[:, 3 * NBLK * 8:3 * NBLK * 8 + NG * 2 * TG]
            bexp, bprev, brow = sb("bexp", [1, NBLK]), sb("bprev", [1, NBLK]), sb("brow", [1, NBLK])
            fill = sb("fill", [1, 8], i32)
            spare, spare2, nmr = sb("spare", [P, 8]), sb("spare2", [P, 1]), sb("nmr", [P, TG])

            ld_x, ld_adj, ld_w, ld_big, ld_w2 = (sem(n) for n in ("ld_x", "ld_adj", "ld_w", "ld_big", "ld_w2"))
            zeroed, zero_fill, scattered = sem("zeroed"), sem("zero_fill"), sem("scattered")
            act_w, dve_w, pool_w = sem("act_w"), sem("dve_w"), sem("pool_w")
            dve_t, pe_t = sem("dve_t"), sem("pe_t")
            B_GNNT, B_GNN, B_HT, B_V = 2, 2, 3, 1
            B_PQ, B_PQS, B_PK, B_PKS = 3, 7, 7, 6
            B_PRT, B_Y = (4, 5), (4, 5)
            B_YT, B_WO, B_FLATT, B_LOGITS, B_RANK = 6, 2, 5, 5, 0
            DEEP = 5
            at = signals(sem, "st0 mv0 var0 rstd0 xb xn gnnT tT gnn x1 st1 mv1 var1 rstd1 nmr hp f base0 "
                             "hT hi lo pq pqs pk pks qc qs kc ks qr kr v vd "
                             "scores mask max nmax exp prT prTc y rden yn yT yTc wo f2 base1 ssq ssv rms flat flatT flatTc logits "
                             "etop z den rec gate rank")
            router = Steps(sem("router"), "lg top topi topf oh carb sel ssum rk ohr slotf slot keep dtop car")

            def sweep(engine, body):
                for i in range(DEEP):
                    body([i - k if i >= k else None for k in range(DEEP + 1)])
                with engine.Fori(DEEP, NG) as i:
                    body([i - k for k in range(DEEP + 1)])
                for i in range(NG, NG + DEEP):
                    body([i - k if i - k < NG else None for k in range(DEEP + 1)])

            with nc.Block() as block:
                @block.sync
                def _(sp):
                    def load_x(g):
                        if g is None:
                            return
                        if has(g - 1):
                            sp.wait_ge(at["xn"], g)
                            sp.wait_ge(at["xb"], g)
                        sp.dma_start(xt[:, :, :], x[bass.ds(g * GT, GT), :].rearrange("(t p) c -> p t c", p=P)).then_inc(ld_x, 16)

                    def load_adj(g):
                        if g is None:
                            return
                        if has(g - 1):
                            sp.wait_ge(at["gnnT"], g)
                        rows = adj_t[bass.ds(g * GT, GT), :].rearrange("(t b m) n -> b m t n", b=2, m=NN)
                        if first(g):
                            sp.wait_ge(zeroed, 1)
                        for b in range(2):
                            sp.dma_start(adjt[b * NN:(b + 1) * NN, :, b * NN:(b + 1) * NN], rows[b]).then_inc(ld_adj, 16)

                    load_x(0)
                    sp.dma_start(cst[:, :], consts).then_inc(ld_w, 16)
                    load_adj(0)
                    for dst, src in ((gw[:, :], gnn0_w), (gb[:, :], gnn0_b.partition_broadcast(P)),
                                     (ln[:, 0:1], ln1), (ln[:, 1:2], ln2), (wo_sb[:, :], wo), (rw[:, :], router0),
                                     (wq_raw[:, :], wqkv)):
                        sp.dma_start(dst, src).then_inc(ld_w, 16)
                    sp.dma_start(stage, w13).then_inc(ld_big, 16)
                    load_x(1)
                    load_adj(1)
                    sp.dma_start(w2_sb[:, :], w2).then_inc(ld_w2, 16)
                    sp.wait_ge(zeroed, 2)
                    for k in range(NDUM):
                        sp.dma_start(slots_in[(DUM + k) * P:(DUM + k + 1) * P, :], zrow[:, :]).then_inc(zero_fill, 16)
                    with sp.Fori(2, NG) as g:
                        load_x(g)
                        load_adj(g)
                    sp.wait_ge(dve_t, 3)
                    for e in range(NE0):
                        row = sp.value_load(fill[0:1, e:e + 1], min_val=0, max_val=ROWS - P)
                        sp.dma_start(slots_in[bass.ds(row, P), :], zrow[:, :]).then_inc(zero_fill, 16)
                    sp.wait_ge(zero_fill, 16 * (NDUM + NE0))
                    sp.wait_ge(ld_w2, 16)

                @block.gpsimd
                def _(pool):
                    G.memset(adjt[:, :, :], 0.0).then_inc(zeroed, 1)
                    G.memset(mhalf[:, :, :], -0.5).then_inc(pool_w, 1)
                    G.memset(zrow[:, :], 0.0).then_inc(zeroed, 1)
                    G.memset(v_diag[:, :, :, :], 0.0).then_inc(pool_w, 1)
                    G.memset(carry[:, :], 0.0).then_inc(pool_w, 1)
                    pool.wait_ge(pool_w, 3)
                    G.memset(v_diag[0:NN, :, :, 32:33], 1.0).then_inc(pool_w, 1)
                    pool.wait_ge(pool_w, 4)
                    G.memset(v_diag[NN:P, :, :, 65:66], 1.0).then_inc(pool_w, 1)
                    pool.wait_ge(pool_w, 5)

                    def rstd0(g):
                        if g is not None:
                            pool.wait_ge(at["var0"], g + 1)
                            if has(g - 1):
                                pool.wait_ge(at["xn"], g)
                            G.tensor_tensor(rs_a[:, :], var_a[:, :], mhalf[:, 0, :], ALU.pow).then_inc(at["rstd0"], 1)

                    def xb_(g):
                        if g is not None:
                            pool.wait_ge(ld_x, g * 16 + 16)
                            if first(g):
                                pool.wait_ge(ld_w, 16 * 8)
                            if has(g - 1):
                                pool.wait_ge(at["x1"], g)
                            G.tensor_tensor(xb[:, :, :], xt[:, :, :], gb[:, :].unsqueeze(1).broadcast_to([P, TG, C]), ALU.add).then_inc(at["xb"], 1)

                    def rstd1(g):
                        if g is not None:
                            pool.wait_ge(at["var1"], g + 1)
                            if has(g - 1):
                                pool.wait_ge(at["f"], g)
                                pool.wait_ge(at["hp"], g)
                            G.tensor_tensor(rs_b[:, :, :], var_b[:, :, :], mhalf[:, :, :], ALU.pow).then_inc(at["rstd1"], 1)

                    def base0(g):
                        if g is not None:
                            pool.wait_ge(at["f"], g + 1)
                            G.tensor_tensor(base_all[:, bass.ds(g * TG, TG), :], x1[:, :, :], f_all[:, bass.ds(g * TG, TG), :], ALU.add).then_inc(at["base0"], 1)

                    def qr(g):
                        if g is not None:
                            pool.wait_ge(at["qc"], g + 1)
                            pool.wait_ge(at["qs"], g + 1)
                            if has(g - 1):
                                pool.wait_ge(at["scores"], g)
                            G.tensor_tensor(q_rot[:, :], q_cos[:, :], q_sin[:, :], ALU.add).then_inc(at["qr"], 1)

                    def kr(g):
                        if g is not None:
                            pool.wait_ge(at["kc"], g + 1)
                            pool.wait_ge(at["ks"], g + 1)
                            if has(g - 1):
                                pool.wait_ge(at["scores"], g)
                            G.tensor_tensor(k_rot[:, :], k_cos[:, :], k_sin[:, :], ALU.add).then_inc(at["kr"], 1)

                    def rms(g):
                        if g is not None:
                            pool.wait_ge(at["ssv"], g + 1)
                            if has(g - 1):
                                pool.wait_ge(at["flat"], g)
                            G.tensor_tensor(rr2[:, :], ssv[:, :], mhalf[:, 0, :], ALU.pow).then_inc(at["rms"], 1)

                    def sc(n, g):
                        if g is not None:
                            if n == 0:
                                pool.wait_ge(router.sem, router.at("slot", g))
                                G.tensor_tensor(spare2[:, :], mhalf[:, 0, 0:1], mhalf[:, 0, 0:1], ALU.add)
                            G.indirect_dma_start(
                                out=slots_in, out_offset=bass.IndirectOffsetOnAxis(ap=slot_now[:, n:n + 1], axis=0),
                                in_=flat[:, n // 2, :], in_offset=None, bounds_check=ROWS - 1).then_inc(scattered, 16)

                    def weights_lo():
                        pool.wait_ge(act_w, 2)
                        G.tensor_tensor(w13_lo[:, :], stage, w13_hi[:, :].bitcast(f32), ALU.subtract).then_inc(pool_w, 1)

                    def body(g):
                        sc(7, g[5])
                        rms(g[4])
                        base0(g[2])
                        rstd0(g[0])
                        xb_(g[0])
                        kr(g[2])
                        rstd1(g[1])
                        sc(0, g[4])
                        sc(1, g[4])
                        sc(2, g[4])
                        sc(3, g[4])
                        qr(g[2])
                        sc(4, g[4])
                        sc(5, g[4])
                        sc(6, g[4])
                        if first(g[4]):
                            weights_lo()
                    sweep(pool, body)
                    pool.wait_ge(scattered, 16 * 2 * TG * NG)

                @block.scalar
                def _(act):
                    S.preload_act_table(ACT.Exp)

                    def weights_hi():
                        act.wait_ge(ld_w, 16 * 8)
                        act.wait_ge(ld_big, 16)
                        S.activation(stage, stage, ACT.Copy, scale=ln[:, 1:2]).then_inc(act_w, 1)
                        act.wait_ge(act_w, 1)
                        S.activation(w13_hi[:, :], stage, ACT.Copy).then_inc(act_w, 1)

                    def tT_(g):
                        if g is not None:
                            act.wait_ge(at["gnnT"], g + 1)
                            if has(g - 1):
                                act.wait_ge(at["gnn"], g)
                            S.activation(tT[:, :, :], banks[B_GNNT][:, :], ACT.Copy).then_inc(at["tT"], 1)

                    def hp_(g):
                        if g is not None:
                            act.wait_ge(at["nmr"], g + 1)
                            if has(g - 1):
                                act.wait_ge(at["hT"], g)
                            for t in range(TG):
                                last = S.activation(hp[:, t, :], x1[:, t, :], ACT.Identity, scale=rs_b[:, 1, t:t + 1], bias=nmr[:, t:t + 1])
                            last.then_inc(at["hp"], 1)

                    def hi(g):
                        if g is not None:
                            act.wait_ge(at["hT"], g + 1)
                            if has(g - 1):
                                act.wait_ge(at["pks"], g)
                                act.wait_ge(at["v"], g)
                            S.activation(hT_hi[:, 0:GT], banks[B_HT][:, :], ACT.Copy)
                            S.activation(hT_hi[:, GT:], banks[B_HT][:, 0:NN], ACT.Copy).then_inc(at["hi"], 1)

                    def vd(g):
                        if g is not None:
                            act.wait_ge(at["v"], g + 1)
                            if first(g):
                                act.wait_ge(pool_w, 5)
                            if has(g - 1):
                                act.wait_ge(at["y"], g)
                            vp = banks[B_V][:, :].rearrange("p (g k d) -> p g k d", g=GR, k=2)
                            S.activation(v_diag[0:NN, :, :, 0:32], vp[0:NN], ACT.Copy)
                            S.activation(v_diag[NN:P, 1:GR, :, 33:65], vp[NN:P, 0:GR - 1], ACT.Copy)
                            S.activation(v_diag[NN:P, 0:1, :, 33:65], vp[NN:P, GR - 1:GR], ACT.Copy).then_inc(at["vd"], 1)

                    def exp(g):
                        if g is not None:
                            act.wait_ge(at["nmax"], g + 1)
                            if has(g - 1):
                                act.wait_ge(at["prT"], g)
                            for t in range(TG):
                                for h in range(NH):
                                    last = S.activation(pr[:, t, h, :], sc[:, t, h, :], ACT.Exp, scale=SCALE,
                                                        bias=nmx[:, t * NH + h:t * NH + h + 1])
                            last.then_inc(at["exp"], 1)

                    def prTc(g):
                        if g is not None:
                            act.wait_ge(at["prT"], g + 1)
                            if has(g - 1):
                                act.wait_ge(at["y"], g)
                            for p in range(2):
                                last = S.activation(prT[:, p, :, :], banks[B_PRT[p]][:, :], ACT.Copy)
                            last.then_inc(at["prTc"], 1)

                    def yTc(g):
                        if g is not None:
                            act.wait_ge(at["yT"], g + 1)
                            if has(g - 1):
                                act.wait_ge(at["wo"], g)
                            S.activation(yT[:, :, :], banks[B_YT][:, :], ACT.Copy).then_inc(at["yTc"], 1)

                    def ssq(g):
                        if g is not None:
                            act.wait_ge(at["f2"], g + 1)
                            if has(g - 1):
                                act.wait_ge(at["ssv"], g)
                            for t in range(TG):
                                last = S.activation(junk[:, t, :], f2[:, t, :], ACT.Square, accum_out=ss[:, t:t + 1])
                            last.then_inc(at["ssq"], 1)

                    def flat_(g):
                        if g is not None:
                            act.wait_ge(at["rms"], g + 1)
                            if has(g - 1):
                                act.wait_ge(scattered, g * 16 * 2 * TG)
                                act.wait_ge(at["flatT"], g)
                            for t in range(TG):
                                last = S.activation(flat[:, t, :], f2[:, t, :], ACT.Copy, scale=rr2[:, t:t + 1])
                            last.then_inc(at["flat"], 1)

                    def flatTc(g):
                        if g is not None:
                            act.wait_ge(at["flatT"], g + 1)
                            if has(g - 1):
                                act.wait_ge(at["logits"], g)
                            S.activation(flatT[:, :, :], banks[B_FLATT][:, :], ACT.Copy).then_inc(at["flatTc"], 1)

                    def etop_(g):
                        if g is not None:
                            act.wait_ge(router.sem, router.at("dtop", g))
                            if has(g - 1):
                                act.wait_ge(at["gate"], g)
                            S.activation(etop[:, :, :], dtop[:, :, :], ACT.Exp).then_inc(at["etop"], 1)

                    def body(g):
                        prTc(g[4])
                        hp_(g[2])
                        hi(g[2])
                        tT_(g[1])
                        yTc(g[4])
                        vd(g[3])
                        etop_(g[5])
                        ssq(g[4])
                        flat_(g[4])
                        flatTc(g[4])
                        exp(g[3])
                        if first(g[4]):
                            weights_hi()
                    sweep(act, body)

                @block.vector
                def _(dve):
                    def weights():
                        dve.wait_ge(ld_w, 16 * 8)
                        V.tensor_copy(trib[:, :], cst[:, C_TRI:C_TRI + P]).then_inc(dve_w, 1)
                        V.tensor_copy(oneb[:, :], cst[:, C_ONE:C_ONE + P]).then_inc(dve_w, 1)
                        V.tensor_scalar(rws[:, :], rw[:, :], ln[:, 1:2], None, ALU.mult).then_inc(dve_w, 1)
                        V.tensor_scalar(wq_raw[:, :], wq_raw[:, :], ln[:, 0:1], None, ALU.mult).then_inc(dve_w, 1)
                        dve.wait_ge(dve_w, 4)
                        V.tensor_copy(wq_hi[:, :], wq_raw[:, :]).then_inc(dve_w, 1)
                        dve.wait_ge(dve_w, 5)
                        V.tensor_tensor(wq_lo[:, :], wq_raw[:, :], wq_hi[:, :].bitcast(f32), ALU.subtract).then_inc(dve_w, 1)

                    def held(n):
                        V.memset(spare[:, n:n + 1], 0.0)

                    def st0(g):
                        if g is not None:
                            dve.wait_ge(ld_x, g * 16 + 16)
                            for t in range(TG):
                                last = V.bn_stats(st_a[:, t, :], xt[:, t, :])
                            last.then_inc(at["st0"], 1)

                    def mv0(g):
                        if g is not None:
                            dve.wait_ge(at["st0"], g + 1)
                            held(0)
                            for t in range(TG):
                                last = V.bn_aggr(mv_a[:, t, :], st_a[:, t, :])
                            last.then_inc(at["mv0"], 1)

                    def var0(g):
                        if g is not None:
                            dve.wait_ge(at["mv0"], g + 1)
                            if has(g - 1):
                                dve.wait_ge(at["rstd0"], g)
                            V.tensor_scalar(var_a[:, :], mv_a[:, :, 1], 1e-5, None, ALU.add).then_inc(at["var0"], 1)

                    def xn_(g):
                        if g is not None:
                            dve.wait_ge(at["rstd0"], g + 1)
                            if has(g - 1):
                                dve.wait_ge(at["gnnT"], g)
                            for t in range(TG):
                                last = V.tensor_scalar(xn[:, t, :], xt[:, t, :], mv_a[:, t, 0:1], rs_a[:, t:t + 1], ALU.subtract, ALU.mult)
                            last.then_inc(at["xn"], 1)

                    def x1_(g):
                        if g is not None:
                            dve.wait_ge(at["gnn"], g + 1)
                            dve.wait_ge(at["xb"], g + 1)
                            if has(g - 1):
                                dve.wait_ge(at["base0"], g)
                                dve.wait_ge(at["hp"], g)
                            V.tensor_tensor(x1[:, :, :], banks[B_GNN][:, :].rearrange("p (t c) -> p t c", t=TG), xb[:, :, :], ALU.add).then_inc(at["x1"], 1)

                    def st1(g):
                        if g is not None:
                            dve.wait_ge(at["x1"], g + 1)
                            for t in range(TG):
                                last = V.bn_stats(st_b[:, t, :], x1[:, t, :])
                            last.then_inc(at["st1"], 1)

                    def mv1(g):
                        if g is not None:
                            dve.wait_ge(at["st1"], g + 1)
                            held(1)
                            for t in range(TG):
                                last = V.bn_aggr(mv_b[:, t, :], st_b[:, t, :])
                            last.then_inc(at["mv1"], 1)

                    def var1(g):
                        if g is not None:
                            dve.wait_ge(at["mv1"], g + 1)
                            if has(g - 1):
                                dve.wait_ge(at["rstd1"], g)
                            V.tensor_scalar(var_b[:, 0, :], mv_b[:, :, 1], 1e-5, None, ALU.add)
                            V.tensor_scalar(var_b[:, 1, :], mv_b[:, :, 1], 1.0 + 1e-6, 1e-11, ALU.mult, ALU.add).then_inc(at["var1"], 1)

                    def nmr_(g):
                        if g is not None:
                            dve.wait_ge(at["rstd1"], g + 1)
                            if has(g - 1):
                                dve.wait_ge(at["hp"], g)
                            V.scalar_tensor_tensor(nmr[:, :], mv_b[:, :, 0], -1.0, rs_b[:, 1, :], ALU.mult, ALU.mult).then_inc(at["nmr"], 1)

                    def f_(g):
                        if g is not None:
                            dve.wait_ge(at["rstd1"], g + 1)
                            for t in range(TG):
                                last = V.tensor_scalar(f_all[:, bass.ds(g * TG + t, 1), :].rearrange("p o c -> p (o c)"), x1[:, t, :],
                                                       mv_b[:, t, 0:1], rs_b[:, 0, t:t + 1], ALU.subtract, ALU.mult)
                            last.then_inc(at["f"], 1)

                    def lo(g):
                        if g is not None:
                            dve.wait_ge(at["hi"], g + 1)
                            if has(g - 1):
                                dve.wait_ge(at["pks"], g)
                                dve.wait_ge(at["v"], g)
                            V.tensor_tensor(hT_lo[:, 0:GT], banks[B_HT][:, :], hT_hi[:, 0:GT].bitcast(f32), ALU.subtract)
                            V.tensor_tensor(hT_lo[:, GT:], banks[B_HT][:, 0:NN], hT_hi[:, GT:].bitcast(f32), ALU.subtract).then_inc(at["lo"], 1)

                    def rope(g, dst, bank, col, projected, done, used):
                        if g is not None:
                            dve.wait_ge(projected, g + 1)
                            if has(g - 1):
                                dve.wait_ge(used, g)
                            V.tensor_tensor(dst[:, :].rearrange("p (g t) -> p g t", g=GR),
                                            banks[bank][:, :].rearrange("p (g t) -> p g t", g=GR),
                                            cst[:, col:col + NN].unsqueeze(1).broadcast_to([P, GR, NN]), ALU.mult).then_inc(done, 1)

                    def qc(g):
                        rope(g, q_cos, B_PQ, C_COS, at["pq"], at["qc"], at["qr"])

                    def qs(g):
                        rope(g, q_sin, B_PQS, C_SIN, at["pqs"], at["qs"], at["qr"])

                    def kc(g):
                        rope(g, k_cos, B_PK, C_COS, at["pk"], at["kc"], at["kr"])

                    def ks(g):
                        rope(g, k_sin, B_PKS, C_SIN, at["pks"], at["ks"], at["kr"])

                    def mask(g):
                        if g is not None:
                            dve.wait_ge(at["scores"], g + 1)
                            if has(g - 1):
                                dve.wait_ge(at["exp"], g)
                            for h in range(NH):
                                last = V.tensor_tensor(sc[:, :, h, :], banks[4 + h][:, 0:TG * NN].rearrange("p (t s) -> p t s", t=TG),
                                                       cst[:, C_MASK:C_MASK + NN].unsqueeze(1).broadcast_to([P, TG, NN]), ALU.add)
                            last.then_inc(at["mask"], 1)

                    def max_(g):
                        if g is not None:
                            dve.wait_ge(at["mask"], g + 1)
                            V.reduce_max(mx[:, :], sc[:, :, :, :].rearrange("p t h s -> p (t h) s"), AX.X).then_inc(at["max"], 1)

                    def nmax(g):
                        if g is not None:
                            dve.wait_ge(at["max"], g + 1)
                            if has(g - 1):
                                dve.wait_ge(at["exp"], g)
                            V.tensor_scalar(nmx[:, :], mx[:, :], -SCALE, None, ALU.mult).then_inc(at["nmax"], 1)

                    def ys(j):
                        return banks[B_Y[j]][:, 0:264].rearrange("p (t h e) -> p t h e", t=2, h=NH)

                    def rden_(g):
                        if g is not None:
                            dve.wait_ge(at["y"], g + 1)
                            for j in range(2):
                                last = V.reciprocal(rden[:, 2 * j:2 * j + 2, :].unsqueeze(3), ys(j)[:, :, :, 32:33])
                            last.then_inc(at["rden"], 1)

                    def yn_(g):
                        if g is not None:
                            dve.wait_ge(at["rden"], g + 1)
                            if has(g - 1):
                                dve.wait_ge(at["yT"], g)
                            for j in range(2):
                                last = V.tensor_tensor(yn[:, 2 * j:2 * j + 2, :].rearrange("p t (h e) -> p t h e", h=NH),
                                                       ys(j)[:, :, :, 0:32],
                                                       rden[:, 2 * j:2 * j + 2, :].unsqueeze(3).broadcast_to([P, 2, NH, HD]), ALU.mult)
                            last.then_inc(at["yn"], 1)

                    att = banks[B_WO][:, :].rearrange("p (t c) -> p t c", t=TG)

                    def f2_(g):
                        if g is not None:
                            dve.wait_ge(at["wo"], g + 1)
                            dve.wait_ge(at["f"], g + 1)
                            if has(g - 1):
                                dve.wait_ge(at["flat"], g)
                            V.tensor_tensor(f2[:, :, :], att, f_all[:, bass.ds(g * TG, TG), :], ALU.add).then_inc(at["f2"], 1)

                    def base1(g):
                        if g is not None:
                            dve.wait_ge(at["wo"], g + 1)
                            dve.wait_ge(at["base0"], g + 1)
                            V.tensor_tensor(base_all[:, bass.ds(g * TG, TG), :], att, base_all[:, bass.ds(g * TG, TG), :], ALU.add).then_inc(at["base1"], 1)

                    def ssv_(g):
                        if g is not None:
                            dve.wait_ge(at["ssq"], g + 1)
                            if has(g - 1):
                                dve.wait_ge(at["rms"], g)
                            V.tensor_scalar(ssv[:, :], ss[:, :], 1.0 / C, 1e-6, ALU.mult, ALU.add).then_inc(at["ssv"], 1)

                    def lg_(g):
                        if g is not None:
                            dve.wait_ge(at["logits"], g + 1)
                            V.tensor_copy(lg[:, :, :], banks[B_LOGITS][:, 0:TG * 8].rearrange("p (t e) -> p t e", t=TG)).then_inc(router.sem, 1)

                    def top_(g):
                        if g is not None:
                            dve.wait_ge(router.sem, router.at("lg", g))
                            held(2)
                            for t in range(TG):
                                last = V.max(top[:, t, :], lg[:, t, :])
                            last.then_inc(router.sem, 1)

                    def topi_(g):
                        if g is not None:
                            dve.wait_ge(router.sem, router.at("top", g))
                            held(3)
                            for t in range(TG):
                                last = V.max_index(topi[:, t, :], top[:, t, :], lg[:, t, :])
                            last.then_inc(router.sem, 1)

                    def topf_(g):
                        if g is not None:
                            dve.wait_ge(router.sem, router.at("topi", g))
                            V.tensor_copy(topf[:, :, :], topi[:, :, 0:2]).then_inc(router.sem, 1)

                    def oh_(g):
                        if g is not None:
                            dve.wait_ge(router.sem, router.at("topf", g))
                            V.tensor_tensor(oh[:, :, :, :], topf[:, :, :].unsqueeze(3).broadcast_to([P, TG, 2, 8]),
                                            iota8.unsqueeze(1).unsqueeze(1).broadcast_to([P, TG, 2, 8]), ALU.is_equal).then_inc(router.sem, 1)

                    def sel_(g):
                        if g is not None:
                            dve.wait_ge(router.sem, router.at("oh", g))
                            if has(g - 1):
                                dve.wait_ge(at["rank"], g)
                            V.tensor_tensor(sel[:, :, :], oh[:, :, 0, :], oh[:, :, 1, :], ALU.add).then_inc(router.sem, 1)

                    def carb(g):
                        if g is not None:
                            if first(g):
                                dve.wait_ge(pool_w, 3)
                            if has(g - 1):
                                dve.wait_ge(router.sem, router.at("car", g - 1))
                                dve.wait_ge(at["rank"], g)
                            V.tensor_copy(carry_b[:, :], carry[:, :]).then_inc(router.sem, 1)

                    def ssum(g):
                        if g is not None:
                            dve.wait_ge(router.sem, router.at("sel", g))
                            V.reduce_sum(selsum[:, :], sel[:, :, :].rearrange("p t e -> p e t"), AX.X).then_inc(router.sem, 1)

                    def car(g):
                        if g is not None:
                            dve.wait_ge(router.sem, router.at("carb", g))
                            dve.wait_ge(router.sem, router.at("ssum", g))
                            V.tensor_tensor(carry[:, :], carry[:, :], selsum[:, :], ALU.add).then_inc(router.sem, 1)

                    def dtop_(g):
                        if g is not None:
                            dve.wait_ge(router.sem, router.at("top", g))
                            if has(g - 1):
                                dve.wait_ge(at["etop"], g)
                            V.tensor_tensor(dtop[:, :, :], top[:, :, :], top[:, :, 0:1].broadcast_to([P, TG, 8]), ALU.subtract).then_inc(router.sem, 1)

                    def z_(g):
                        if g is not None:
                            dve.wait_ge(at["etop"], g + 1)
                            V.reduce_sum(z[:, :], etop[:, :, :], AX.X)
                            V.tensor_tensor(s2[:, :], etop[:, :, 0], etop[:, :, 1], ALU.add).then_inc(at["z"], 1)

                    def den_(g):
                        if g is not None:
                            dve.wait_ge(at["z"], g + 1)
                            V.scalar_tensor_tensor(den[:, :], z[:, :], 1e-9, s2[:, :], ALU.mult, ALU.add).then_inc(at["den"], 1)

                    def rec_(g):
                        if g is not None:
                            dve.wait_ge(at["den"], g + 1)
                            V.reciprocal(rec[:, :], den[:, :]).then_inc(at["rec"], 1)

                    def gate(g):
                        if g is not None:
                            dve.wait_ge(at["rec"], g + 1)
                            V.tensor_tensor(gates_all[:, bass.ds(g, 1), :].rearrange("p o (t k) -> p (o t) k", k=2), etop[:, :, 0:2],
                                            rec[:, :].unsqueeze(2).broadcast_to([P, TG, 2]), ALU.mult).then_inc(at["gate"], 1)

                    def rk(g):
                        if g is not None:
                            dve.wait_ge(at["rank"], g + 1)
                            V.tensor_tensor(rank[:, :, :], banks[B_RANK][:, 0:TG * 8].rearrange("p (t e) -> p t e", t=TG),
                                            cst[:, C_BASE:C_BASE + 8].unsqueeze(1).broadcast_to([P, TG, 8]), ALU.add).then_inc(router.sem, 1)

                    def ohr_(g):
                        if g is not None:
                            dve.wait_ge(router.sem, router.at("rk", g))
                            V.tensor_tensor(ohr[:, :, :, :], oh[:, :, :, :], rank[:, :, :].unsqueeze(2).broadcast_to([P, TG, 2, 8]), ALU.mult).then_inc(router.sem, 1)

                    def slotf_(g):
                        if g is not None:
                            dve.wait_ge(router.sem, router.at("ohr", g))
                            V.reduce_sum(slotf[:, :], ohr[:, :, :, :].rearrange("p t k e -> p (t k) e"), AX.X).then_inc(router.sem, 1)

                    def slot(g):
                        if g is not None:
                            dve.wait_ge(router.sem, router.at("slotf", g))
                            if has(g - 1):
                                dve.wait_ge(scattered, g * 16 * 2 * TG)
                            V.tensor_copy(slot_now[:, :], slotf[:, :]).then_inc(router.sem, 1)
                            V.tensor_copy(slots_f[:, bass.ds(g, 1), :].rearrange("p o s -> p (o s)"), slotf[:, :]).then_inc(router.sem, 1)

                    def body(g):
                        z_(g[5])
                        st0(g[0])
                        ssv_(g[4])
                        mv0(g[0])
                        mask(g[3])
                        max_(g[3])
                        nmax(g[3])
                        x1_(g[1])
                        lg_(g[4])
                        var0(g[0])
                        top_(g[4])
                        topi_(g[4])
                        den_(g[5])
                        topf_(g[4])
                        kc(g[2])
                        oh_(g[4])
                        ks(g[2])
                        carb(g[4])
                        sel_(g[4])
                        st1(g[1])
                        ssum(g[4])
                        mv1(g[1])
                        rk(g[4])
                        var1(g[1])
                        ohr_(g[4])
                        slotf_(g[4])
                        slot(g[4])
                        qc(g[2])
                        nmr_(g[1])
                        xn_(g[0])
                        qs(g[2])
                        rden_(g[3])
                        yn_(g[3])
                        dtop_(g[4])
                        f_(g[1])
                        rec_(g[5])
                        car(g[4])
                        lo(g[1])
                        gate(g[5])
                        f2_(g[3])
                        base1(g[3])
                        if first(g[0]):
                            weights()
                    sweep(dve, body)

                    n = [0]

                    def link(ins):
                        n[0] += 1
                        ins.then_inc(dve_t, 1)
                        dve.wait_ge(dve_t, n[0])

                    dve.wait_ge(router.sem, router.at("keep", NG - 1))
                    link(V.tensor_copy(carry_b[:, :], carry[:, :]))
                    dve.wait_ge(pe_t, 1)
                    link(V.tensor_scalar(cnti[:, :], banks[0][:, 0:8], float(P - 1), None, ALU.add))
                    link(V.tensor_tensor(fill[:, :], banks[0][0:1, 0:8], cst[0:1, C_BASE:C_BASE + 8], ALU.add))
                    link(V.tensor_scalar(cnti[:, :], cnti[:, :], 7, None, ALU.arith_shift_right))
                    link(V.tensor_copy(nblk[:, :], cnti[:, :]))
                    link(V.tensor_tensor(tri_nb[:, :, :], nblk[0:1, :].unsqueeze(1).broadcast_to([1, 8, 8]),
                                         cst[0:1, C_TRI8:C_TRI8 + 64].rearrange("p (a b) -> p a b", a=8), ALU.mult))
                    link(V.reduce_sum(cum[:, :], tri_nb[:, :, :], AX.X))
                    link(V.tensor_tensor(past[:, :, :], cst[0:1, C_BLK:C_BLK + NBLK].unsqueeze(2).broadcast_to([1, NBLK, 8]),
                                         cum[:, :].unsqueeze(1).broadcast_to([1, NBLK, 8]), ALU.is_ge))
                    link(V.tensor_tensor(pastn[:, :, :], past[:, :, :], nblk[0:1, :].unsqueeze(1).broadcast_to([1, NBLK, 8]), ALU.mult))
                    link(V.reduce_sum(bexp[:, :], past[:, :, :], AX.X))
                    link(V.reduce_sum(bprev[:, :], pastn[:, :, :], AX.X))
                    link(V.tensor_tensor(brow[:, :], cst[0:1, C_BLK:C_BLK + NBLK], bprev[:, :], ALU.subtract))
                    link(V.scalar_tensor_tensor(brow[:, :], bexp[:, :], float(REG), brow[:, :], ALU.mult, ALU.add))
                    link(V.tensor_scalar(table[:, 1, :], brow[:, :], float(P), None, ALU.mult))
                    link(V.tensor_scalar(table[:, 0, :], bexp[:, :], float(NE0 - 1), None, ALU.min))
                    link(V.tensor_scalar(gaps[:, :], nblk[:, :], -float(REG), float(P), ALU.add, ALU.mult))
                    slots = slots_f[:, :, :].rearrange("p g s -> p (g s)")
                    link(V.tensor_tensor(gap[:, :, :], slots.unsqueeze(2).broadcast_to([P, NG * 2 * TG, 7]),
                                         cst[:, C_BASE + 1:C_BASE + 8].unsqueeze(1).broadcast_to([P, NG * 2 * TG, 7]), ALU.is_ge))
                    link(V.tensor_tensor(gap[:, :, :], gap[:, :, :], gaps[:, 0:7].unsqueeze(1).broadcast_to([P, NG * 2 * TG, 7]), ALU.mult))
                    link(V.reduce_sum(back[:, :], gap[:, :, :], AX.X))
                    link(V.tensor_tensor(slots_all[:, :, :].rearrange("p g s -> p (g s)"), slots, back[:, :], ALU.add))
                @block.tensor
                def _(pe):
                    def gnnT(g):
                        if g is not None:
                            pe.wait_ge(ld_adj, g * 32 + 32)
                            pe.wait_ge(at["xn"], g + 1)
                            if exists(g - 1):
                                pe.wait_ge(at["x1"], g)
                            elif exists(g - 4):
                                pe.wait_ge(at["f2"], g - 3)
                                pe.wait_ge(at["base1"], g - 3)
                            for t in range(TG):
                                last = T.matmul(banks[B_GNNT][:, t * P:(t + 1) * P], xn[:, t, :], adjt[:, t, :], start=True, stop=True)
                            last.then_inc(at["gnnT"], 1)

                    def gnn(g):
                        if g is not None:
                            if first(g):
                                pe.wait_ge(ld_w, 16 * 8)
                            pe.wait_ge(at["tT"], g + 1)
                            if exists(g - 3):
                                pe.wait_ge(at["f2"], g - 2)
                                pe.wait_ge(at["base1"], g - 2)
                            elif exists(g):
                                pass
                            for t in range(TG):
                                last = T.matmul(banks[B_GNN][:, t * P:(t + 1) * P], tT[:, t, :], gw[:, :], start=True, stop=True)
                            last.then_inc(at["gnn"], 1)

                    def hT(g):
                        if g is not None:
                            pe.wait_ge(at["hp"], g + 1)
                            if exists(g - 1):
                                pe.wait_ge(at["qc"], g)
                            for t in range(TG):
                                last = T.transpose(banks[B_HT][:, t * P:(t + 1) * P], hp[:, t, :], ident)
                            last.then_inc(at["hT"], 1)

                    def project(g, n, bank, done):
                        for q, (w, h) in enumerate(((wq_hi, hT_hi), (wq_hi, hT_lo), (wq_lo, hT_hi))):
                            last = T.matmul(banks[bank][:, :], w[:, n * P:(n + 1) * P], h[:, 0:GT], start=q == 0, stop=q == 2)
                        last.then_inc(done, 1)

                    def pq(g):
                        if g is not None:
                            pe.wait_ge(at["lo"], g + 1)
                            if first(g):
                                pe.wait_ge(dve_w, 6)
                            if exists(g):
                                pe.wait_ge(at["hi"], g + 1)
                            project(g, 0, B_PQ, at["pq"])

                    def pqs(g):
                        if g is not None:
                            pe.wait_ge(at["lo"], g + 1)
                            if first(g):
                                pe.wait_ge(dve_w, 6)
                            if exists(g):
                                pe.wait_ge(at["kc"], g + 1)
                            project(g, 1, B_PQS, at["pqs"])

                    def pk(g):
                        if g is not None:
                            pe.wait_ge(at["lo"], g + 1)
                            if first(g):
                                pe.wait_ge(dve_w, 6)
                            if exists(g - 1):
                                pe.wait_ge(at["mask"], g)
                            project(g, 2, B_PK, at["pk"])

                    def pks(g):
                        if g is not None:
                            pe.wait_ge(at["lo"], g + 1)
                            if first(g):
                                pe.wait_ge(dve_w, 6)
                            if exists(g - 1):
                                pe.wait_ge(at["mask"], g)
                            elif exists(g - 2):
                                pe.wait_ge(at["yTc"], g - 1)
                            project(g, 3, B_PKS, at["pks"])

                    def v(g):
                        if g is not None:
                            pe.wait_ge(at["lo"], g + 1)
                            if first(g):
                                pe.wait_ge(dve_w, 6)
                            if exists(g - 1):
                                pe.wait_ge(at["vd"], g)
                            for gr in range(GR):
                                for q, (h, w) in enumerate(((hT_hi, wq_hi), (hT_hi, wq_lo), (hT_lo, wq_hi))):
                                    last = T.matmul(banks[B_V][:, gr * NN:(gr + 1) * NN], h[:, gr * NN:gr * NN + P],
                                                    w[:, 512:576], start=q == 0, stop=q == 2)
                            last.then_inc(at["v"], 1)

                    def scores(g):
                        if g is not None:
                            pe.wait_ge(at["qr"], g + 1)
                            pe.wait_ge(at["kr"], g + 1)
                            if exists(g - 1):
                                pe.wait_ge(at["rden"], g)
                                pe.wait_ge(at["yn"], g)
                            if exists(g - 1):
                                pe.wait_ge(at["rden"], g)
                                pe.wait_ge(at["yn"], g)
                            elif exists(g - 2):
                                pe.wait_ge(router.sem, router.at("lg", g - 2))
                            if exists(g - 1):
                                pe.wait_ge(at["yTc"], g)
                            elif exists(g):
                                pe.wait_ge(at["ks"], g + 1)
                            if exists(g):
                                pe.wait_ge(at["qs"], g + 1)
                            for t in range(TG):
                                for gi in range(2):
                                    tok = slice(t * P + gi * NN, t * P + (gi + 1) * NN)
                                    for h in range(NH):
                                        hs = slice(h * HD, (h + 1) * HD)
                                        last = T.matmul(banks[4 + h][gi * NN:(gi + 1) * NN, t * NN:(t + 1) * NN],
                                                        q_rot[hs, tok], k_rot[hs, tok], start=True, stop=True)
                            last.then_inc(at["scores"], 1)

                    def prT_(g):
                        if g is not None:
                            pe.wait_ge(at["exp"], g + 1)
                            if exists(g):
                                pe.wait_ge(at["mask"], g + 1)
                            if exists(g - 1):
                                pe.wait_ge(router.sem, router.at("lg", g - 1))
                            elif exists(g):
                                pe.wait_ge(at["mask"], g + 1)
                            for p in range(2):
                                for t in range(TG):
                                    last = T.transpose(banks[B_PRT[p]][:, t * P:(t + 1) * P],
                                                       pr[:, t, 2 * p:2 * p + 2, :].rearrange("p h s -> p (h s)"), ident)
                            last.then_inc(at["prT"], 1)

                    def y(g):
                        if g is not None:
                            pe.wait_ge(at["prTc"], g + 1)
                            pe.wait_ge(at["vd"], g + 1)
                            for t in range(TG):
                                for gi in range(2):
                                    for p in range(2):
                                        last = T.matmul(banks[B_Y[t // 2]][gi * NN:(gi + 1) * NN, (t % 2) * 132 + p * 66:(t % 2) * 132 + p * 66 + 66],
                                                        prT[:, p, t, gi * NN:(gi + 1) * NN], v_diag[:, 2 * t + gi, p, :],
                                                        start=True, stop=True)
                            last.then_inc(at["y"], 1)

                    def yT_(g):
                        if g is not None:
                            pe.wait_ge(at["yn"], g + 1)
                            if exists(g + 1):
                                pe.wait_ge(at["ks"], g + 2)
                            elif exists(g):
                                pe.wait_ge(at["mask"], g + 1)
                            for t in range(TG):
                                last = T.transpose(banks[B_YT][:, t * P:(t + 1) * P], yn[:, t, :], ident)
                            last.then_inc(at["yT"], 1)

                    def wo_(g):
                        if g is not None:
                            pe.wait_ge(at["yTc"], g + 1)
                            if exists(g + 3):
                                pe.wait_ge(at["tT"], g + 4)
                            elif exists(g + 2):
                                pe.wait_ge(at["x1"], g + 3)
                            elif exists(g - 1):
                                pe.wait_ge(at["f2"], g)
                                pe.wait_ge(at["base1"], g)
                            for t in range(TG):
                                last = T.matmul(banks[B_WO][:, t * P:(t + 1) * P], yT[:, t, :], wo_sb[:, :], start=True, stop=True)
                            last.then_inc(at["wo"], 1)

                    def flatT_(g):
                        if g is not None:
                            pe.wait_ge(at["flat"], g + 1)
                            if exists(g + 1):
                                pe.wait_ge(at["mask"], g + 2)
                            elif exists(g):
                                pe.wait_ge(at["rden"], g + 1)
                                pe.wait_ge(at["yn"], g + 1)
                            for t in range(TG):
                                last = T.transpose(banks[B_FLATT][:, t * P:(t + 1) * P], flat[:, t, :], ident)
                            last.then_inc(at["flatT"], 1)

                    def logits(g):
                        if g is not None:
                            pe.wait_ge(at["flatTc"], g + 1)
                            for t in range(TG):
                                last = T.matmul(banks[B_LOGITS][:, t * 8:t * 8 + 8], flatT[:, t, :], rws[:, :], start=True, stop=True)
                            last.then_inc(at["logits"], 1)

                    def rank(g):
                        if g is not None:
                            pe.wait_ge(router.sem, router.at("sel", g))
                            pe.wait_ge(router.sem, router.at("carb", g))
                            if exists(g - 1):
                                pe.wait_ge(router.sem, router.at("rk", g - 1))
                            bank = banks[B_RANK]
                            T.matmul(bank[:, 0:TG * 8], trib[:, :], sel[:, :, :].rearrange("p t e -> p (t e)"), start=True, stop=False)
                            T.matmul(bank[:, 0:TG * 8], oneb[:, :], carry_b[:, :].unsqueeze(1).broadcast_to([P, TG, 8]), start=False, stop=False)
                            for t in range(TG - 1):
                                last = T.matmul(bank[:, (t + 1) * 8:TG * 8], oneb[:, :],
                                                sel[:, t:t + 1, :].broadcast_to([P, TG - 1 - t, 8]), start=False, stop=t == TG - 2)
                            last.then_inc(at["rank"], 1)

                    def body(g):
                        scores(g[3])
                        gnn(g[1])
                        pq(g[2])
                        flatT_(g[4])
                        pk(g[2])
                        logits(g[4])
                        pks(g[2])
                        v(g[2])
                        rank(g[4])
                        prT_(g[3])
                        pqs(g[2])
                        y(g[3])
                        hT(g[1])
                        gnnT(g[0])
                        yT_(g[3])
                        wo_(g[3])
                    sweep(pe, body)
                    pe.wait_ge(dve_t, 1)
                    T.matmul(banks[0][:, 0:8], oneb[:, :], carry_b[:, :], start=True, stop=True).then_inc(pe_t, 1)

        with ExitStack() as ctx:
            sb, sem = sb_in(ctx), sem_in(ctx)
            xs, ys = sb("xs", [P, 4, C]), sb("ys", [P, 4, C])
            xT_hi, xT_lo = sb("xT_hi", [P, 2, P], f32r), sb("xT_lo", [P, 2, P], f32r)
            act1, prod = sb("act1", [P, 2, HIDP]), sb("prod", [P, 2, KC * P])
            prodT = sb("prodT", [P, 2, KC * P])
            ld = [sem(f"ld_slots{u}") for u in range(4)]
            st = [sem(f"st_slots{u}") for u in range(4)]
            padded = sem("padded")
            pt = [sem(n) for n in ("pe_xT", "pe_h", "pe_prodT", "pe_y")]
            xT_done, h_done, prodT_done, y_done = pt
            hi_done, silu_done, prodT_copied = sem("hi_done"), sem("silu_done"), sem("prodT_copied")
            lo_done, prod_done, y_copied = sem("lo_done"), sem("prod_done"), sem("y_copied")

            def quarter(k, u):
                return (k // 4 + 1) * 16 if isinstance(k, int) else (k - u) * 4 + 16

            def blocks(engine, body, skew):
                for k in range(8):
                    body(k, k % 4)
                with engine.Fori(2, NBLK // 4) as j:
                    for u in range(4):
                        body(j * 4 + u, u)
                for k in range(NBLK, NBLK + skew):
                    body(k, k % 4)

            def live(k, back):
                return not isinstance(k, int) or 0 <= k - back < NBLK

            def live_prior(k, back):
                return not isinstance(k, int) or k - back >= 0

            with nc.Block() as block:
                @block.sync
                def _(sp):
                    def row_of(k):
                        return sp.value_load(table[0:1, 1, bass.ds(k, 1)], min_val=0, max_val=ROWS - P)

                    def body(k, u):
                        if live(k, 0):
                            row = row_of(k)
                            if live_prior(k, 4):
                                sp.wait_ge(xT_done, k - 3)
                            sp.dma_start(xs[:, u, :], slots_in[bass.ds(row, P), :]).then_inc(ld[u], 16)
                        if live(k, 8):
                            sp.wait_ge(y_copied, k - 7)
                            sp.dma_start(slots_out[bass.ds((k - 8) * P, P), :], ys[:, u, :]).then_inc(st[u], 16)
                    blocks(sp, body, 8)
                    for u in range(4):
                        sp.wait_ge(st[u], NBLK // 4 * 16)

                @block.gpsimd
                def _(pool):
                    G.memset(prod[:, :, :], 0.0).then_inc(padded, 1)

                @block.scalar
                def _(act):
                    S.preload_act_table(ACT.Silu)

                    def body(k, u):
                        if live(k, 2):
                            act.wait_ge(h_done, k - 1)
                            if live_prior(k, 4):
                                act.wait_ge(prod_done, k - 3)
                            S.activation(act1[:, u % 2, :], banks[1 + u % 2][:, 0:HIDP], ACT.Silu).then_inc(silu_done, 1)
                        if live(k, 3):
                            act.wait_ge(prodT_done, k - 2)
                            if live_prior(k, 5):
                                act.wait_ge(y_done, k - 4)
                            S.activation(prodT[:, (u - 3) % 2, :], banks[5 + (u - 3) % 2][:, 0:KC * P], ACT.Copy).then_inc(prodT_copied, 1)
                        if live(k, 0):
                            act.wait_ge(xT_done, k + 1)
                            if live_prior(k, 2):
                                act.wait_ge(h_done, k - 1)
                            S.activation(xT_hi[:, u % 2, :], banks[0][:, 0:P], ACT.Copy).then_inc(hi_done, 1)
                    blocks(act, body, 3)

                @block.vector
                def _(dve):
                    dve.wait_ge(padded, 1)

                    def body(k, u):
                        if live(k, 1):
                            dve.wait_ge(hi_done, k)
                            if live_prior(k, 3):
                                dve.wait_ge(h_done, k - 2)
                            V.tensor_tensor(xT_lo[:, (u - 1) % 2, :], banks[0][:, 0:P], xT_hi[:, (u - 1) % 2, :].bitcast(f32), ALU.subtract).then_inc(lo_done, 1)
                        if live(k, 2):
                            dve.wait_ge(silu_done, k - 1)
                            if live_prior(k, 4):
                                dve.wait_ge(prodT_done, k - 3)
                            V.tensor_tensor(prod[:, u % 2, 0:HIDP], banks[3 + u % 2][:, 0:HIDP], act1[:, u % 2, :],
                                            ALU.mult).then_inc(prod_done, 1)
                        if live(k, 4):
                            dve.wait_ge(y_done, k - 3)
                            if live_prior(k, 8):
                                dve.wait_ge(st[u], quarter(k - 8, u))
                            V.tensor_copy(ys[:, u, :], banks[7][:, 0:C]).then_inc(y_copied, 1)
                    blocks(dve, body, 4)

                @block.tensor
                def _(pe):
                    def expert(k):
                        return pe.value_load(table[0:1, 0, bass.ds(k, 1)], min_val=0, max_val=NE0 - 1)

                    def body(k, u):
                        if live(k, 4):
                            e = expert(k - 4)
                            pe.wait_ge(prodT_copied, k - 3)
                            if live_prior(k, 5):
                                pe.wait_ge(y_copied, k - 4)
                            for n in range(KC):
                                last = T.matmul(banks[7][:, 0:C], prodT[:, u % 2, n * P:(n + 1) * P],
                                                w2_sb[:, bass.ds(e * (KC * C) + n * C, C)], start=n == 0, stop=n == KC - 1)
                            last.then_inc(y_done, 1)
                        if live(k, 0):
                            pe.wait_ge(ld[u], quarter(k, u))
                            if live_prior(k, 1):
                                pe.wait_ge(lo_done, k)
                            T.transpose(banks[0][:, 0:P], xs[:, u, :], ident).then_inc(xT_done, 1)
                        if live(k, 1):
                            e, par = expert(k - 1), (u - 1) % 2
                            pe.wait_ge(lo_done, k)
                            if live_prior(k, 3):
                                pe.wait_ge(prod_done, k - 2)
                            for n in range(2):
                                for q, (xx, ww) in enumerate(((xT_hi, w13_hi), (xT_hi, w13_lo), (xT_lo, w13_hi))):
                                    last = T.matmul(banks[1 + 2 * n + par][:, 0:HIDP], xx[:, par, :],
                                                    ww[:, bass.ds(e * (2 * HIDP) + n * HIDP, HIDP)], start=q == 0, stop=q == 2)
                            last.then_inc(h_done, 1)
                        if live(k, 2):
                            pe.wait_ge(prod_done, k - 1)
                            if live_prior(k, 4):
                                pe.wait_ge(prodT_copied, k - 3)
                            for n in range(KC):
                                last = T.transpose(banks[5 + u % 2][:, n * P:(n + 1) * P], prod[:, u % 2, n * P:(n + 1) * P], ident)
                            last.then_inc(prodT_done, 1)
                    blocks(pe, body, 4)

        with ExitStack() as ctx:
            sb, sem = sb_in(ctx), sem_in(ctx)
            gw, gb = sb("gw1", [P, C]), sb("gb1", [P, C])
            rw1, rw1_hi, rw1_lo = sb("rw1", [P, RH]), sb("rw1_hi", [P, RH], f32r), sb("rw1_lo", [P, RH], f32r)
            rb1, rw2, rb2 = sb("rb1", [RH, 1]), sb("rw2", [RH, 8]), sb("rb2", [P, 8])
            ew1_hi, ew1_lo = sb("ew1_hi", [P, NE1 * C], f32r), sb("ew1_lo", [P, NE1 * C], f32r)
            ew1, ew2, ew3 = (sb(n, [P, NE1 * C]) for n in ("ew1", "ew2", "ew3"))
            eb1, eb2, eb3 = sb("eb1", [P, NE1]), sb("eb2", [P, NE1]), sb("eb3", [NE1, C])
            mhalf = sb("mhalf1", [P, TG])
            adjt = [sb(f"adjt_c{i}", [P, TG, C]) for i in range(2)]
            rows = [sb(f"expert_rows{i}", [P, 2 * TG, C]) for i in range(2)]
            slot_now = [sb(f"slot_c{i}", [P, 2 * TG], u32) for i in range(2)]
            gate_now = [sb(f"gate_c{i}", [P, 2 * TG]) for i in range(2)]
            deg = [sb(f"deg{i}", [P, TG]) for i in range(2)]
            f3_hi = [sb(f"f3_hi{i}", [P, GT], f32r) for i in range(2)]
            f3_lo = [sb(f"f3_lo{i}", [P, GT], f32r) for i in range(2)]
            gateT = [sb(f"gateT{i}", [8, GT]) for i in range(2)]
            gate_bc = [sb(f"gate_bc{i}", [P, NE1, GT]) for i in range(2)]
            x2a, x2, xn, xb, tT, f3, ob = (sb(n, [P, TG, C]) for n in ("x2a", "x2", "xn_c", "xb_c", "tT_c", "f3", "ob"))
            degv, dscale, xscale = sb("degv", [P, TG]), sb("dscale", [P, TG]), sb("xscale", [P, TG])
            st_a, mv_a, var_a, rs_a = sb("st_c", [P, TG, 6]), sb("mv_c", [P, TG, 2]), sb("var_c", [P, TG]), sb("rs_c", [P, TG])
            st_b, mv_b, var_b, rs_b = sb("st_d", [P, TG, 6]), sb("mv_d", [P, TG, 2]), sb("var_d", [P, TG]), sb("rs_d", [P, TG])
            rhT = sb("rhT", [RH, GT])
            lg, top, topi = sb("lg_c", [P, TG, 8]), sb("top_c", [P, TG, 8]), sb("topi_c", [P, TG, 8], u32)
            topf, oh, dtop, etop = sb("topf_c", [P, TG, 2]), sb("oh_c", [P, TG, 2, 8]), sb("dtop_c", [P, TG, 8]), sb("etop_c", [P, TG, 8])
            z, zr, pk, dp, ep, e1 = sb("z_c", [P, TG]), sb("zr", [P, TG]), sb("pk", [P, TG, 2]), sb("dp", [P, TG]), sb("ep", [P, TG]), sb("e1", [P, TG])
            rk, ohr, gate = sb("rk", [P, TG, 2]), sb("ohr_c", [P, TG, 2, 8]), sb("gate", [P, TG, 8])
            h1 = [sb(f"h1_{i}", [P, GT]) for i in range(2)]
            h2 = [sb(f"h2_{i}", [P, GT]) for i in range(2)]
            h2g = [sb(f"h2g_{i}", [P, GT]) for i in range(2)]
            oT = sb("oT", [P, GT])
            spare, spare2 = sb("spare_c", [P, 1]), sb("spare_d", [P, 8])

            ld_w, ld_adj = sem("ld_w1"), [sem(f"ld_adj_c{i}") for i in range(2)]
            zeroed, dve_w = sem("zeroed1"), sem("dve_w1")
            gathered = [sem(f"gathered{i}") for i in range(2)]
            gates_loaded = [sem(f"gates_loaded{i}") for i in range(2)]
            gates_stored, stored = sem("gates_stored"), sem("stored")
            NW = 12
            B_DEG, B_AT, B_GNN, B_F3T, B_RH, B_LOGITS, B_GATET, B_OT = 5, 7, 7, 6, 5, 6, 6, 5
            DEEP = 6
            EVEN = DEEP + DEEP % 2
            at = signals(sem, "pick held add0 add1 st0 mv0 var0 rstd0 deg degv degp scale xn xb aT tT gnn x3 "
                              "st1 mv1 var1 rstd1 f3 f3T hi lo rh rhr logits "
                              "etop ep gateT gTc oTc oT ob")
            per = signals(sem, "a ra b rb m c")
            router = Steps(sem("router"), "lg top dtop topi z zr pk topf dp e1 rk0 oh rk1 ohr gate")

            def sweep(engine, body):
                def step(i, u):
                    g = [i - k for k in range(DEEP + 1)]
                    if isinstance(i, int):
                        g = [n if 0 <= n < NG else None for n in g]
                    body(g, [(u - k) % 2 for k in range(DEEP + 1)])
                for i in range(EVEN):
                    step(i, i)
                with engine.Fori(EVEN // 2, NG // 2) as j:
                    for u in range(2):
                        step(j * 2 + u, u)
                for i in range(NG, NG + DEEP):
                    step(i, i)

            def pair(g, p):
                return (g // 2 + 1) * 16 if isinstance(g, int) else (g - p) * 8 + 16

            def stream(g, t):
                return base_all[:, bass.ds(g * TG + t, 1), :].rearrange("p o c -> p (o c)")

            with nc.Block() as block:
                @block.sync
                def _(sp):
                    for dst, src in ((gw[:, :], gnn1_w), (gb[:, :], gnn1_b.partition_broadcast(P)), (rw1[:, :], r1_w1),
                                     (rb1[:, :], r1_b1), (rw2[:, :], r1_w2), (ew1[:, :], e_w1), (ew2[:, :], e_w2), (ew3[:, :], e_w3),
                                     (eb1[:, :], e_b1), (eb2[:, :], e_b2), (eb3[:, :], e_b3)):
                        sp.dma_start(dst, src).then_inc(ld_w, 16)
                    sp.wait_ge(zeroed, 4)
                    sp.dma_start(rb2[:, 0:NE1], r1_b2.partition_broadcast(P)).then_inc(ld_w, 16)

                    def lda(g, p):
                        if g is not None:
                            if has(g - 2):
                                sp.wait_ge(at["aT"], g - 1)
                                sp.wait_ge(at["deg"], g - 1)
                            src = adj_t[bass.ds(g * GT, GT), :].rearrange("(t b m) n -> b m t n", b=2, m=NN)
                            for k in range(2):
                                sp.dma_start(adjt[p][k * NN:(k + 1) * NN, :, k * NN:(k + 1) * NN], src[k]).then_inc(ld_adj[p], 16)

                    def gst(g, p):
                        if g is not None:
                            sp.wait_ge(at["gTc"], g + 1)
                            if has(g - 2):
                                sp.wait_ge(per["m"], g * NE1 - NE1)
                            sp.dma_start(gates_dram[p], gateT[p][0:NE1, :]).then_inc(gates_stored, 16)

                    def gld(g, p):
                        if g is not None:
                            sp.wait_ge(gates_stored, g * 16 + 16)
                            sp.dma_start(gate_bc[p][:, :, :], gates_dram[p].partition_broadcast(P)).then_inc(gates_loaded[p], 16)

                    def store(g):
                        if g is not None:
                            sp.wait_ge(at["ob"], g + 1)
                            sp.dma_start(out[bass.ds(g * GT, GT), :].rearrange("(t p) c -> p t c", p=P), ob[:, :, :]).then_inc(stored, 16)

                    def body(g, p):
                        store(g[6])
                        lda(g[0], p[0])
                        gst(g[3], p[3])
                        gld(g[3], p[3])
                    sweep(sp, body)
                    sp.wait_ge(stored, 16 * NG)

                @block.gpsimd
                def _(pool):
                    G.memset(adjt[0][:, :, :], 0.0).then_inc(zeroed, 1)
                    G.memset(adjt[1][:, :, :], 0.0).then_inc(zeroed, 1)
                    G.memset(rb2[:, :], -1e30).then_inc(zeroed, 1)
                    G.memset(mhalf[:, :], -0.5).then_inc(zeroed, 1)
                    pool.wait_ge(zeroed, 4)

                    def gt(n, g, p):
                        if g is not None:
                            if n == 0:
                                pool.wait_ge(at["pick"], g + 1)
                                if has(g - 2):
                                    pool.wait_ge(at["add1"], g - 1)
                                if has(g - 1):
                                    pool.wait_ge(at["held"], g)
                                G.tensor_tensor(spare[:, :], mhalf[:, 0:1], mhalf[:, 0:1], ALU.add).then_inc(at["held"], 1)
                            G.indirect_dma_start(out=rows[p][:, n, :], out_offset=None, in_=slots_out,
                                                 in_offset=bass.IndirectOffsetOnAxis(ap=slot_now[p][:, n:n + 1], axis=0),
                                                 bounds_check=NBLK * P - 1).then_inc(gathered[p], 16)

                    def xb_(g):
                        if g is not None:
                            if first(g):
                                pool.wait_ge(ld_w, 16 * NW)
                            if has(g - 1):
                                pool.wait_ge(at["x3"], g)
                            pool.wait_ge(at["add1"], g + 1)
                            G.tensor_tensor(xb[:, :, :], x2[:, :, :], gb[:, :].unsqueeze(1).broadcast_to([P, TG, C]), ALU.add).then_inc(at["xb"], 1)

                    def rstd0(g):
                        if g is not None:
                            pool.wait_ge(at["var0"], g + 1)
                            if has(g - 1):
                                pool.wait_ge(at["scale"], g)
                            G.tensor_tensor(rs_a[:, :], var_a[:, :], mhalf[:, :], ALU.pow).then_inc(at["rstd0"], 1)

                    def rstd1(g):
                        if g is not None:
                            pool.wait_ge(at["var1"], g + 1)
                            if has(g - 1):
                                pool.wait_ge(at["f3"], g)
                            G.tensor_tensor(rs_b[:, :], var_b[:, :], mhalf[:, :], ALU.pow).then_inc(at["rstd1"], 1)

                    def degp(g, p):
                        if g is not None:
                            if has(g - 2):
                                pool.wait_ge(at["x3"], g - 1)
                            pool.wait_ge(at["degv"], g + 1)
                            G.tensor_tensor(deg[p][:, :], degv[:, :], mhalf[:, :], ALU.pow).then_inc(at["degp"], 1)

                    def body(g, p):
                        gt(1, g[2], p[2])
                        gt(2, g[2], p[2])
                        gt(3, g[2], p[2])
                        gt(4, g[2], p[2])
                        gt(5, g[2], p[2])
                        degp(g[3], p[3])
                        gt(6, g[2], p[2])
                        rstd0(g[3])
                        rstd1(g[4])
                        gt(7, g[2], p[2])
                        gt(0, g[1], p[1])
                        xb_(g[3])
                    sweep(pool, body)

                @block.scalar
                def _(act):
                    S.preload_act_table(ACT.Exp)
                    act.wait_ge(ld_w, 16 * NW)

                    def ra(n, g):
                        if g is not None:
                            act.wait_ge(per["a"], g * NE1 + n + 1)
                            if n >= 2 or has(g - 1):
                                act.wait_ge(per["b"], g * NE1 + n - 1)
                            S.activation(h1[n % 2][:, :], banks[n % 2][:, :], ACT.Relu, bias=eb1[:, n:n + 1]).then_inc(per["ra"], 1)

                    def rb(n, g):
                        if g is not None:
                            act.wait_ge(per["b"], g * NE1 + n + 1)
                            if n >= 2 or has(g - 1):
                                act.wait_ge(per["m"], g * NE1 + n - 1)
                            S.activation(h2[n % 2][:, :], banks[2 + n % 2][:, :], ACT.Relu, bias=eb2[:, n:n + 1]).then_inc(per["rb"], 1)

                    def tT_(g):
                        if g is not None:
                            act.wait_ge(at["aT"], g + 1)
                            if has(g - 1):
                                act.wait_ge(at["gnn"], g)
                            S.activation(tT[:, :, :], banks[B_AT][:, :], ACT.Copy).then_inc(at["tT"], 1)

                    def hi(g, p):
                        if g is not None:
                            act.wait_ge(at["f3T"], g + 1)
                            if has(g - 2):
                                act.wait_ge(per["a"], g * NE1 - NE1)
                                act.wait_ge(at["rh"], g - 1)
                            S.activation(f3_hi[p][:, :], banks[B_F3T][:, :], ACT.Copy).then_inc(at["hi"], 1)

                    def rhr(g):
                        if g is not None:
                            act.wait_ge(at["rh"], g + 1)
                            if has(g - 1):
                                act.wait_ge(at["logits"], g)
                            S.activation(rhT[:, :], banks[B_RH][0:RH, :], ACT.Relu, bias=rb1[:, :]).then_inc(at["rhr"], 1)

                    def etop_(g):
                        if g is not None:
                            act.wait_ge(router.sem, router.at("dtop", g))
                            if has(g - 1):
                                act.wait_ge(router.sem, router.at("pk", g - 1))
                            S.activation(etop[:, :, :], dtop[:, :, :], ACT.Exp).then_inc(at["etop"], 1)

                    def ep_(g):
                        if g is not None:
                            act.wait_ge(router.sem, router.at("dp", g))
                            if has(g - 1):
                                act.wait_ge(router.sem, router.at("rk1", g - 1))
                            S.activation(ep[:, :], dp[:, :], ACT.Exp).then_inc(at["ep"], 1)

                    def gTc(g, p):
                        if g is not None:
                            act.wait_ge(at["gateT"], g + 1)
                            if has(g - 2):
                                act.wait_ge(gates_stored, g * 16 - 16)
                                act.wait_ge(per["c"], g * NE1 - NE1)
                            S.activation(gateT[p][:, :], banks[B_GATET][0:8, :], ACT.Copy).then_inc(at["gTc"], 1)

                    def oTc(g):
                        if g is not None:
                            act.wait_ge(per["c"], g * NE1 + NE1)
                            if has(g - 1):
                                act.wait_ge(at["oT"], g)
                            S.activation(oT[:, :], banks[4][:, :], ACT.Copy).then_inc(at["oTc"], 1)

                    def body(g, p):
                        ra(5, g[4])
                        rb(3, g[4])
                        ra(0, g[3])
                        rb(4, g[4])
                        ra(1, g[3])
                        rb(5, g[4])
                        ep_(g[3])
                        ra(2, g[3])
                        ra(3, g[3])
                        gTc(g[3], p[3])
                        rb(0, g[3])
                        rb(1, g[3])
                        hi(g[2], p[2])
                        ra(4, g[3])
                        oTc(g[4])
                        rhr(g[2])
                        tT_(g[1])
                        rb(2, g[3])
                        etop_(g[2])
                    sweep(act, body)

                @block.vector
                def _(dve):
                    def weights():
                        dve.wait_ge(ld_w, 16 * NW)
                        for high, w in ((ew1_hi, ew1), (rw1_hi, rw1)):
                            V.tensor_copy(high[:, :], w[:, :]).then_inc(dve_w, 1)
                        dve.wait_ge(dve_w, 2)
                        for high, low, w in ((ew1_hi, ew1_lo, ew1), (rw1_hi, rw1_lo, rw1)):
                            V.tensor_tensor(low[:, :], w[:, :], high[:, :].bitcast(f32), ALU.subtract).then_inc(dve_w, 1)

                    def held(n):
                        V.memset(spare2[:, n:n + 1], 0.0)

                    def pick(g, p):
                        if g is not None:
                            if has(g - 2):
                                dve.wait_ge(gathered[p], pair(g, p) * (2 * TG) - 16 * 2 * TG)
                            V.tensor_copy(slot_now[p][:, :], slots_all[:, bass.ds(g, 1), :].rearrange("p o s -> p (o s)"))
                            V.tensor_copy(gate_now[p][:, :], gates_all[:, bass.ds(g, 1), :].rearrange("p o s -> p (o s)")).then_inc(at["pick"], 1)

                    def add0(g, p):
                        if g is not None:
                            dve.wait_ge(gathered[p], pair(g, p) * (2 * TG))
                            for t in range(TG):
                                last = V.scalar_tensor_tensor(x2a[:, t, :], rows[p][:, 2 * t, :], gate_now[p][:, 2 * t:2 * t + 1], stream(g, t), ALU.mult, ALU.add)
                            last.then_inc(at["add0"], 1)

                    def add1(g, p):
                        if g is not None:
                            dve.wait_ge(at["add0"], g + 1)
                            if has(g - 1):
                                dve.wait_ge(at["xb"], g)
                            for t in range(TG):
                                last = V.scalar_tensor_tensor(x2[:, t, :], rows[p][:, 2 * t + 1, :], gate_now[p][:, 2 * t + 1:2 * t + 2],
                                                              x2a[:, t, :], ALU.mult, ALU.add)
                            last.then_inc(at["add1"], 1)

                    def st0(g):
                        if g is not None:
                            dve.wait_ge(at["add1"], g + 1)
                            for t in range(TG):
                                last = V.bn_stats(st_a[:, t, :], x2[:, t, :])
                            last.then_inc(at["st0"], 1)

                    def mv0(g):
                        if g is not None:
                            dve.wait_ge(at["st0"], g + 1)
                            held(0)
                            for t in range(TG):
                                last = V.bn_aggr(mv_a[:, t, :], st_a[:, t, :])
                            last.then_inc(at["mv0"], 1)

                    def var0(g):
                        if g is not None:
                            dve.wait_ge(at["mv0"], g + 1)
                            if has(g - 1):
                                dve.wait_ge(at["rstd0"], g)
                            V.tensor_scalar(var_a[:, :], mv_a[:, :, 1], 1e-5, None, ALU.add).then_inc(at["var0"], 1)

                    def degv_(g):
                        if g is not None:
                            dve.wait_ge(at["deg"], g + 1)
                            if has(g - 1):
                                dve.wait_ge(at["degp"], g)
                            V.tensor_scalar(degv[:, :], banks[B_DEG][:, 0:TG], 1e-5, None, ALU.add).then_inc(at["degv"], 1)

                    def scale(g, p):
                        if g is not None:
                            dve.wait_ge(at["rstd0"], g + 1)
                            dve.wait_ge(at["degp"], g + 1)
                            V.tensor_tensor(xscale[:, :], rs_a[:, :], deg[p][:, :], ALU.mult).then_inc(at["scale"], 1)

                    def xn_(g):
                        if g is not None:
                            dve.wait_ge(at["scale"], g + 1)
                            if has(g - 1):
                                dve.wait_ge(at["aT"], g)
                            for t in range(TG):
                                last = V.tensor_scalar(xn[:, t, :], x2[:, t, :], mv_a[:, t, 0:1], xscale[:, t:t + 1], ALU.subtract, ALU.mult)
                            last.then_inc(at["xn"], 1)

                    def x3(g, p):
                        if g is not None:
                            dve.wait_ge(at["gnn"], g + 1)
                            dve.wait_ge(at["xb"], g + 1)
                            for t in range(TG):
                                last = V.scalar_tensor_tensor(stream(g, t), banks[B_GNN][:, t * P:(t + 1) * P], deg[p][:, t:t + 1], xb[:, t, :], ALU.mult, ALU.add)
                            last.then_inc(at["x3"], 1)

                    def st1(g):
                        if g is not None:
                            dve.wait_ge(at["x3"], g + 1)
                            held(1)
                            for t in range(TG):
                                last = V.bn_stats(st_b[:, t, :], stream(g, t))
                            last.then_inc(at["st1"], 1)

                    def mv1(g):
                        if g is not None:
                            dve.wait_ge(at["st1"], g + 1)
                            held(2)
                            for t in range(TG):
                                last = V.bn_aggr(mv_b[:, t, :], st_b[:, t, :])
                            last.then_inc(at["mv1"], 1)

                    def var1(g):
                        if g is not None:
                            dve.wait_ge(at["mv1"], g + 1)
                            if has(g - 1):
                                dve.wait_ge(at["rstd1"], g)
                            V.tensor_scalar(var_b[:, :], mv_b[:, :, 1], 1e-5, None, ALU.add).then_inc(at["var1"], 1)

                    def f3_(g):
                        if g is not None:
                            dve.wait_ge(at["rstd1"], g + 1)
                            if has(g - 1):
                                dve.wait_ge(at["f3T"], g)
                            for t in range(TG):
                                last = V.tensor_scalar(f3[:, t, :], stream(g, t), mv_b[:, t, 0:1], rs_b[:, t:t + 1], ALU.subtract, ALU.mult)
                            last.then_inc(at["f3"], 1)

                    def lo(g, p):
                        if g is not None:
                            dve.wait_ge(at["hi"], g + 1)
                            if has(g - 2):
                                dve.wait_ge(per["a"], g * NE1 - NE1)
                                dve.wait_ge(at["rh"], g - 1)
                            V.tensor_tensor(f3_lo[p][:, :], banks[B_F3T][:, :], f3_hi[p][:, :].bitcast(f32), ALU.subtract).then_inc(at["lo"], 1)

                    def m(n, g, p):
                        if g is not None:
                            dve.wait_ge(per["rb"], g * NE1 + n + 1)
                            if n == 0:
                                dve.wait_ge(gates_loaded[p], pair(g, p))
                            if n >= 2 or has(g - 1):
                                dve.wait_ge(per["c"], g * NE1 + n - 1)
                            V.tensor_tensor(h2g[n % 2][:, :], h2[n % 2][:, :], gate_bc[p][:, n, :], ALU.mult).then_inc(per["m"], 1)

                    def lg_(g):
                        if g is not None:
                            dve.wait_ge(at["logits"], g + 1)
                            V.tensor_tensor(lg[:, :, :], banks[B_LOGITS][:, 0:TG * 8].rearrange("p (t e) -> p t e", t=TG),
                                            rb2[:, :].unsqueeze(1).broadcast_to([P, TG, 8]), ALU.add).then_inc(router.sem, 1)

                    def top_(g):
                        if g is not None:
                            dve.wait_ge(router.sem, router.at("lg", g))
                            held(3)
                            for t in range(TG):
                                last = V.max(top[:, t, :], lg[:, t, :])
                            last.then_inc(router.sem, 1)

                    def topi_(g):
                        if g is not None:
                            dve.wait_ge(router.sem, router.at("top", g))
                            held(4)
                            for t in range(TG):
                                last = V.max_index(topi[:, t, :], top[:, t, :], lg[:, t, :])
                            last.then_inc(router.sem, 1)

                    def topf_(g):
                        if g is not None:
                            dve.wait_ge(router.sem, router.at("topi", g))
                            V.tensor_copy(topf[:, :, :], topi[:, :, 0:2]).then_inc(router.sem, 1)

                    def oh_(g):
                        if g is not None:
                            dve.wait_ge(router.sem, router.at("topf", g))
                            V.tensor_tensor(oh[:, :, :, :], topf[:, :, :].unsqueeze(3).broadcast_to([P, TG, 2, 8]),
                                            iota8.unsqueeze(1).unsqueeze(1).broadcast_to([P, TG, 2, 8]), ALU.is_equal).then_inc(router.sem, 1)

                    def dtop_(g):
                        if g is not None:
                            dve.wait_ge(router.sem, router.at("top", g))
                            if has(g - 1):
                                dve.wait_ge(at["etop"], g)
                            V.tensor_tensor(dtop[:, :, :], top[:, :, :], top[:, :, 0:1].broadcast_to([P, TG, 8]), ALU.subtract).then_inc(router.sem, 1)

                    def z_(g):
                        if g is not None:
                            dve.wait_ge(at["etop"], g + 1)
                            V.reduce_sum(z[:, :], etop[:, :, :], AX.X).then_inc(router.sem, 1)

                    def zr_(g):
                        if g is not None:
                            dve.wait_ge(router.sem, router.at("z", g))
                            V.reciprocal(zr[:, :], z[:, :]).then_inc(router.sem, 1)

                    def pk_(g):
                        if g is not None:
                            dve.wait_ge(router.sem, router.at("zr", g))
                            V.tensor_tensor(pk[:, :, :], etop[:, :, 0:2], zr[:, :].unsqueeze(2).broadcast_to([P, TG, 2]), ALU.mult).then_inc(router.sem, 1)

                    def dp_(g):
                        if g is not None:
                            dve.wait_ge(router.sem, router.at("pk", g))
                            if has(g - 1):
                                dve.wait_ge(at["ep"], g)
                            V.tensor_tensor(dp[:, :], pk[:, :, 1], pk[:, :, 0], ALU.subtract).then_inc(router.sem, 1)

                    def e1_(g):
                        if g is not None:
                            dve.wait_ge(at["ep"], g + 1)
                            V.tensor_scalar(e1[:, :], ep[:, :], 1.0, None, ALU.add).then_inc(router.sem, 1)

                    def rk0(g):
                        if g is not None:
                            dve.wait_ge(router.sem, router.at("e1", g))
                            V.reciprocal(rk[:, :, 0], e1[:, :]).then_inc(router.sem, 1)

                    def rk1(g):
                        if g is not None:
                            dve.wait_ge(router.sem, router.at("rk0", g))
                            V.tensor_tensor(rk[:, :, 1], ep[:, :], rk[:, :, 0], ALU.mult).then_inc(router.sem, 1)

                    def ohr_(g):
                        if g is not None:
                            dve.wait_ge(router.sem, router.at("rk1", g))
                            V.tensor_tensor(ohr[:, :, :, :], oh[:, :, :, :], rk[:, :, :].unsqueeze(3).broadcast_to([P, TG, 2, 8]), ALU.mult).then_inc(router.sem, 1)

                    def gate_(g):
                        if g is not None:
                            dve.wait_ge(router.sem, router.at("ohr", g))
                            if has(g - 1):
                                dve.wait_ge(at["gateT"], g)
                            V.tensor_tensor(gate[:, :, :], ohr[:, :, 0, :], ohr[:, :, 1, :], ALU.add).then_inc(router.sem, 1)

                    def ob_(g):
                        if g is not None:
                            dve.wait_ge(at["oT"], g + 1)
                            if has(g - 1):
                                dve.wait_ge(stored, g * 16)
                            V.tensor_tensor(ob[:, :, :], banks[B_OT][:, :].rearrange("p (t c) -> p t c", t=TG), base_all[:, bass.ds(g * TG, TG), :],
                                            ALU.add).then_inc(at["ob"], 1)

                    def body(g, p):
                        xn_(g[3])
                        m(5, g[6], p[6])
                        lo(g[4], p[4])
                        add0(g[2], p[2])
                        add1(g[2], p[2])
                        st0(g[2])
                        m(0, g[5], p[5])
                        lg_(g[4])
                        top_(g[4])
                        dtop_(g[4])
                        topi_(g[4])
                        ob_(g[6])
                        z_(g[4])
                        m(1, g[5], p[5])
                        zr_(g[4])
                        pk_(g[4])
                        m(2, g[5], p[5])
                        topf_(g[4])
                        x3(g[3], p[3])
                        m(3, g[5], p[5])
                        dp_(g[4])
                        mv0(g[2])
                        st1(g[3])
                        e1_(g[4])
                        mv1(g[3])
                        var0(g[2])
                        degv_(g[1])
                        rk0(g[4])
                        oh_(g[4])
                        pick(g[0], p[0])
                        rk1(g[4])
                        var1(g[3])
                        ohr_(g[4])
                        gate_(g[4])
                        scale(g[2], p[2])
                        f3_(g[3])
                        m(4, g[5], p[5])
                        if first(g[2]):
                            weights()
                    sweep(dve, body)

                @block.tensor
                def _(pe):
                    def deg_(g, p):
                        if g is not None:
                            pe.wait_ge(ld_adj[p], pair(g, p) * 2)
                            if exists(g - 5):
                                pe.wait_ge(at["ob"], g - 4)
                            elif exists(g - 3):
                                pe.wait_ge(at["rhr"], g - 2)
                            elif exists(g - 1):
                                pe.wait_ge(at["degv"], g)
                            for t in range(TG):
                                last = T.matmul(banks[B_DEG][:, t:t + 1], adjt[p][:, t, :], cst[:, C_ONE:C_ONE + 1], start=True, stop=True)
                            last.then_inc(at["deg"], 1)

                    def aT(g, p):
                        if g is not None:
                            pe.wait_ge(at["xn"], g + 1)
                            if exists(g - 1):
                                pe.wait_ge(at["x3"], g)
                            for t in range(TG):
                                last = T.matmul(banks[B_AT][:, t * P:(t + 1) * P], xn[:, t, :], adjt[p][:, t, :], start=True, stop=True)
                            last.then_inc(at["aT"], 1)

                    def gnn(g):
                        if g is not None:
                            if first(g):
                                pe.wait_ge(ld_w, 16 * NW)
                            pe.wait_ge(at["tT"], g + 1)
                            for t in range(TG):
                                last = T.matmul(banks[B_GNN][:, t * P:(t + 1) * P], tT[:, t, :], gw[:, :], start=True, stop=True)
                            last.then_inc(at["gnn"], 1)

                    def f3T(g):
                        if g is not None:
                            pe.wait_ge(at["f3"], g + 1)
                            if exists(g - 1):
                                pe.wait_ge(at["gTc"], g)
                            for t in range(TG):
                                last = T.transpose(banks[B_F3T][:, t * P:(t + 1) * P], f3[:, t, :], ident)
                            last.then_inc(at["f3T"], 1)

                    def rh(g, p):
                        if g is not None:
                            pe.wait_ge(at["lo"], g + 1)
                            if first(g):
                                pe.wait_ge(dve_w, 4)
                            if exists(g + 2):
                                pe.wait_ge(at["degv"], g + 3)
                            elif exists(g - 3):
                                pe.wait_ge(at["ob"], g - 2)
                            elif exists(g - 1):
                                pe.wait_ge(at["rhr"], g)
                            for q, (ww, ff) in enumerate(((rw1_hi, f3_hi), (rw1_hi, f3_lo), (rw1_lo, f3_hi))):
                                last = T.matmul(banks[B_RH][0:RH, :], ww[:, :], ff[p][:, :], start=q == 0, stop=q == 2)
                            last.then_inc(at["rh"], 1)

                    def logits(g):
                        if g is not None:
                            pe.wait_ge(at["rhr"], g + 1)
                            if exists(g):
                                pe.wait_ge(at["hi"], g + 1)
                                pe.wait_ge(at["lo"], g + 1)
                            for t in range(TG):
                                last = T.matmul(banks[B_LOGITS][:, t * 8:t * 8 + 8], rhT[:, t * P:(t + 1) * P], rw2[:, :], start=True, stop=True)
                            last.then_inc(at["logits"], 1)

                    def gateT_(g):
                        if g is not None:
                            pe.wait_ge(router.sem, router.at("gate", g))
                            if exists(g):
                                pe.wait_ge(router.sem, router.at("lg", g))
                            for t in range(TG):
                                last = T.transpose(banks[B_GATET][0:8, t * P:(t + 1) * P], gate[:, t, :], ident)
                            last.then_inc(at["gateT"], 1)

                    def a(n, g, p):
                        if g is not None:
                            if n == 0:
                                pe.wait_ge(at["lo"], g + 1)
                                if first(g):
                                    pe.wait_ge(dve_w, 4)
                            if n >= 2 or has(g - 1):
                                pe.wait_ge(per["ra"], g * NE1 + n - 1)
                            w = slice(n * C, (n + 1) * C)
                            for q, (ww, ff) in enumerate(((ew1_hi, f3_hi), (ew1_hi, f3_lo), (ew1_lo, f3_hi))):
                                last = T.matmul(banks[n % 2][:, :], ww[:, w], ff[p][:, :], start=q == 0, stop=q == 2)
                            last.then_inc(per["a"], 1)

                    def b(n, g):
                        if g is not None:
                            pe.wait_ge(per["ra"], g * NE1 + n + 1)
                            if n >= 2 or has(g - 1):
                                pe.wait_ge(per["rb"], g * NE1 + n - 1)
                            T.matmul(banks[2 + n % 2][:, :], ew2[:, n * C:(n + 1) * C], h1[n % 2][:, :], start=True, stop=True).then_inc(per["b"], 1)

                    def c(n, g, p):
                        if g is not None:
                            pe.wait_ge(per["m"], g * NE1 + n + 1)
                            if n == 0 and has(g - 1):
                                pe.wait_ge(at["oTc"], g)
                            last = T.matmul(banks[4][:, :], ew3[:, n * C:(n + 1) * C], h2g[n % 2][:, :], start=n == 0, stop=False)
                            if n == NE1 - 1:
                                last = T.matmul(banks[4][:, :], eb3[:, :], gateT[p][0:NE1, :], start=False, stop=True)
                            last.then_inc(per["c"], 1)

                    def oT_(g):
                        if g is not None:
                            pe.wait_ge(at["oTc"], g + 1)
                            if exists(g + 2):
                                pe.wait_ge(at["rhr"], g + 3)
                            elif exists(g + 4):
                                pe.wait_ge(at["degv"], g + 5)
                            elif exists(g - 1):
                                pe.wait_ge(at["ob"], g)
                            for t in range(TG):
                                last = T.transpose(banks[B_OT][:, t * P:(t + 1) * P], oT[:, t * P:(t + 1) * P], ident)
                            last.then_inc(at["oT"], 1)

                    def body(g, p):
                        a(2, g[5], p[5])
                        a(3, g[5], p[5])
                        b(1, g[5])
                        gateT_(g[5])
                        a(4, g[5], p[5])
                        c(3, g[6], p[6])
                        a(5, g[5], p[5])
                        f3T(g[4])
                        b(2, g[5])
                        aT(g[3], p[3])
                        c(4, g[6], p[6])
                        c(5, g[6], p[6])
                        rh(g[4], p[4])
                        b(3, g[5])
                        oT_(g[6])
                        logits(g[4])
                        gnn(g[3])
                        a(0, g[4], p[4])
                        c(0, g[5], p[5])
                        b(4, g[5])
                        a(1, g[4], p[4])
                        c(1, g[5], p[5])
                        c(2, g[5], p[5])
                        deg_(g[1], p[1])
                        b(5, g[5])
                        b(0, g[4])
                    sweep(pe, body)


def laid_out(inp):
    a = {k: np.ascontiguousarray(v) for k, v in inp.items()}
    half = HD // 2

    def swapped(w):
        return w.reshape(-1, 2, half, C)[:, ::-1].reshape(-1, C)

    def repeated(w):
        return np.repeat(w.reshape(NH // 2, 1, HD, C), 2, 1).reshape(-1, C)

    wq, wk, wv = a["L0_ffn_wq"], repeated(a["L0_ffn_wk"]), a["L0_ffn_wv"]
    w13 = np.zeros((C, NE0, 2, HIDP), np.float32)
    w13[:, :, 0, :HID] = a["L0_ffn_w1"].transpose(2, 0, 1)
    w13[:, :, 1, :HID] = a["L0_ffn_w3"].transpose(2, 0, 1)
    w2 = np.zeros((NE0, KC * P, C), np.float32)
    w2[:, :HID] = a["L0_ffn_w2"].transpose(0, 2, 1)
    r2 = np.zeros((RH, 8), np.float32)
    r2[:, :NE1] = a["L1_ffn_router_w2"]
    return dict(
        x=a["x"].reshape(TOK, C),
        adj_t=a["adj"].transpose(0, 2, 1).reshape(TOK, NN),
        gnn0_w=a["L0_gnn_weight"], gnn0_b=a["L0_gnn_bias"],
        ln1=a["L0_ffn_ln1_w"].reshape(C, 1), ln2=a["L0_ffn_ln2_w"].reshape(C, 1),
        wqkv=np.concatenate([wq, swapped(wq), wk, swapped(wk), wv], 0).T,
        wo=a["L0_ffn_wo"].T, router0=a["L0_ffn_router_w"].T,
        w13=w13.reshape(C, -1), w2=w2.reshape(NE0, KC, P, C).transpose(2, 0, 1, 3).reshape(P, -1),
        gnn1_w=a["L1_gnn_weight"], gnn1_b=a["L1_gnn_bias"],
        r1_w1=a["L1_ffn_router_w1"], r1_b1=a["L1_ffn_router_b1"].reshape(RH, 1),
        r1_w2=r2, r1_b2=a["L1_ffn_router_b2"],
        e_w1=a["L1_ffn_expert_w1"].transpose(1, 0, 2).reshape(C, -1), e_b1=a["L1_ffn_expert_b1"].T,
        e_w2=a["L1_ffn_expert_w2"].transpose(1, 0, 2).reshape(C, -1), e_b2=a["L1_ffn_expert_b2"].T,
        e_w3=a["L1_ffn_expert_w3"].transpose(1, 0, 2).reshape(C, -1), e_b3=a["L1_ffn_expert_b3"],
        consts=constants(),
    )


def kernel(**inputs):
    import concourse.bacc as _bacc
    from concourse.bass_utils import run_bass_kernel_spmd as _run

    nc = _bacc.Bacc("TRN2", target_bir_lowering=False, num_devices=1)
    arrays = {f"in_{k}": np.ascontiguousarray(v) for k, v in laid_out(inputs).items()}
    args = {k[3:]: nc.dram_tensor(k, v.shape, mybir.dt.float32, kind="ExternalInput").ap() for k, v in arrays.items()}
    out = nc.dram_tensor("out_0", (TOK, C), mybir.dt.float32, kind="ExternalOutput").ap()
    build(nc, out=out, **args)
    r = _run(nc, [arrays], core_ids=[0])
    return r.results[0]["out_0"].reshape(NB, NN, C)
```
